# Optimizing a Trainium2 kernel written in Bass

```python
import numpy as np
import jax
import jax.numpy as jnp

def _softmax(x, axis=-1):
    return jax.nn.softmax(x, axis=axis)

def _gelu(x):
    return jax.nn.gelu(x, approximate=True)

def _silu(x):
    return jax.nn.silu(x)

def _sigmoid(x):
    return jax.nn.sigmoid(x)

def _layernorm(x, axis=-1, eps=1e-05):
    m = jnp.mean(x, axis=axis, keepdims=True)
    v = jnp.var(x, axis=axis, keepdims=True)
    return (x - m) / jnp.sqrt(v + eps)

def _scatter_add(tgt, idx, src, axis=0):
    return tgt.at[idx].add(src)

def _segment_sum(src, seg, n):
    return jax.ops.segment_sum(src, seg, n)
kernel_name = 'mk_gnn_preln_d4_gnn_r32_286106'

def setup_inputs(seed: int=0):
    np.random.seed(seed)
    _w = jnp.asarray

    def _rec_inputs():
        import jax
        import jax.numpy as jnp
        _gk = jax.random.key(seed)
        x = -0.000202 + 1 * jax.random.normal(jax.random.fold_in(_gk, 1), (3125, 64), jnp.float32)
        _s = jax.random.randint(jax.random.fold_in(_gk, 2), (50000,), 0, 3125, jnp.int32)
        _d = jax.random.randint(jax.random.fold_in(_gk, 3), (50000,), 0, 3125, jnp.int32)
        _loop = jnp.arange(3125, dtype=jnp.int32)
        src = jnp.concatenate([_s, _d, _loop])
        dst = jnp.concatenate([_d, _s, _loop])
        _o = jnp.argsort(dst, stable=True)
        src = src[_o]
        dst = dst[_o]
        edge_attr_32 = 0.000283511 + 1.00007 * jax.random.normal(jax.random.fold_in(_gk, 12), (103125, 32), jnp.float32)
        edge_attr_64 = -2.25437e-05 + 0.999858 * jax.random.normal(jax.random.fold_in(_gk, 13), (103125, 64), jnp.float32)
        edge_weight = jax.random.uniform(jax.random.fold_in(_gk, 15), (103125,), jnp.float32, 0.0, 0.999999)
        return (x, src, dst, edge_attr_32, edge_attr_64, edge_weight)
    x, src, dst, edge_attr_32, edge_attr_64, edge_weight = _rec_inputs()

    def _L0_gnn_setup():
        import jax, jax.numpy as jnp
        import numpy as np
        N_NODES = 3125
        N_EDGES = 50000
        D = 64
        K = 10
        ALPHA = 0.1
        key = jax.random.key(seed)
        kx, kw, kb, ks, kd = jax.random.split(key, 5)
        x = jax.random.normal(kx, (N_NODES, D), dtype=jnp.float32)
        lim = 1.0 / np.sqrt(D)
        W = jax.random.uniform(kw, (D, D), minval=-lim, maxval=lim, dtype=jnp.float32)
        b = jax.random.uniform(kb, (D,), minval=-lim, maxval=lim, dtype=jnp.float32)
        src = jax.random.randint(ks, (N_EDGES,), 0, N_NODES, dtype=jnp.int32)
        dst = jax.random.randint(kd, (N_EDGES,), 0, N_NODES, dtype=jnp.int32)
        return {'x': x, 'W': W, 'b': b, 'src': src, 'dst': dst}
    _L0_gnn_all = _L0_gnn_setup()
    _L0_gnn_in = {k: v for k, v in _L0_gnn_all.items() if k in ('W', 'b')}
    del _L0_gnn_all

    def _L1_gnn_setup():
        import jax, jax.numpy as jnp
        import numpy as np
        N_NODES = 3125
        N_EDGES = 50000
        D = 64

        def _gcn_norm(edge_index, edge_weight, n):
            src = jnp.concatenate([edge_index[0], jnp.arange(n, dtype=edge_index.dtype)])
            dst = jnp.concatenate([edge_index[1], jnp.arange(n, dtype=edge_index.dtype)])
            w = jnp.concatenate([edge_weight, jnp.ones((n,), edge_weight.dtype)])
            deg = jax.ops.segment_sum(w, dst, num_segments=n)
            dinv = jnp.where(deg > 0, jax.lax.rsqrt(deg), 0.0)
            norm = dinv[src] * w * dinv[dst]
            return (src, dst, norm)

        def _gcn_conv(x, W, b, src, dst, norm, n):
            h = x @ W
            msg = h[src] * norm[:, None]
            out = jax.ops.segment_sum(msg, dst, num_segments=n)
            return out + b
        key = jax.random.key(seed)
        ks = jax.random.split(key, 9)
        x = jax.random.normal(ks[0], (N_NODES, D), dtype=jnp.float32)
        edge_index = jax.random.randint(ks[1], (2, N_EDGES), 0, N_NODES, dtype=jnp.int64)
        edge_attr = jax.random.uniform(ks[2], (N_EDGES,), dtype=jnp.float32)

        def glorot(k, din, dout):
            s = np.sqrt(6.0 / (din + dout)).astype(np.float32)
            return jax.random.uniform(k, (din, dout), jnp.float32, -s, s)
        return {'x': x, 'edge_index': edge_index, 'edge_attr': edge_attr, 'W1': glorot(ks[3], D, D), 'b1': jnp.zeros((D,), jnp.float32), 'W2': glorot(ks[4], D, D), 'b2': jnp.zeros((D,), jnp.float32), 'W3': glorot(ks[5], D, D), 'b3': jnp.zeros((D,), jnp.float32)}
    _L1_gnn_all = _L1_gnn_setup()
    _L1_gnn_in = {k: v for k, v in _L1_gnn_all.items() if k in ('W1', 'b1', 'W2', 'b2', 'W3', 'b3')}
    del _L1_gnn_all

    def _L2_gnn_setup():
        import math
        import jax, jax.numpy as jnp
        import numpy as np
        N_NODES = 50000
        N_EDGES = 18750
        IN_CH = 64
        HEADS = 2
        C = 64
        HC = HEADS * C
        EDGE_DIM = 32

        def _layernorm(x, g, b, eps=1e-05):
            m = jnp.mean(x, axis=-1, keepdims=True)
            v = jnp.mean(jnp.square(x - m), axis=-1, keepdims=True)
            return (x - m) / jnp.sqrt(v + eps) * g + b
        key = jax.random.key(seed)
        ks = jax.random.split(key, 12)
        s = 0.05
        return {'x': jax.random.normal(ks[0], (N_NODES, IN_CH), jnp.float32), 'edge_index': jax.random.randint(ks[1], (2, N_EDGES), 0, N_NODES, dtype=jnp.int64), 'edge_attr': jax.random.normal(ks[2], (N_EDGES, EDGE_DIM), jnp.float32), 'Wq': s * jax.random.normal(ks[3], (IN_CH, HC), jnp.float32), 'bq': jnp.zeros((HC,), jnp.float32), 'Wk': s * jax.random.normal(ks[4], (IN_CH, HC), jnp.float32), 'bk': jnp.zeros((HC,), jnp.float32), 'Wv': s * jax.random.normal(ks[5], (IN_CH, HC), jnp.float32), 'bv': jnp.zeros((HC,), jnp.float32), 'We': s * jax.random.normal(ks[6], (EDGE_DIM, HC), jnp.float32), 'Wp': s * jax.random.normal(ks[7], (HC, IN_CH), jnp.float32), 'bp': jnp.zeros((IN_CH,), jnp.float32), 'ln1_g': jnp.ones((IN_CH,), jnp.float32), 'ln1_b': jnp.zeros((IN_CH,), jnp.float32), 'ln2_g': jnp.ones((IN_CH,), jnp.float32), 'ln2_b': jnp.zeros((IN_CH,), jnp.float32), 'W1': s * jax.random.normal(ks[8], (IN_CH, IN_CH), jnp.float32), 'b1': jnp.zeros((IN_CH,), jnp.float32), 'W2': s * jax.random.normal(ks[9], (IN_CH, IN_CH), jnp.float32), 'b2': jnp.zeros((IN_CH,), jnp.float32)}
    _L2_gnn_all = _L2_gnn_setup()
    _L2_gnn_in = {k: v for k, v in _L2_gnn_all.items() if k in ('Wq', 'bq', 'Wk', 'bk', 'Wv', 'bv', 'We', 'Wp', 'bp', 'ln1_g', 'ln1_b', 'ln2_g', 'ln2_b', 'W1', 'b1', 'W2', 'b2')}
    del _L2_gnn_all

    def _L3_gnn_setup():
        import jax, jax.numpy as jnp
        import numpy as np
        N_NODES = 3125
        N_EDGES = 31250
        D_H = 64
        D_E = 64
        D_M = 64
        D_O = 64
        key = jax.random.key(seed)
        ks = jax.random.split(key, 8)
        hid = jax.random.normal(ks[0], (N_NODES, D_H), dtype=jnp.float32)
        edge_feat = jax.random.normal(ks[1], (N_EDGES, D_E), dtype=jnp.float32)
        src = jax.random.randint(ks[2], (N_EDGES,), 0, N_NODES)
        dst = jax.random.randint(ks[3], (N_EDGES,), 0, N_NODES)
        W1 = jax.random.normal(ks[4], (D_E + D_H, D_M), dtype=jnp.float32) * (1.0 / np.sqrt(D_E + D_H))
        b1 = jnp.zeros((D_M,), dtype=jnp.float32)
        W2 = jax.random.normal(ks[5], (D_M + D_H, D_O), dtype=jnp.float32) * (1.0 / np.sqrt(D_M + D_H))
        b2 = jnp.zeros((D_O,), dtype=jnp.float32)
        return {'hid': hid, 'edge_feat': edge_feat, 'src': src, 'dst': dst, 'W1': W1, 'b1': b1, 'W2': W2, 'b2': b2}
    _L3_gnn_all = _L3_gnn_setup()
    _L3_gnn_in = {k: v for k, v in _L3_gnn_all.items() if k in ('W1', 'b1', 'W2', 'b2')}
    del _L3_gnn_all
    return {'x': x, 'src': src, 'dst': dst, 'edge_attr_32': edge_attr_32, 'edge_attr_64': edge_attr_64, 'edge_weight': edge_weight, 'L0_gnn_W': _L0_gnn_in['W'], 'L0_gnn_b': _L0_gnn_in['b'], 'L1_gnn_W1': _L1_gnn_in['W1'], 'L1_gnn_b1': _L1_gnn_in['b1'], 'L1_gnn_W2': _L1_gnn_in['W2'], 'L1_gnn_b2': _L1_gnn_in['b2'], 'L1_gnn_W3': _L1_gnn_in['W3'], 'L1_gnn_b3': _L1_gnn_in['b3'], 'L2_gnn_Wq': _L2_gnn_in['Wq'], 'L2_gnn_bq': _L2_gnn_in['bq'], 'L2_gnn_Wk': _L2_gnn_in['Wk'], 'L2_gnn_bk': _L2_gnn_in['bk'], 'L2_gnn_Wv': _L2_gnn_in['Wv'], 'L2_gnn_bv': _L2_gnn_in['bv'], 'L2_gnn_We': _L2_gnn_in['We'], 'L2_gnn_Wp': _L2_gnn_in['Wp'], 'L2_gnn_bp': _L2_gnn_in['bp'], 'L2_gnn_ln1_g': _L2_gnn_in['ln1_g'], 'L2_gnn_ln1_b': _L2_gnn_in['ln1_b'], 'L2_gnn_ln2_g': _L2_gnn_in['ln2_g'], 'L2_gnn_ln2_b': _L2_gnn_in['ln2_b'], 'L2_gnn_W1': _L2_gnn_in['W1'], 'L2_gnn_b1': _L2_gnn_in['b1'], 'L2_gnn_W2': _L2_gnn_in['W2'], 'L2_gnn_b2': _L2_gnn_in['b2'], 'L3_gnn_W1': _L3_gnn_in['W1'], 'L3_gnn_b1': _L3_gnn_in['b1'], 'L3_gnn_W2': _L3_gnn_in['W2'], 'L3_gnn_b2': _L3_gnn_in['b2']}

def reference(x, src, dst, edge_attr_32, edge_attr_64, edge_weight, L0_gnn_W, L0_gnn_b, L1_gnn_W1, L1_gnn_b1, L1_gnn_W2, L1_gnn_b2, L1_gnn_W3, L1_gnn_b3, L2_gnn_Wq, L2_gnn_bq, L2_gnn_Wk, L2_gnn_bk, L2_gnn_Wv, L2_gnn_bv, L2_gnn_We, L2_gnn_Wp, L2_gnn_bp, L2_gnn_ln1_g, L2_gnn_ln1_b, L2_gnn_ln2_g, L2_gnn_ln2_b, L2_gnn_W1, L2_gnn_b1, L2_gnn_W2, L2_gnn_b2, L3_gnn_W1, L3_gnn_b1, L3_gnn_W2, L3_gnn_b2):
    import jax
    import jax.numpy as jnp

    def _L0_gnn_ref(x, W, b, src, dst):
        import jax, jax.numpy as jnp
        import numpy as np
        N_NODES = 3125
        N_EDGES = 50000
        D = 64
        K = 10
        ALPHA = 0.1
        h0 = x @ W + b
        ones = jnp.ones((src.shape[0],), dtype=x.dtype)
        deg_out = jax.ops.segment_sum(ones, src, num_segments=N_NODES)
        deg_in = jax.ops.segment_sum(ones, dst, num_segments=N_NODES)
        norm_src = jnp.where(deg_out > 0, jax.lax.rsqrt(jnp.maximum(deg_out, 1.0)), 0.0)[:, None]
        norm_dst = jnp.where(deg_in > 0, jax.lax.rsqrt(jnp.maximum(deg_in, 1.0)), 0.0)[:, None]
        h = h0
        for _ in range(K):
            msg = (h * norm_src)[src]
            agg = jax.ops.segment_sum(msg, dst, num_segments=N_NODES)
            h = (1.0 - ALPHA) * (agg * norm_dst) + ALPHA * h0
        return h

    def _L1_gnn_ref(x, edge_index, edge_attr, W1, b1, W2, b2, W3, b3):
        import jax, jax.numpy as jnp
        import numpy as np
        N_NODES = 3125
        N_EDGES = 50000
        D = 64

        def _gcn_norm(edge_index, edge_weight, n):
            src = jnp.concatenate([edge_index[0], jnp.arange(n, dtype=edge_index.dtype)])
            dst = jnp.concatenate([edge_index[1], jnp.arange(n, dtype=edge_index.dtype)])
            w = jnp.concatenate([edge_weight, jnp.ones((n,), edge_weight.dtype)])
            deg = jax.ops.segment_sum(w, dst, num_segments=n)
            dinv = jnp.where(deg > 0, jax.lax.rsqrt(deg), 0.0)
            norm = dinv[src] * w * dinv[dst]
            return (src, dst, norm)

        def _gcn_conv(x, W, b, src, dst, norm, n):
            h = x @ W
            msg = h[src] * norm[:, None]
            out = jax.ops.segment_sum(msg, dst, num_segments=n)
            return out + b
        n = x.shape[0]
        src, dst, norm = _gcn_norm(edge_index, edge_attr, n)
        h = jax.nn.relu(_gcn_conv(x, W1, b1, src, dst, norm, n))
        h = jax.nn.relu(_gcn_conv(h, W2, b2, src, dst, norm, n))
        return _gcn_conv(h, W3, b3, src, dst, norm, n)

    def _L2_gnn_ref(x, edge_index, edge_attr, Wq, bq, Wk, bk, Wv, bv, We, Wp, bp, ln1_g, ln1_b, ln2_g, ln2_b, W1, b1, W2, b2):
        import math
        import jax, jax.numpy as jnp
        import numpy as np
        N_NODES = 50000
        N_EDGES = 18750
        IN_CH = 64
        HEADS = 2
        C = 64
        HC = HEADS * C
        EDGE_DIM = 32

        def _layernorm(x, g, b, eps=1e-05):
            m = jnp.mean(x, axis=-1, keepdims=True)
            v = jnp.mean(jnp.square(x - m), axis=-1, keepdims=True)
            return (x - m) / jnp.sqrt(v + eps) * g + b
        n = x.shape[0]
        residual = x
        h = _layernorm(x, ln1_g, ln1_b)
        q = (h @ Wq + bq).reshape(n, HEADS, C)
        k = (h @ Wk + bk).reshape(n, HEADS, C)
        v = (h @ Wv + bv).reshape(n, HEADS, C)
        src, tgt = (edge_index[0], edge_index[1])
        e = (edge_attr @ We).reshape(-1, HEADS, C)
        qi = q[tgt]
        kj = k[src] + e
        vj = v[src] + e
        alpha = jnp.sum(qi * kj, axis=-1) / math.sqrt(C)
        amax = jax.ops.segment_max(alpha, tgt, num_segments=n)
        ex = jnp.exp(alpha - amax[tgt])
        den = jax.ops.segment_sum(ex, tgt, num_segments=n)
        a = ex / (den[tgt] + 1e-08)
        agg = jax.ops.segment_sum(a[:, :, None] * vj, tgt, num_segments=n)
        out = agg.reshape(n, HC) @ Wp + bp
        out = out + residual
        res2 = out
        o = _layernorm(out, ln2_g, ln2_b)
        o = jax.nn.gelu(o @ W1 + b1, approximate=False) @ W2 + b2
        return o + res2

    def _L3_gnn_ref(hid, edge_feat, src, dst, W1, b1, W2, b2):
        import jax, jax.numpy as jnp
        import numpy as np
        N_NODES = 3125
        N_EDGES = 31250
        D_H = 64
        D_E = 64
        D_M = 64
        D_O = 64
        edge_in = jnp.concatenate([edge_feat, hid[src]], axis=1)
        msg = jax.nn.relu(edge_in @ W1 + b1)
        msg_sum = jax.ops.segment_sum(msg, dst, num_segments=N_NODES)
        cnt = jax.ops.segment_sum(jnp.ones((msg.shape[0],), dtype=msg.dtype), dst, num_segments=N_NODES)
        reduced = msg_sum / jnp.maximum(cnt, 1.0)[:, None]
        node_in = jnp.concatenate([reduced, hid], axis=1)
        return jax.nn.relu(node_in @ W2 + b2)
    edge_index = jnp.stack([src, dst])
    h = jnp.maximum(_layernorm(x, axis=-1), 0.0)
    x = x + _L0_gnn_ref(h, L0_gnn_W, L0_gnn_b, src, dst)
    h = jnp.maximum(_layernorm(x, axis=-1), 0.0)
    x = x + _L1_gnn_ref(h, edge_index, edge_weight, L1_gnn_W1, L1_gnn_b1, L1_gnn_W2, L1_gnn_b2, L1_gnn_W3, L1_gnn_b3)
    h = jnp.maximum(_layernorm(x, axis=-1), 0.0)
    x = x + _L2_gnn_ref(h, edge_index, edge_attr_32, L2_gnn_Wq, L2_gnn_bq, L2_gnn_Wk, L2_gnn_bk, L2_gnn_Wv, L2_gnn_bv, L2_gnn_We, L2_gnn_Wp, L2_gnn_bp, L2_gnn_ln1_g, L2_gnn_ln1_b, L2_gnn_ln2_g, L2_gnn_ln2_b, L2_gnn_W1, L2_gnn_b1, L2_gnn_W2, L2_gnn_b2)
    h = jnp.maximum(_layernorm(x, axis=-1), 0.0)
    x = x + _L3_gnn_ref(h, edge_attr_64, src, dst, L3_gnn_W1, L3_gnn_b1, L3_gnn_W2, L3_gnn_b2)
    return x

_drawn_inputs = setup_inputs


def setup_inputs(seed=0):
    import zlib

    import numpy as np

    out = dict(_drawn_inputs(seed))
    spreads = {'L1_gnn_b1': (0.0, 0.1),
     'L1_gnn_b2': (0.0, 0.1),
     'L1_gnn_b3': (0.0, 0.1),
     'L2_gnn_bq': (0.0, 0.8),
     'L2_gnn_bk': (0.0, 2.0),
     'L2_gnn_bv': (0.0, 0.341),
     'L2_gnn_bp': (0.0, 0.1),
     'L2_gnn_ln1_g': (1.0, 0.6),
     'L2_gnn_ln1_b': (0.0, 0.8),
     'L2_gnn_ln2_g': (1.0, 0.6),
     'L2_gnn_ln2_b': (0.0, 2.0),
     'L2_gnn_b1': (0.0, 0.662),
     'L2_gnn_b2': (0.0, 0.1),
     'L3_gnn_b1': (0.0, 0.639),
     'L3_gnn_b2': (0.0, 0.29)}
    factors = {'edge_attr_32': 3.4,
     'edge_weight': 7.327,
     'L2_gnn_Wq': 7.382,
     'L2_gnn_Wk': 8.0,
     'L2_gnn_We': 3.3,
     'edge_attr_64': 3.729}
    for name, (base, spread) in spreads.items():
        noise = np.random.default_rng([zlib.crc32(name.encode()), seed]).standard_normal(out[name].shape)
        drawn = base * np.exp(spread * noise) if base else spread * noise
        out[name] = jnp.asarray(drawn.astype(out[name].dtype))
    for name, factor in factors.items():
        out[name] = (out[name] * factor).astype(out[name].dtype)
    return out
```

```python
from contextlib import ExitStack

import numpy as np

import concourse.bass as bass
from concourse import mybir

F32 = mybir.dt.float32
F16 = mybir.dt.float16
BF16 = mybir.dt.bfloat16
I32 = mybir.dt.int32
I16 = mybir.dt.int16
ALU = mybir.AluOpType
ACT = mybir.ActivationFunctionType
X = mybir.AxisListType.X

P = 128
NODES = 3125
EDGES = 103125
D = 64
NCH = 25
NPAD = NCH * P
HOPS = 10
ALPHA = 0.1
EPS = 1e-5

TE = 256
T1 = -(-EDGES // TE)
EPAD = T1 * TE
BW = 16
J1 = -(-NODES // BW)
NDST = J1 * BW
V1 = T1 + J1 - 1
V1P = 640
BCOL = NCH * BW
OH = 3
RING = 2
J2 = NCH
V2 = T1 + J2 - 1
V2P = 448
DC = 512
NDC = -(-NDST // DC)
BLOCK1, PLACE, TILE2, BLOCK2 = 0, 32, 64, 96
FAR = 1 << 20


class Chain:

    def __init__(self, eng, sem):
        self.eng, self.sem, self.n = eng, sem, 0

    def __call__(self, ins):
        self.n += 1
        ins.then_inc(self.sem, 1)
        self.eng.wait_ge(self.sem, self.n)


def spread(v, n):
    return v.unsqueeze(2).to_broadcast([P, v.shape[1], n])


def along(v, k):
    return v.unsqueeze(1).to_broadcast([P, k, v.shape[1]])


class Mem:

    def __init__(self, nc, ctx):
        sb = lambda name, shape, dt: ctx.enter_context(nc.sbuf_tensor(name, shape, dt))
        self.big = sb("big", [P, NCH * NDST // 2], F32)
        self.work = sb("work", [P, 4 * NCH * D], F32)
        self.work2 = sb("work2", [P, NDST + NCH * D], F32)
        self.rel2 = sb("rel2", [P, 2, V2P], F32)
        self.src2 = sb("src2", [P, 2, V2P], I32)
        self.vis = sb("vis", [P, V1P], I16)
        self.ident = sb("ident", [P, P], F32)
        self.iotaH = sb("iotaH", [P, BCOL], F16)
        self.onesB = sb("onesB", [P, P], BF16)
        self.colsN = sb("colsN", [P, 8, NCH], F32)
        self.smalls = self.work2[:, 3 * DC + NCH * D:3 * DC + NCH * D + 8 * D]
        self.PB = [ctx.enter_context(nc.psum_tensor(f"bank{i}", [P, 512], F32)) for i in range(8)]

    def counts(self):
        return self.big[:, :].bitcast(F16).rearrange("p (a n) -> p a n", a=NCH)

    def small(self, i):
        return self.smalls[:, i * D:(i + 1) * D]

    def zbuf(self, k):
        base = self.work[:, 0:NCH * D] if k == 0 else self.work2[:, 3 * DC:3 * DC + NCH * D]
        return base.bitcast(F16).rearrange("p (a s d) -> p a s d", a=NCH, s=2)

    def node(self, i):
        return self.work[:, i * NCH * D:(i + 1) * NCH * D].rearrange("p (a d) -> p a d", a=NCH)


def stage_tables(nc, m, last, dst, src, w, t1):
    C = last.shape[1]
    K1, K2 = V1P // P, -(-V2P // P)
    with ExitStack() as ctx:
        sem = lambda n: ctx.enter_context(nc.semaphore(n))
        raw = m.big
        at = [0]

        def take(n):
            at[0] += n
            return raw[:, at[0] - n:at[0]]

        iotaI = take(V1P).bitcast(I32)
        iotaF = take(V1P)
        vmodI = take(V1P).bitcast(I32)
        vmodF = take(V1P)
        schemes = []
        lastI = take(C).bitcast(I32)
        for K, shift in ((K1, 4), (K2, 7)):
            VP = K * P
            schemes.append(dict(
                VP=VP, K=K, shift=shift, blkI=take(C).bitcast(I32),
                tI=take(C).bitcast(I32), blkF=take(C), tF=take(C), end=take(C), cmp=take(C * VP // 2).bitcast(BF16).rearrange("p (c v) -> p c v", c=C),
                tv=take(VP), tvc=take(VP), jv=take(VP + 2), tcol=take(K).bitcast(I32)))
        rowsI = take(K1 * 3 * TE + K2 * 2 * TE).bitcast(I32)
        rowsF = take(K1 * 4 * TE + K2 * 2 * TE)
        abI = take(K1 * 2 * TE).bitcast(I32)
        tabT = take(4 * 2 * V1P).rearrange("p (k h v) -> p k h v", k=4, h=2)
        valid, tmp = take(2 * V1P).rearrange("p (h v) -> p h v", h=2), take(2 * V1P).rearrange("p (h v) -> p h v", h=2)
        src2F = take(2 * V2P).rearrange("p (h v) -> p h v", h=2)
        wB = take(V1P).bitcast(BF16).rearrange("p (h v) -> p h v", h=2)
        r1 = rowsI[:, 0:K1 * 3 * TE].rearrange("p (k a e) -> p k a e", k=K1, a=3)
        r2 = rowsI[:, K1 * 3 * TE:].rearrange("p (k a e) -> p k a e", k=K2, a=2)
        f1 = rowsF[:, 0:K1 * 4 * TE].rearrange("p (k a e) -> p k a e", k=K1, a=4)
        f2 = rowsF[:, K1 * 4 * TE:].rearrange("p (k a e) -> p k a e", k=K2, a=2)
        ab = abI.rearrange("p (k a e) -> p k a e", k=K1, a=2)

        s_iota = sem("tab_iota"); s_last = sem("tab_last"); s_dve = sem("tab_dve"); s_cmp = sem("tab_cmp")
        s_tv = sem("tab_tv"); s_tvs = sem("tab_tvs"); s_tc = sem("tab_tcol"); s_tcs = sem("tab_tcols")
        s_rows = sem("tab_rows"); s_rowsF = sem("tab_rowsF"); s_tr = sem("tab_tr"); s_trs = sem("tab_trs")
        s_pool = sem("tab_pool"); s_dve2 = sem("tab_dve2")
        items = []
        for k in range(K1):
            for arr in range(4):
                for h in range(2):
                    items.append((f1[:, k, arr, h * P:(h + 1) * P], tabT[:, arr, h, k * P:(k + 1) * P]))
        for k in range(K2):
            for arr, to in enumerate((m.rel2, src2F)):
                for h in range(2):
                    items.append((f2[:, k, arr, h * P:(h + 1) * P], to[:, h, k * P:min((k + 1) * P, V2P)]))
        block = ctx.enter_context(nc.Block())

        @block.sync
        def _(sp):
            sp.dma_start(lastI, last).then_inc(s_last, 16)

        @block.gpsimd
        def _(po):
            po.iota(iotaI, pattern=[[1, V1P]], base=0, channel_multiplier=0).then_inc(s_iota, 1)
            po.iota(vmodI, pattern=[[0, V1P // RING], [1, RING]], base=0, channel_multiplier=0).then_inc(s_iota, 1)
            for s in schemes:
                po.iota(s["tI"], pattern=[[P, C]], base=0, channel_multiplier=1).then_inc(s_iota, 1)
            po.memset(m.ident[:, :], 0.0).then_inc(s_pool, 1)
            po.wait_ge(s_pool, 1)
            po.affine_select(out=m.ident[:, :], in_=m.ident[:, :], compare_op=ALU.not_equal, fill=1.0, base=0,
                             pattern=[[-1, P]], channel_multiplier=1).then_inc(s_iota, 1)
            po.wait_ge(s_tcs, 1)
            for k in range(K1):
                for a, arr in enumerate((dst, src)):
                    po.indirect_dma_start(r1[:, k, a, :], None, arr, bass.IndirectOffsetOnAxis(
                        ap=schemes[0]["tcol"][:, k:k + 1], axis=0)).then_inc(s_rows, 16)
                po.indirect_dma_start(r1[:, k, 2, :].bitcast(F32), None, w, bass.IndirectOffsetOnAxis(
                    ap=schemes[0]["tcol"][:, k:k + 1], axis=0)).then_inc(s_rows, 16)
            po.wait_ge(s_tcs, 2)
            for k in range(K2):
                for a, arr in enumerate((dst, src)):
                    po.indirect_dma_start(r2[:, k, a, :], None, arr, bass.IndirectOffsetOnAxis(
                        ap=schemes[1]["tcol"][:, k:k + 1], axis=0)).then_inc(s_rows, 16)

        @block.tensor
        def _(pe):
            pe.wait_ge(s_iota, 5)
            for n, s in enumerate(schemes):
                pe.wait_ge(s_cmp, n + 1)
                half = s["VP"] // 2
                for q in range(2):
                    for c in range(C):
                        ins = pe.matmul(m.PB[2 * n + q][:, 0:half], m.onesB[:, :], s["cmp"][:, c, q * half:(q + 1) * half],
                                        start=(c == 0), stop=(c == C - 1))
                ins.then_inc(s_tv, 1)
            for n, s in enumerate(schemes):
                pe.wait_ge(s_tvs, n + 1)
                for k in range(s["K"]):
                    ins = pe.transpose(m.PB[4 + 2 * n + k // 4][:, (k % 4) * P:(k % 4 + 1) * P], s["tvc"][:, k * P:(k + 1) * P], m.ident[:, :])
                ins.then_inc(s_tc, 1)
            pe.wait_ge(s_rowsF, 1)
            for i, (a, _) in enumerate(items):
                if i % 4 == 0 and i >= 8:
                    pe.wait_ge(s_trs, i // 4 - 1)
                ins = pe.transpose(m.PB[i // 4 % 2][:, (i % 4) * P:(i % 4 + 1) * P], a, m.ident[:, :])
                if i % 4 == 3 or i == len(items) - 1:
                    ins.then_inc(s_tr, 1)

        @block.scalar
        def _(act):
            for i0 in range(0, len(items), 4):
                act.wait_ge(s_tr, i0 // 4 + 1)
                for i in range(i0, min(i0 + 4, len(items))):
                    ins = nc.scalar.copy(items[i][1], m.PB[i // 4 % 2][:, (i % 4) * P:(i % 4) * P + items[i][1].shape[-1]])
                ins.then_inc(s_trs, 1)

        @block.vector
        def _(dve):
            chain = Chain(dve, s_dve)
            chain(dve.memset(m.onesB[:, :], 1.0))
            dve.wait_ge(s_iota, 5)
            chain(dve.tensor_copy(iotaF, iotaI))
            chain(dve.tensor_copy(vmodF, vmodI))
            chain(dve.tensor_copy(m.iotaH[:, :], iotaI[:, 0:BCOL]))
            dve.wait_ge(s_last, 16)
            for s in schemes:
                chain(dve.tensor_scalar(s["blkI"], lastI, s["shift"], None, ALU.arith_shift_right))
                chain(dve.tensor_copy(s["blkF"], s["blkI"]))
                chain(dve.tensor_copy(s["tF"], s["tI"]))
                chain(dve.tensor_tensor(s["end"], s["blkF"], s["tF"], ALU.add))
                for c in range(C):
                    ins = dve.tensor_scalar(s["cmp"][:, c, :], iotaF[:, 0:s["VP"]], s["end"][:, c:c + 1], None, ALU.is_gt)
                ins.then_inc(s_cmp, 1)
            for n, s in enumerate(schemes):
                dve.wait_ge(s_tv, n + 1)
                half = s["VP"] // 2
                for q in range(2):
                    part = slice(q * half, (q + 1) * half)
                    chain(dve.tensor_copy(s["tv"][:, part], m.PB[2 * n + q][:, 0:half]))
                dve.memset(s["jv"][:, 0:1], -1.0)
                chain(dve.tensor_tensor(s["jv"][:, 1:s["VP"] + 1], iotaF[:, 0:s["VP"]], s["tv"], ALU.subtract))
                dve.tensor_scalar(s["tvc"], s["tv"], float(T1 - 1), None, ALU.min).then_inc(s_tvs, 1)
            for n, s in enumerate(schemes):
                dve.wait_ge(s_tc, n + 1)
                for g in range(-(-s["K"] // 4)):
                    k = min(4, s["K"] - 4 * g)
                    ins = dve.tensor_copy(s["tcol"][:, 4 * g:4 * g + k],
                                          m.PB[4 + 2 * n + g][:, 0:k * P].rearrange("p (k v) -> p k v", k=k)[:, :, 0])
                ins.then_inc(s_tcs, 1)
            j1 = schemes[0]["jv"][:, 1:V1P + 1]
            dve.wait_ge(s_tvs, 2)
            more = tmp[:, 0, :]
            chain(dve.memset(more, 0.0))
            chain(dve.tensor_tensor(more[:, 0:V1 - 1], schemes[0]["jv"][:, 2:V1 + 1], j1[:, 0:V1 - 1], ALU.is_equal))
            spare = tmp[:, 1, :]
            chain(dve.tensor_scalar(spare, vmodF, float(J1), None, ALU.add))
            chain(dve.tensor_tensor(spare, spare, j1, ALU.subtract))
            chain(dve.tensor_tensor(spare, spare, more, ALU.mult))
            chain(dve.tensor_tensor(spare, spare, j1, ALU.add))
            chain(dve.tensor_scalar(m.vis[PLACE:PLACE + 1, 0:V1], spare[PLACE:PLACE + 1, 0:V1], 0.0, None, ALU.add))
            chain(dve.tensor_scalar(m.vis[BLOCK1:BLOCK1 + 1, 0:V1], j1[BLOCK1:BLOCK1 + 1, 0:V1], 0.0, None, ALU.add))
            chain(dve.tensor_tensor(t1["keep"], j1, schemes[0]["jv"][:, 0:V1P], ALU.is_equal))
            dve.wait_ge(s_rows, 16 * (3 * K1 + 2 * K2))
            for k in range(K1):
                chain(dve.tensor_scalar(ab[:, k, 0, :], r1[:, k, 1, :], 7, None, ALU.arith_shift_right))
                chain(dve.tensor_scalar(ab[:, k, 1, :], r1[:, k, 1, :], P - 1, None, ALU.bitwise_and))
                dve.tensor_copy(f1[:, k, 0, :], r1[:, k, 0, :])
                dve.tensor_copy(f1[:, k, 1, :], ab[:, k, 0, :])
                dve.tensor_copy(f1[:, k, 2, :], ab[:, k, 1, :])
                chain(dve.tensor_copy(f1[:, k, 3, :], r1[:, k, 2, :].bitcast(F32)))
            dve.tensor_copy(f2.rearrange("p k a e -> p (k a e)"), r2.rearrange("p k a e -> p (k a e)")).then_inc(s_rowsF, 1)
            dve.wait_ge(s_trs, -(-len(items) // 4))
            dstT, chT, rowT, wT = (tabT[:, i, :, :] for i in range(4))
            for h in range(2):
                chain(dve.scalar_tensor_tensor(tmp[:, h, :], j1, -float(BW), dstT[:, h, :], ALU.mult, ALU.add))
            chain(dve.tensor_scalar(valid, tmp, 0.0, None, ALU.is_ge))
            chain(dve.scalar_tensor_tensor(valid, tmp, float(BW - 1), valid, ALU.is_le, ALU.mult))
            chain(dve.scalar_tensor_tensor(tmp, chT, float(BW), tmp, ALU.mult, ALU.add))
            chain(dve.scalar_tensor_tensor(tmp, tmp, 1.0, valid, ALU.add, ALU.mult))
            chain(dve.tensor_scalar(t1["col"], tmp, -1.0, None, ALU.add))
            chain(dve.tensor_copy(t1["row"], rowT))
            for i in range(3):
                chain(dve.tensor_copy(wB, wT))
                chain(dve.tensor_copy(t1["w"][i], wB))
                if i < 2:
                    chain(dve.tensor_tensor(wT, wT, t1["w"][i], ALU.subtract))
            j2 = schemes[1]["jv"][:, 1:V2P + 1]
            for h in range(2):
                chain(dve.scalar_tensor_tensor(m.rel2[:, h, :], j2, -float(P), m.rel2[:, h, :], ALU.mult, ALU.add))
            chain(dve.tensor_copy(m.src2[:, :, :], src2F))
            chain(dve.tensor_scalar(m.vis[TILE2:TILE2 + 1, 0:V2P], schemes[1]["tvc"][TILE2:TILE2 + 1, 0:V2P], 0.0, None, ALU.add))
            chain(dve.tensor_scalar(m.vis[BLOCK2:BLOCK2 + 1, 0:V2P], j2[BLOCK2:BLOCK2 + 1, :], 0.0, None, ALU.add))


def stage_build(nc, m, t1, aw):
    with ExitStack() as ctx:
        sem = lambda n: ctx.enter_context(nc.semaphore(n))
        cur_c = [m.work2[:, i * BCOL:(i + 1) * BCOL] for i in range(2)]
        cur_w = [m.work2[:, (2 + i) * BCOL:(3 + i) * BCOL] for i in range(2)]
        o = 4 * BCOL
        rows, cols = [], []
        for i in range(OH):
            rows.append(m.work2[:, o:o + 2 * 4 * P // 2].bitcast(BF16).rearrange("p (h k r) -> p h k r", h=2, k=4))
            o += 4 * P
            cols.append(m.work2[:, o:o + BCOL].bitcast(F16).rearrange("p (h c) -> p h c", h=2))
            o += BCOL
        gate, gateP, zero = m.colsN[:, 0, 0:1], m.colsN[:, 1, 0:1], m.colsN[:, 2, 0:1]
        psc = [m.PB[0], m.PB[1]]
        psw = [m.PB[2], m.PB[3]]
        counts = m.counts()

        oh_ready = sem("oh_ready")
        rows_ready = sem("rows_ready")
        vis_done = sem("vis_done")
        cur_ready = sem("cur_ready")
        cnt_stored = sem("cnt_stored")
        w_stored = [sem("w_stored0"), sem("w_stored1")]
        gated = sem("gated")
        gatedP = sem("gatedP")
        init = sem("build_init")
        block = ctx.enter_context(nc.Block())

        @block.sync
        def _(sp):
            with sp.Fori(0, V1, 2) as v:
                for k in range(2):
                    place = sp.value_load(m.vis[PLACE:PLACE + 1, bass.ds(v + k, 1)], min_val=0, max_val=J1 + RING - 1)
                    sp.wait_ge(cur_ready, v + k + 1)
                    sp.dma_start(aw[bass.ds(place, 1), :, :].rearrange("j p c -> p (j c)"), cur_w[k]).then_inc(w_stored[k], 16)
            for k in range(2):
                sp.wait_ge(w_stored[k], 16 * (V1 // 2))

        @block.vector
        def _(dve):
            dve.memset(zero, 0.0)
            dve.memset(gate, 0.0)
            dve.memset(gateP, 0.0)
            dve.memset(m.work2[:, 0:4 * BCOL], 0.0).then_inc(init, 1)
            dve.wait_ge(init, 1)

            def onehots(v, k, first=False):
                if not first:
                    dve.wait_ge(vis_done, v - OH + 1)
                for h in range(2):
                    dve.tensor_scalar(rows[k][:, h, 0, :], m.iotaH[:, 0:P], t1["row"][:, h, bass.ds(v, 1)], None, ALU.is_equal)
                    ins = dve.tensor_scalar(cols[k][:, h, :], m.iotaH[:, :], t1["col"][:, h, bass.ds(v, 1)], None, ALU.is_equal)
                ins.then_inc(oh_ready, 1)

            def running(v, k, first=False):
                keep = t1["keep"][:, bass.ds(v, 1)]
                dve.wait_ge(vis_done, v + 1)
                if not first:
                    dve.wait_ge(cnt_stored, v - 1)
                    dve.wait_ge(w_stored[k], 8 * (v - k))
                if not first or k:
                    dve.wait_ge(cur_ready, v)
                dve.scalar_tensor_tensor(cur_c[k], cur_c[1 - k], keep, psc[k][:, 0:BCOL], ALU.mult, ALU.add)
                dve.scalar_tensor_tensor(cur_w[k], cur_w[1 - k], keep, psw[k][:, 0:BCOL], ALU.mult, ALU.add).then_inc(cur_ready, 1)

            onehots(0, 0, True)
            onehots(1, 1, True)
            onehots(2, 2, True)
            running(0, 0, True)
            onehots(3, 0)
            running(1, 1, True)
            with dve.Fori(2, V1 - 2, 6) as v:
                for u in range(6):
                    onehots(v + u + 2, (4 + u) % OH)
                    running(v + u, u % 2)
            running(V1 - 2, 0)
            running(V1 - 1, 1)

        @block.scalar
        def _(act):
            act.wait_ge(init, 1)

            def weigh(v, k):
                act.wait_ge(gated, v)
                act.wait_ge(oh_ready, v + 1)
                nc.scalar.copy(gate, zero).then_inc(gated, 1)
                for h in range(2):
                    for i in range(3):
                        ins = nc.scalar.activation(rows[k][:, h, 1 + i, :], rows[k][:, h, 0, :], ACT.Copy,
                                                   scale=t1["w"][i][:, h, bass.ds(v, 1)])
                ins.then_inc(rows_ready, 1)

            weigh(0, 0)
            weigh(1, 1)
            with act.Fori(2, V1 - 2, 6) as v:
                for u in range(6):
                    weigh(v + u, (2 + u) % OH)
            weigh(V1 - 2, (V1 - 2) % OH)
            weigh(V1 - 1, (V1 - 1) % OH)

        @block.tensor
        def _(pe):
            def products(v, k, r, first=False, last=False):
                pe.wait_ge(rows_ready, v + 1)
                if not first:
                    pe.wait_ge(cur_ready, v - 1)
                for h in range(2):
                    pe.matmul(psc[k][:, 0:BCOL], rows[r][:, h, 0, :], cols[r][:, h, :], start=(h == 0), stop=(h == 1))
                    pe.matmul(m.PB[4][:, 0:BCOL], rows[r][:, h, 0, :], cols[r][:, h, :],
                              start=(first and v == 0 and h == 0), stop=(last and h == 1))
                    for i in range(3):
                        ins = pe.matmul(psw[k][:, 0:BCOL], rows[r][:, h, 1 + i, :], cols[r][:, h, :],
                                        start=(h == 0 and i == 0), stop=(h == 1 and i == 2))
                ins.then_inc(vis_done, 1)

            products(0, 0, 0, True)
            products(1, 1, 1, True)
            with pe.Fori(2, V1 - 2, 6) as v:
                for u in range(6):
                    products(v + u, u % 2, (2 + u) % OH)
            products(V1 - 2, 0, (V1 - 2) % OH)
            products(V1 - 1, 1, (V1 - 1) % OH, last=True)

        @block.gpsimd
        def _(po):
            po.wait_ge(init, 1)
            with po.Fori(0, V1, 2) as v:
                for k in range(2):
                    j = po.value_load(m.vis[BLOCK1:BLOCK1 + 1, bass.ds(v + k, 1)], min_val=0, max_val=J1 - 1)
                    po.wait_ge(cnt_stored, v + k)
                    po.wait_ge(cur_ready, v + k + 1)
                    po.tensor_tensor(gateP, zero, zero, ALU.add).then_inc(gatedP, 1)
                    po.tensor_copy(counts[:, :, bass.ds(j * BW, BW)], cur_c[k].rearrange("p (a w) -> p a w", a=NCH)).then_inc(cnt_stored, 1)

GROUP = DC // P
LO = 2048.0
HSCALE = 16.0


def width(c):
    return min(DC, NDST - c * DC)


def dve_norm(dve, chain, out, x, tmp, stat, var_ready, std_ready, n):
    mean, var = stat
    chain(dve.tensor_reduce(mean, x, op=ALU.add, axis=X))
    chain(dve.tensor_scalar(mean, mean, 1.0 / D, None, ALU.mult))
    chain(dve.tensor_tensor(out, x, spread(mean, D), ALU.subtract))
    chain(dve.tensor_tensor(tmp, out, out, ALU.mult))
    chain(dve.tensor_reduce(var, tmp, op=ALU.add, axis=X))
    dve.tensor_scalar(var, var, 1.0 / D, EPS, ALU.mult, ALU.add).then_inc(var_ready, 1)
    dve.wait_ge(std_ready, n)
    chain(dve.reciprocal(var, var))
    chain(dve.tensor_tensor(out, out, spread(var, D), ALU.mult))


class Linear:

    def __init__(self, nc, ctx, name, m, buf, cin, cout, banks=(0, 1, 2, 3)):
        sem = lambda n: ctx.enter_context(nc.semaphore(f"{name}_{n}"))
        self.turned, self.copied, self.done, self.taken = sem("turned"), sem("copied"), sem("done"), sem("taken")
        self.buf = buf
        self.cin, self.cout = cin, cout
        self.psT = [m.PB[banks[0]], m.PB[banks[1]]]
        self.psO = [m.PB[banks[2]], m.PB[banks[3]]]
        self.ident = m.ident[:, :]

    def tensor(self, pe, rows, weight):
        for a in range(NCH + 1):
            if a < NCH:
                if a >= 2:
                    pe.wait_ge(self.copied, a - 1)
                pe.transpose(self.psT[a % 2][0:self.cin, 0:P], rows(a), self.ident).then_inc(self.turned, 1)
            if a >= 1:
                b = a - 1
                pe.wait_ge(self.copied, b + 1)
                if b >= 2:
                    pe.wait_ge(self.taken, b - 1)
                pe.matmul(self.psO[b % 2][:, 0:self.cout], self.buf[b % 2], weight, start=True, stop=True).then_inc(self.done, 1)

    def scalar(self, act, nc):
        for a in range(NCH):
            act.wait_ge(self.turned, a + 1)
            if a >= 2:
                act.wait_ge(self.done, a - 1)
            nc.scalar.copy(self.buf[a % 2], self.psT[a % 2][0:self.cin, 0:P]).then_inc(self.copied, 1)

    def result(self, eng, a):
        eng.wait_ge(self.done, a + 1)
        return self.psO[a % 2][:, 0:self.cout]


def stage_layer0_start(nc, m, x, wt, bias):
    with ExitStack() as ctx:
        sem = lambda n: ctx.enter_context(nc.semaphore(n))
        small = m.small
        w_sb, bias_sb = small(0), small(1)
        ones16 = small(2).bitcast(F16)
        comb = small(3)
        buf = [m.work2[0:D, i * P:(i + 1) * P] for i in range(2)]
        lin = Linear(nc, ctx, "l0", m, buf, D, D, banks=(5, 5, 6, 6))
        lin.psT = [m.PB[5], m.PB[6]]
        lin.psO = [m.PB[7], m.PB[4]]
        xs, h0, hs, tmp = m.work2[:, 1536:3136].rearrange("p (a d) -> p a d", a=NCH), m.node(1), m.node(2), m.node(3)
        degrow = m.work[:, 2 * NCH * D:4 * NCH * D]
        counts = m.counts()
        cols = m.colsN
        mean, var, din, dout, c1s, c1n, ns = (cols[:, i, :] for i in range(7))
        gm = cols[:, 7, 0:1]; gall = cols[:, 7, 1:2]; ginv = cols[:, 7, 2:3]; gback = cols[:, 7, 3:4]
        s_in = sem("l0_in"); s_dve = sem("l0_dve"); s_one = sem("l0_one"); s_var = sem("l0_var"); s_std = sem("l0_std")
        s_rows = sem("l0_rows"); s_deg = sem("l0_deg"); s_gm = sem("l0_gm"); s_gall = sem("l0_gall")
        s_nvar = sem("l0_nvar"); s_nstd = sem("l0_nstd"); s_dout = sem("l0_dout")
        z16 = m.node(0).rearrange("p a d -> p (a d)").bitcast(F16).rearrange("p (a s d) -> p a s d", a=NCH, s=2)
        block = ctx.enter_context(nc.Block())

        @block.sync
        def _(sp):
            sp.dma_start(xs, x).then_inc(s_in, 16)
            sp.dma_start(w_sb[0:D, :], wt).then_inc(s_in, 16)
            sp.dma_start(bias_sb, bias.partition_broadcast(P)).then_inc(s_in, 16)

        @block.tensor
        def _(pe):
            pe.wait_ge(s_one, 1)
            for c in range(4):
                pe.matmul(m.PB[c][:, 0:width(c)], ones16, counts[:, 0, c * DC:c * DC + width(c)], start=True, stop=False)
            with pe.Fori(1, NCH - 1) as a:
                for c in range(4):
                    pe.matmul(m.PB[c][:, 0:width(c)], ones16, counts[:, bass.ds(a, 1), c * DC:c * DC + width(c)],
                              start=False, stop=False)
            for c in range(4):
                pe.matmul(m.PB[c][:, 0:width(c)], ones16, counts[:, NCH - 1, c * DC:c * DC + width(c)],
                          start=False, stop=True).then_inc(s_deg, 1)
            pe.wait_ge(s_dout, 2)
            for c in range(4, NDC):
                pe.matmul(m.PB[c - 4][:, 0:width(c)], ones16, counts[:, 0, c * DC:c * DC + width(c)], start=True, stop=False)
            with pe.Fori(1, NCH - 1) as a:
                for c in range(4, NDC):
                    pe.matmul(m.PB[c - 4][:, 0:width(c)], ones16, counts[:, bass.ds(a, 1), c * DC:c * DC + width(c)],
                              start=False, stop=False)
            for c in range(4, NDC):
                pe.matmul(m.PB[c - 4][:, 0:width(c)], ones16, counts[:, NCH - 1, c * DC:c * DC + width(c)],
                          start=False, stop=True).then_inc(s_deg, 1)
            pe.wait_ge(s_rows, 1)
            pe.wait_ge(s_in, 48)
            lin.tensor(pe, lambda a: h0[:, a, :], w_sb[0:D, :])

        @block.scalar
        def _(act):
            act.wait_ge(s_var, 1)
            nc.scalar.sqrt(var, var).then_inc(s_std, 1)
            act.wait_ge(s_nvar, 1)
            nc.scalar.sqrt(ns, ns).then_inc(s_nstd, 1)
            nc.scalar.sqrt(c1n, c1n).then_inc(s_nstd, 1)
            lin.scalar(act, nc)

        @block.gpsimd
        def _(po):
            po.wait_ge(s_gm, 1)
            po.partition_all_reduce(gall, gm, P, bass.bass_isa.ReduceOp.max).then_inc(s_gall, 1)

        @block.vector
        def _(dve):
            chain = Chain(dve, s_dve)
            dve.memset(ones16, 1.0).then_inc(s_one, 1)
            dve.tensor_copy(comb[0:D, :], m.ident[0:D, 0:D])
            chain(dve.tensor_scalar(comb[D:P, :], m.ident[D:P, D:P], 1.0 / LO, None, ALU.mult))
            dve.wait_ge(s_in, 48)
            dve_norm(dve, chain, h0, xs, tmp, (mean, var), s_var, s_std, 1)
            dve.tensor_scalar(h0, h0, 0.0, None, ALU.max).then_inc(s_rows, 1)
            chain(dve.memset(degrow[:, NDST:], 0.0))
            chain(dve.tensor_reduce(dout, m.PB[4][:, 0:BCOL].rearrange("p (a w) -> p a w", a=NCH), op=ALU.add, axis=X))
            dve.wait_ge(s_deg, 4)
            for c in range(4):
                ins = dve.tensor_copy(degrow[:, c * DC:(c + 1) * DC], m.PB[c][:, :])
            ins.then_inc(s_dout, 2)
            dve.wait_ge(s_deg, NDC)
            for c in range(4, NDC):
                ins = dve.tensor_copy(degrow[:, c * DC:c * DC + width(c)], m.PB[c - 4][:, 0:width(c)])
            chain(ins)
            dr = degrow.rearrange("p (a n) -> p a n", a=NCH)
            chain(dve.tensor_tensor(dr, dr, along(m.ident[:, :], NCH), ALU.mult))
            chain(dve.tensor_reduce(din, dr, op=ALU.add, axis=X))
            chain(dve.tensor_scalar(ns, dout, 1.0, None, ALU.max))
            dve.tensor_scalar(c1n, din, 1.0, None, ALU.max).then_inc(s_nvar, 1)
            dve.wait_ge(s_nstd, 2)
            chain(dve.reciprocal(ns, ns))
            chain(dve.reciprocal(c1n, c1n))
            chain(dve.scalar_tensor_tensor(ns, dout, 0.0, ns, ALU.is_gt, ALU.mult))
            chain(dve.scalar_tensor_tensor(c1n, din, 0.0, c1n, ALU.is_gt, ALU.mult))
            chain(dve.tensor_scalar(c1n, c1n, 1.0 - ALPHA, None, ALU.mult))
            chain(dve.tensor_tensor(c1s, c1n, ns, ALU.mult))
            for a in range(NCH):
                ps = lin.result(dve, a)
                ins = dve.tensor_tensor(h0[:, a, :], ps, bias_sb, ALU.add)
                ins.then_inc(lin.taken, 1)
            dve.wait_ge(lin.taken, NCH)
            chain(dve.tensor_reduce(gm, h0.rearrange("p a d -> p (a d)"), op=ALU.max, axis=X, apply_absolute_value=True))
            dve.tensor_scalar(gm, gm, 1e-30, None, ALU.max).then_inc(s_gm, 1)
            dve.wait_ge(s_gall, 1)
            chain(dve.reciprocal(ginv, gall))
            chain(dve.tensor_scalar(ginv, ginv, HSCALE, None, ALU.mult))
            chain(dve.tensor_scalar(gback, gall, 1.0 / HSCALE, None, ALU.mult))
            chain(dve.tensor_scalar(h0, h0, ginv, None, ALU.mult))
            chain(dve.tensor_tensor(hs, h0, spread(ns, D), ALU.mult))
            chain(dve.tensor_copy(z16[:, :, 0, :], hs))
            chain(dve.tensor_tensor(tmp, hs, z16[:, :, 0, :], ALU.subtract))
            chain(dve.tensor_scalar(z16[:, :, 1, :], tmp, LO, None, ALU.mult))
            zb = m.zbuf(1)
            chain(dve.memset(zb[:, NCH - 1, :, :], 0.0))
            chain(dve.tensor_scalar(h0, h0, ALPHA, None, ALU.mult))
            chain(dve.tensor_scalar(hs, hs, ALPHA, None, ALU.mult))


def stage_layer0_hops(nc, m, x):
    with ExitStack() as ctx:
        sem = lambda n: ctx.enter_context(nc.semaphore(n))
        counts = m.counts()
        z = [m.zbuf(0), m.zbuf(1)]
        comb = m.small(3)
        h0, hs0, tmp = m.node(1), m.node(2), m.node(3)
        xs = m.node(0)
        c1s, c1n, gback = m.colsN[:, 4, :], m.colsN[:, 5, :], m.colsN[:, 7, 3:4]
        rt = [m.work2[:, i * DC:(i + 1) * DC] for i in range(3)]
        prod_done = sem("hop_prod")
        copied = sem("hop_copied")
        back_done = sem("hop_back")
        mixed = sem("hop_mixed")
        s_dve = sem("hop_dve")
        s_x = sem("hop_x")
        block = ctx.enter_context(nc.Block())

        @block.tensor
        def _(pe):
            def back(t, c):
                pe.wait_ge(copied, NDC * t + c + 1)
                if c >= 2:
                    pe.wait_ge(mixed, NDC * t + c - 1)
                n = width(c)
                for i in range(-(-n // P)):
                    k = min(P, n - i * P)
                    ins = pe.matmul(m.PB[6 + c % 2][0:k, i * D:(i + 1) * D], rt[c % 3][:, i * P:i * P + k], comb,
                                    start=True, stop=True)
                ins.then_inc(back_done, 1)

            def hop(t, k, first=False):
                for c in range(NDC):
                    for a in range(NCH):
                        if c == 0 and a % GROUP == 0 and not first:
                            pe.wait_ge(mixed, NDC * (t - 1) + a // GROUP + 1)
                        ins = pe.matmul(m.PB[c % 4][:, 0:width(c)], z[k][:, a, :, :], counts[:, a, c * DC:c * DC + width(c)],
                                        start=(a == 0), stop=(a == NCH - 1))
                    ins.then_inc(prod_done, 1)
                    if c >= 1:
                        back(t, c - 1)
                back(t, NDC - 1)

            hop(0, 0, True)
            hop(1, 1)
            with pe.Fori(2, HOPS, 2) as t:
                hop(t, 0)
                hop(t + 1, 1)

        @block.scalar
        def _(act):
            with act.Fori(0, HOPS) as t:
                for c in range(NDC):
                    act.wait_ge(prod_done, NDC * t + c + 1)
                    if c >= 3:
                        act.wait_ge(back_done, NDC * t + c - 2)
                    nc.scalar.copy(rt[c % 3][:, 0:width(c)], m.PB[c % 4][:, 0:width(c)]).then_inc(copied, 1)

        @block.sync
        def _(sp):
            sp.wait_ge(prod_done, NDC * (HOPS - 1))
            sp.dma_start(xs, x).then_inc(s_x, 16)

        @block.vector
        def _(dve):
            def mix(t, k, n0, last):
                step = [n0]

                def chain(ins):
                    ins.then_inc(s_dve, 1)
                    step[0] = step[0] + 1
                    dve.wait_ge(s_dve, step[0])

                for c in range(NDC):
                    rows = P if c < NDC - 1 else width(c)
                    g = GROUP if c < NDC - 1 else 1
                    a = slice(c * GROUP, c * GROUP + g)
                    part = lambda v: v[0:rows, a]
                    sp_ = lambda v: v[0:rows, a].unsqueeze(2).to_broadcast([rows, g, D])
                    dve.wait_ge(back_done, NDC * t + c + 1)
                    ps = m.PB[6 + c % 2][0:rows, 0:g * D].rearrange("p (a d) -> p a d", a=g)
                    tc = tmp[0:rows, a, :]
                    if last:
                        chain(dve.tensor_tensor(tc, ps, sp_(c1n), ALU.mult))
                        chain(dve.tensor_tensor(tc, tc, h0[0:rows, a, :], ALU.add))
                        dve.scalar_tensor_tensor(xs[0:rows, a, :], tc, gback[0:rows, :], xs[0:rows, a, :], ALU.mult, ALU.add).then_inc(mixed, 1)
                    else:
                        zn = z[1 - k]
                        chain(dve.tensor_tensor(tc, ps, sp_(c1s), ALU.mult))
                        chain(dve.tensor_tensor(tc, tc, hs0[0:rows, a, :], ALU.add))
                        chain(dve.tensor_copy(zn[0:rows, a, 0, :], tc))
                        chain(dve.tensor_tensor(tc, tc, zn[0:rows, a, 0, :], ALU.subtract))
                        dve.tensor_scalar(zn[0:rows, a, 1, :], tc, LO, None, ALU.mult).then_inc(mixed, 1)

            per = 4 * NDC
            with dve.Fori(0, HOPS - 2, 2) as t:
                mix(t, 0, per * t, False)
                mix(t + 1, 1, per * (t + 1), False)
            mix(HOPS - 2, 0, per * (HOPS - 2), False)
            dve.wait_ge(s_x, 16)
            mix(HOPS - 1, 1, per * (HOPS - 1), True)


def stage_layer1(nc, m, aw, wts, biases):
    with ExitStack() as ctx:
        sem = lambda n: ctx.enter_context(nc.semaphore(n))
        NB = DC // BW
        st = [m.big[:, i * NB * BCOL:(i + 1) * NB * BCOL].rearrange("p (j c) -> p j c", j=NB) for i in range(2)]
        xs, tmp = m.node(0), m.node(3)
        z = [m.node(1), m.node(2)]
        w_sb = [m.small(i) for i in range(3)]
        b_sb = [m.small(3 + i) for i in range(3)]
        ones = m.work2[:, 2 * DC:2 * DC + P]
        rt = [m.work2[:, i * DC:(i + 1) * DC] for i in range(2)]
        degrow = m.big[:, 2 * NB * BCOL:2 * NB * BCOL + NPAD]
        mean, var, deg, dinv = (m.colsN[:, i, :] for i in range(4))
        s_in = sem("l1_in"); s_ones = sem("l1_ones"); s_dve = sem("l1_dve")
        s_ld = [sem("l1_ld0"), sem("l1_ld1")]; prod_done = sem("l1_prod"); copied = sem("l1_copied")
        back_done = sem("l1_back"); mixed = sem("l1_mixed"); s_var = sem("l1_var"); s_std = sem("l1_std"); s_z = sem("l1_z")
        block = ctx.enter_context(nc.Block())

        @block.sync
        def _(sp):
            def load(u, k, c, first=False):
                n = width(c) // BW
                if not first:
                    sp.wait_ge(prod_done, u - 1)
                sp.dma_start(st[k][:, 0:n, :], aw[c * NB:c * NB + n, :, :].rearrange("j p c -> p j c")).then_inc(s_ld[k], 16)

            load(0, 0, 0, True)
            load(1, 1, 1, True)
            for i in range(3):
                sp.dma_start(w_sb[i][0:D, :], wts[i]).then_inc(s_in, 16)
                sp.dma_start(b_sb[i], biases[i].partition_broadcast(P)).then_inc(s_in, 16)
            for u in range(2, 4 * NDC):
                load(u, u % 2, u % NDC)

        @block.tensor
        def _(pe):
            def product(l, c, lhsT, rows):
                u = l * NDC + c
                n = width(c)
                pe.wait_ge(s_ld[u % 2], 16 * (u // 2 + 1))
                out = m.PB[u % 3][0:rows, 0:n]
                for a in range(NCH):
                    ins = pe.matmul(out, lhsT(a), st[u % 2][:, 0:n // BW, a * BW:(a + 1) * BW], start=(a == 0),
                                    stop=(a == NCH - 1 and l == 0))
                if l:
                    for i in range(-(-n // P)):
                        k = min(P, n - i * P)
                        ins = pe.matmul(m.PB[u % 3][0:rows, i * P:i * P + k], lhsT(c * GROUP + i), m.ident[:, 0:k], start=False,
                                        stop=(i == -(-n // P) - 1))
                ins.then_inc(prod_done, 1)

            def back(l, c):
                u = (l - 1) * NDC + c
                pe.wait_ge(copied, u + NDC + 1)
                if u >= 2:
                    pe.wait_ge(mixed, u - 1)
                n = width(c)
                for i in range(-(-n // P)):
                    k = min(P, n - i * P)
                    ins = pe.matmul(m.PB[6 + u % 2][0:k, i * D:(i + 1) * D], rt[u % 2][0:D, i * P:i * P + k],
                                    w_sb[l - 1][0:D, :], start=True, stop=True)
                ins.then_inc(back_done, 1)

            pe.wait_ge(s_ones, 1)
            for c in range(NDC):
                if c >= 3:
                    pe.wait_ge(copied, c - 2)
                product(0, c, lambda a: ones, P)
            pe.wait_ge(s_in, 96)
            pe.wait_ge(s_z, 1)
            for l in range(1, 4):
                for c in range(NDC):
                    u = l * NDC + c
                    if l > 1 and c == 0:
                        pe.wait_ge(mixed, (l - 1) * NDC)
                    pe.wait_ge(copied, u - 2)
                    product(l, c, lambda a: z[(l - 1) % 2][:, a, :], D)
                    if c:
                        back(l, c - 1)
                back(l, NDC - 1)

        @block.scalar
        def _(act):
            for c in range(NDC):
                act.wait_ge(prod_done, c + 1)
                nc.scalar.copy(degrow[:, c * DC:c * DC + width(c)], m.PB[c % 3][:, 0:width(c)]).then_inc(copied, 1)
            for n in range(2):
                act.wait_ge(s_var, n + 1)
                v = (var, dinv)[n]
                nc.scalar.sqrt(v, v).then_inc(s_std, 1)
            for u in range(3 * NDC):
                act.wait_ge(prod_done, NDC + u + 1)
                if u >= 2:
                    act.wait_ge(back_done, u - 1)
                n = width(u % NDC)
                nc.scalar.copy(rt[u % 2][0:D, 0:n], m.PB[(NDC + u) % 3][0:D, 0:n]).then_inc(copied, 1)

        @block.vector
        def _(dve):
            chain = Chain(dve, s_dve)
            dve.memset(ones, 1.0).then_inc(s_ones, 1)
            dve_norm(dve, chain, z[0], xs, tmp, (mean, var), s_var, s_std, 1)
            chain(dve.tensor_scalar(z[0], z[0], 0.0, None, ALU.max))
            chain(dve.memset(degrow[:, NDST:], 0.0))
            chain(dve.memset(z[1][:, NCH - 1, :], 0.0))
            dve.wait_ge(copied, NDC)
            dr = degrow.rearrange("p (a n) -> p a n", a=NCH)
            chain(dve.tensor_tensor(dr, dr, along(m.ident[:, :], NCH), ALU.mult))
            chain(dve.tensor_reduce(deg, dr, op=ALU.add, axis=X))
            chain(dve.tensor_scalar(deg, deg, 1.0, None, ALU.add))
            dve.tensor_scalar(dinv, deg, 1e-30, None, ALU.max).then_inc(s_var, 1)
            dve.wait_ge(s_std, 2)
            chain(dve.reciprocal(dinv, dinv))
            chain(dve.scalar_tensor_tensor(dinv, deg, 0.0, dinv, ALU.is_gt, ALU.mult))
            dve.tensor_tensor(z[0], z[0], spread(dinv, D), ALU.mult).then_inc(s_z, 1)
            dve.wait_ge(s_in, 96)
            for u in range(3 * NDC):
                l, c = divmod(u, NDC)
                dve.wait_ge(back_done, u + 1)
                rows = P if c < NDC - 1 else width(c)
                g = GROUP if c < NDC - 1 else 1
                a = slice(c * GROUP, c * GROUP + g)
                ps = m.PB[6 + u % 2][0:rows, 0:g * D].rearrange("p (a d) -> p a d", a=g)
                di = dinv[0:rows, a].unsqueeze(2).to_broadcast([rows, g, D])
                bb = b_sb[l][0:rows, :].unsqueeze(1).to_broadcast([rows, g, D])
                tc = tmp[0:rows, a, :]
                chain(dve.tensor_tensor(tc, ps, di, ALU.mult))
                chain(dve.tensor_tensor(tc, tc, bb, ALU.add))
                if l < 2:
                    chain(dve.tensor_scalar(tc, tc, 0.0, None, ALU.max))
                    dve.tensor_tensor(z[1 - l][0:rows, a, :], tc, di, ALU.mult).then_inc(mixed, 1)
                else:
                    dve.tensor_tensor(xs[0:rows, a, :], xs[0:rows, a, :], tc, ALU.add).then_inc(mixed, 1)

HEADS = 2
HC = HEADS * D
DE = 32
VW = D + 1
SUM = (0, D)
VAL = (1, 0)
BIG = 1e30
LOW = 1e20
R = 6


class Visit:

    def __init__(self, g, c):
        self.g, self.c = g, c

    def __add__(self, n):
        return Visit(self.g, self.c + n)

    @property
    def fixed(self):
        return isinstance(self.g, int)

    @property
    def n(self):
        return self.g * R + self.c

    def slot(self, k):
        return self.c % k

    def landed(self):
        return (self.g + (self.c // R + 1)) * 16

    def exists(self):
        return not self.fixed or 0 <= self.n < V2


def walk(eng, step, before, after):
    head = 2 * R - 2
    rounds = (V2 - head) // R - 1
    for i in range(-before, head):
        step(Visit(0, i))
    with eng.Fori(0, rounds) as g:
        for u in range(R):
            step(Visit(g, head + u))
    for i in range(head + rounds * R, V2 + after):
        step(Visit(0, i))


def wait(eng, sem, n):
    if not isinstance(n, int) or n > 0:
        eng.wait_ge(sem, n)


class Take:
    def __init__(self, region):
        self.region, self.at = region, 0

    def __call__(self, n, rows=P):
        self.at += n
        return self.region[0:rows, self.at - n:self.at]


def stage_attend_tables(nc, m, keep, wq, wk, wv, bq, bk, bv, g1, b1, kv_t, q_t):
    with ExitStack() as ctx:
        sem = lambda n: ctx.enter_context(nc.semaphore(n))
        take = Take(m.big)
        kv = take(NCH * 2 * HC).rearrange("p (a c) -> p a c", a=NCH)
        qT = take(NCH * HEADS * P).rearrange("p (a h n) -> p a h n", a=NCH, h=HEADS)
        w_kv, w_q = take(2 * HC, D), take(HC, D)
        b_kv, bq_c = take(2 * HC), take(1)
        g_sb, b_sb = take(D), take(D)
        hT = [take(P, D) for _ in range(2)]
        xs, h, hn, tmp = (m.node(i) for i in range(4))
        mean, var = m.colsN[:, 0, :], m.colsN[:, 1, :]
        s_in = sem("at_in"); s_dve = sem("at_dve"); s_var = sem("at_var"); s_std = sem("at_std"); s_rows = sem("at_rows")
        turned = sem("at_turned"); copied = sem("at_copied"); done = sem("at_done"); taken = sem("at_taken"); s_out = sem("at_out")
        block = ctx.enter_context(nc.Block())

        @block.sync
        def _(sp):
            sp.dma_start(w_kv[:, 0:HC], wk).then_inc(s_in, 16)
            sp.dma_start(w_kv[:, HC:], wv).then_inc(s_in, 16)
            sp.dma_start(w_q, wq).then_inc(s_in, 16)
            sp.dma_start(b_kv[:, 0:HC], bk.partition_broadcast(P)).then_inc(s_in, 16)
            sp.dma_start(b_kv[:, HC:], bv.partition_broadcast(P)).then_inc(s_in, 16)
            sp.dma_start(bq_c, bq.unsqueeze(1)).then_inc(s_in, 16)
            sp.dma_start(g_sb, g1.partition_broadcast(P)).then_inc(s_in, 16)
            sp.dma_start(b_sb, b1.partition_broadcast(P)).then_inc(s_in, 16)
            for i in range(5):
                sp.wait_ge(taken, 5 * (i + 1))
                a = slice(5 * i, 5 * i + 5)
                sp.dma_start(kv_t[a, :, :].rearrange("a p c -> p a c"), kv[:, a, :]).then_inc(s_out, 16)
                sp.dma_start(q_t[a, :, :].rearrange("a p n -> p a n"), qT[:, a, :, :].rearrange("p a h n -> p a (h n)")).then_inc(s_out, 16)
            sp.wait_ge(s_out, 160)

        @block.tensor
        def _(pe):
            pe.wait_ge(s_rows, 1)
            pe.wait_ge(s_in, 128)
            for a in range(NCH + 1):
                if a < NCH:
                    wait(pe, copied, a - 1)
                    pe.transpose(m.PB[a % 2][0:D, 0:P], hn[:, a, :], m.ident[:, :]).then_inc(turned, 1)
                if a >= 1:
                    b = a - 1
                    pe.wait_ge(copied, b + 1)
                    wait(pe, taken, b - 1)
                    pe.matmul(m.PB[2 + b % 2][:, 0:2 * HC], hT[b % 2], w_kv, start=True, stop=True)
                    pe.matmul(m.PB[4 + b % 2][:, 0:P], w_q, hT[b % 2], start=True, stop=True).then_inc(done, 1)

        @block.scalar
        def _(act):
            for n in range(2):
                act.wait_ge(s_var, n + 1)
                nc.scalar.sqrt(var, var).then_inc(s_std, 1)
            for a in range(NCH):
                act.wait_ge(turned, a + 1)
                wait(act, done, a - 1)
                nc.scalar.copy(hT[a % 2], m.PB[a % 2][0:D, 0:P]).then_inc(copied, 1)

        @block.vector
        def _(dve):
            chain = Chain(dve, s_dve)
            chain(dve.memset(qT, 0.0))
            dve_norm(dve, chain, h, xs, tmp, (mean, var), s_var, s_std, 1)
            chain(dve.tensor_scalar(h, h, 0.0, None, ALU.max))
            dve_norm(dve, chain, hn, h, tmp, (mean, var), s_var, s_std, 2)
            dve.wait_ge(s_in, 128)
            chain(dve.tensor_tensor(hn, hn, along(g_sb, NCH), ALU.mult))
            dve.tensor_tensor(hn, hn, along(b_sb, NCH), ALU.add).then_inc(s_rows, 1)
            for a in range(NCH):
                dve.wait_ge(done, a + 1)
                dve.tensor_tensor(kv[:, a, :], m.PB[2 + a % 2][:, 0:2 * HC], b_kv, ALU.add)
                for hd in range(HEADS):
                    rows = slice(hd * D, (hd + 1) * D)
                    ins = dve.tensor_scalar(qT[rows, a, hd, :], m.PB[4 + a % 2][rows, 0:P], bq_c[rows, :], float(D) ** -0.5, ALU.add, ALU.mult)
                ins.then_inc(taken, 1)


def stage_attend(nc, m, keep, we, eaT, kv_t, q_t):
    with ExitStack() as ctx:
        sem = lambda n: ctx.enter_context(nc.semaphore(n))
        take = Take(m.big)
        halves = lambda a: a.rearrange("p (s c) -> p s c", s=2)
        acc = keep["acc"]
        take.at = keep["end"]
        nmax = take(NCH * HEADS).rearrange("p (a h) -> p a h", a=NCH)
        w_e = take(HC, DE)
        pen = take(P).bitcast(BF16)
        G = [halves(take(2 * 2 * HC)) for _ in range(R)]
        ea = [take(TE, DE) for _ in range(R)]
        qT = [take(HEADS * P) for _ in range(R)]
        KV = [halves(take(2 * 2 * (HC + 1))) for _ in range(R)]
        idx = take(2 * R).bitcast(I32)
        oh = [halves(take(P).bitcast(BF16)) for _ in range(3)]
        KT = [take(TE) for _ in range(2)]
        Pm = [take(2 * TE) for _ in range(2)]
        PT = [take(2 * TE) for _ in range(2)]
        nm = [take(HEADS) for _ in range(3)]
        rm, df = [take(HEADS) for _ in range(3)], [take(HEADS) for _ in range(3)]
        corr = [take(HEADS) for _ in range(3)]
        gateP, gz = take(1), take(1)
        assert take.at <= NCH * NDST // 2
        psE = halves(m.PB[0][:, 0:2 * HC])
        psK = m.PB[1][:, 0:TE]
        psS = [m.PB[2][:, :], m.PB[3][:, :]]
        psT = [m.PB[4][:, :], m.PB[5][:, :]]
        psA = [m.PB[6][:, 0:2 * VW], m.PB[7][:, 0:2 * VW]]

        init = sem("av_init"); s_in = sem("av_in")
        idx_ready = sem("av_idx")
        landed_g = [sem(f"av_g{i}") for i in range(R)]
        landed_e = [sem(f"av_e{i}") for i in range(R)]
        gated = sem("av_gated")
        e_done = sem("av_E")
        kv_ready = sem("av_kv")
        k_turned = sem("av_kT")
        k_copied = sem("av_kTs")
        oh_ready = sem("av_oh")
        scored = sem("av_S")
        max_ready = sem("av_max")
        exp_ready = sem("av_P")
        p_turned = sem("av_PT")
        p_copied = sem("av_PTs")
        summed = sem("av_A")
        s_small = sem("av_small")
        acc_ready = sem("av_acc")
        block = ctx.enter_context(nc.Block())

        @block.sync
        def _(sp):
            sp.dma_start(w_e, we).then_inc(s_in, 16)

            def step(v):
                k = v.slot(R)
                t = sp.value_load(m.vis[TILE2:TILE2 + 1, bass.ds(v.n, 1)], min_val=0, max_val=T1 - 1)
                j = sp.value_load(m.vis[BLOCK2:BLOCK2 + 1, bass.ds(v.n, 1)], min_val=0, max_val=J2 - 1)
                wait(sp, scored, v.n - R + 1)
                sp.dma_start(ea[k], eaT[:, bass.ds(t * TE, TE)]).then_inc(landed_e[k], 16)
                sp.dma_start(qT[k], q_t[bass.ds(j, 1), :, :].rearrange("j p n -> p (j n)")).then_inc(landed_e[k], 16)

            walk(sp, step, 0, 0)

        @block.gpsimd
        def _(po):
            po.wait_ge(init, 1)

            def step(v):
                k = v.slot(R)
                wait(po, idx_ready, v.n + 1)
                wait(po, kv_ready, v.n - R + 1)
                wait(po, gated, v.n)
                po.tensor_tensor(gateP, gz, gz, ALU.add).then_inc(gated, 1)
                for s in range(2):
                    po.indirect_dma_start(G[k][:, s, :], None, kv_t.rearrange("a p c -> (a p) c"), bass.IndirectOffsetOnAxis(
                        ap=idx[:, 2 * k + s:2 * k + s + 1], axis=0)).then_inc(landed_g[k], 16)

            walk(po, step, 0, 0)

        @block.tensor
        def _(pe):
            pe.wait_ge(init, 1)
            pe.wait_ge(s_in, 16)

            def step(i):
                v = i + 2
                if v.exists():
                    pe.wait_ge(landed_e[v.slot(R)], v.landed() * 2)
                    wait(pe, kv_ready, v.n)
                    for s in range(2):
                        ins = pe.matmul(psE[:, s, :], ea[v.slot(R)][:, s * P:(s + 1) * P], w_e, start=True, stop=True)
                    ins.then_inc(e_done, 1)
                v = i + 1
                if v.exists():
                    pe.wait_ge(kv_ready, v.n + 1)
                    wait(pe, k_copied, v.n)
                    for s in range(2):
                        ins = pe.transpose(psK[:, s * P:(s + 1) * P], KV[v.slot(R)][:, s, 0:HC], m.ident[:, :])
                    ins.then_inc(k_turned, 1)
                v = i
                if v.exists():
                    s = psS[v.slot(2)]
                    pe.wait_ge(oh_ready, v.n + 1)
                    wait(pe, exp_ready, v.n - 1)
                    for e in range(2):
                        pe.matmul(s.rearrange("p (h s e) -> p h s e", h=HEADS, s=2)[:, :, e, :], oh[v.slot(3)][:, e, :],
                                  pen, start=(e == 0), stop=False)
                    pe.wait_ge(k_copied, v.n + 1)
                    for h in range(HEADS):
                        ins = pe.matmul(s[:, h * TE:(h + 1) * TE], qT[v.slot(R)][:, h * P:(h + 1) * P], KT[v.slot(2)], start=False, stop=(h == 1))
                    ins.then_inc(scored, 1)
                v = i + -1
                if v.exists():
                    pe.wait_ge(exp_ready, v.n + 1)
                    wait(pe, p_copied, v.n - 1)
                    for x in range(2 * HEADS):
                        part = slice(x * P, (x + 1) * P)
                        ins = pe.transpose(psT[v.slot(2)][:, part], Pm[v.slot(2)][:, part], m.ident[:, :])
                    ins.then_inc(p_turned, 1)
                v = i + -2
                if v.exists():
                    pe.wait_ge(p_copied, v.n + 1)
                    wait(pe, acc_ready, v.n - 1)
                    for h in range(HEADS):
                        for s in range(2):
                            x = 2 * h + s
                            ins = pe.matmul(psA[v.slot(2)][:, h * VW:(h + 1) * VW], PT[v.slot(2)][:, x * P:(x + 1) * P],
                                            KV[v.slot(R)][:, s, HC + h * VW:HC + (h + 1) * VW], start=(s == 0), stop=(s == 1))
                    ins.then_inc(summed, 1)

            walk(pe, step, 2, 2)

        @block.scalar
        def _(act):
            def step(i):
                v = i + 1
                if v.exists():
                    act.wait_ge(k_turned, v.n + 1)
                    wait(act, scored, v.n - 1)
                    nc.scalar.copy(KT[v.slot(2)], psK).then_inc(k_copied, 1)
                v = i + -1
                if v.exists():
                    act.wait_ge(p_turned, v.n + 1)
                    wait(act, summed, v.n - 1)
                    nc.scalar.copy(PT[v.slot(2)], psT[v.slot(2)]).then_inc(p_copied, 1)
                v = i
                if v.exists():
                    act.wait_ge(max_ready, v.n + 1)
                    wait(act, p_turned, v.n - 1)
                    nc.scalar.activation(corr[v.slot(3)], df[v.slot(3)], ACT.Exp)
                    for h in range(HEADS):
                        ins = nc.scalar.activation(Pm[v.slot(2)][:, h * TE:(h + 1) * TE], psS[v.slot(2)][:, h * TE:(h + 1) * TE], ACT.Exp,
                                                   bias=nm[v.slot(3)][:, h:h + 1])
                    ins.then_inc(exp_ready, 1)

            walk(act, step, 2, 2)

        @block.vector
        def _(dve):
            dve.memset(nmax, LOW)
            dve.memset(gz, 0.0)
            dve.memset(gateP, 0.0)
            for k in range(R):
                dve.memset(KV[k][:, :, HC:HC + 1], 1.0)
                dve.memset(KV[k][:, :, 2 * HC + 1:], 1.0)
            for h in range(HEADS):
                dve.tensor_scalar(pen[:, h * P:(h + 1) * P], m.ident[:, :], BIG, None, ALU.mult)
            dve.memset(acc, 0.0).then_inc(init, 1)
            dve.wait_ge(init, 1)

            def index(v):
                if not v.fixed or v.n >= R:
                    dve.wait_ge(landed_g[v.slot(R)], (v + -R).landed() * 2)
                dve.tensor_scalar(idx[:, 2 * v.slot(R):2 * v.slot(R) + 2], m.src2[:, :, bass.ds(v.n, 1)].rearrange("p s v -> p (s v)"),
                                  0, None, ALU.add).then_inc(idx_ready, 1)

            def onehot(v):
                wait(dve, scored, v.n - 2)
                for s in range(2):
                    ins = dve.tensor_scalar(oh[v.slot(3)][:, s, :], m.iotaH[:, 0:P], m.rel2[:, s, bass.ds(v.n, 1)], -1.0, ALU.is_equal, ALU.add)
                ins.then_inc(oh_ready, 1)

            def step(i):
                v = i + 5
                if v.exists():
                    index(v)
                m0 = i
                small = 3 * m0.n
                if m0.exists():
                    j = dve.value_load(m.vis[BLOCK2:BLOCK2 + 1, bass.ds(m0.n, 1)], min_val=0, max_val=J2 - 1)
                    dve.wait_ge(scored, m0.n + 1)
                    s3 = m0.slot(3)
                    dve.tensor_reduce(rm[s3], psS[m0.slot(2)].rearrange("p (h e) -> p h e", h=HEADS), op=ALU.max, axis=X, negate=True).then_inc(s_small, 1)
                v = i + 2
                if v.exists():
                    dve.wait_ge(landed_g[v.slot(R)], v.landed() * 2)
                    dve.wait_ge(e_done, v.n + 1)
                    wait(dve, summed, v.n - R + 1)
                    k = v.slot(R)
                    dve.tensor_tensor(KV[k].rearrange("p s (x c) -> p s x c", x=2)[:, :, :, 0:HC],
                                      G[k].rearrange("p s (x c) -> p s x c", x=2),
                                      psE.unsqueeze(2).to_broadcast([P, 2, 2, HC]), ALU.add).then_inc(kv_ready, 1)
                if m0.exists():
                    nmj = nmax[:, bass.ds(j, 1), :].rearrange("p j h -> p (j h)")
                    dve.wait_ge(s_small, small + 1)
                    dve.tensor_tensor(nm[s3], nmj, rm[s3], ALU.min).then_inc(s_small, 1)
                v = i + 1
                if v.exists():
                    onehot(v)
                if m0.exists():
                    dve.wait_ge(s_small, small + 2)
                    dve.tensor_tensor(df[s3], nm[s3], nmj, ALU.subtract).then_inc(max_ready, 1)
                v = i + -2
                if v.exists():
                    ja = dve.value_load(m.vis[BLOCK2:BLOCK2 + 1, bass.ds(v.n, 1)], min_val=0, max_val=J2 - 1)
                    dve.wait_ge(summed, v.n + 1)
                    wait(dve, acc_ready, v.n)
                    for h in range(HEADS):
                        a = acc[:, bass.ds(ja, 1), h, :].rearrange("p j c -> p (j c)")
                        ins = dve.scalar_tensor_tensor(a, a, corr[v.slot(3)][:, h:h + 1], psA[v.slot(2)][:, h * VW:(h + 1) * VW], ALU.mult, ALU.add)
                    ins.then_inc(acc_ready, 1)
                if m0.exists():
                    dve.wait_ge(max_ready, m0.n + 1)
                    dve.tensor_scalar(nmj, nm[s3], 0.0, None, ALU.add).then_inc(s_small, 1)

            walk(dve, step, 5, 2)


def stage_nodes(nc, m, keep, wp, bp, g2, b2, w1, b1, w2, bb2, w3, b3, g_t):
    with ExitStack() as ctx:
        sem = lambda n: ctx.enter_context(nc.semaphore(n))
        take = Take(m.big)
        take.at = keep["end"]
        acc = keep["acc"]
        agg = take(NCH * HC).rearrange("p (a c) -> p a c", a=NCH)
        gt = take(NCH * D).rearrange("p (a d) -> p a d", a=NCH)
        rden = take(NCH * HEADS).rearrange("p (a h) -> p a h", a=NCH)
        w_p, w_1, w_2, w_3 = take(D), take(D, D), take(D, D), take(D, D)
        rows = [take(D) for _ in range(6)]
        bp_s, g2_s, b2_s, b1_s, bb2_s, b3_s = rows
        bufs = [take(P) for _ in range(2)]
        half = [b[0:D, :] for b in bufs]
        xs, h, t, tmp = (m.node(i) for i in range(4))
        mean, var = m.colsN[:, 0, :], m.colsN[:, 1, :]
        L = [Linear(nc, ctx, f"n{i}", m, bufs if i == 0 else half, HC if i == 0 else D, D) for i in range(4)]
        s_in = sem("nd_in"); s_dve = sem("nd_dve"); s_var = sem("nd_var"); s_std = sem("nd_std")
        s_rows = [sem(f"nd_rows{i}") for i in range(4)]; s_gelu = sem("nd_gelu"); s_out = sem("nd_out")
        s_g = sem("nd_g")
        block = ctx.enter_context(nc.Block())

        @block.sync
        def _(sp):
            for a, b in ((w_p, wp), (w_1, w1), (w_2, w2), (w_3, w3)):
                sp.dma_start(a, b).then_inc(s_in, 16)
            for a, b in zip(rows, (bp, g2, b2, b1, bb2, b3)):
                sp.dma_start(a, b.partition_broadcast(P)).then_inc(s_in, 16)
            sp.wait_ge(L[3].taken, NCH)
            sp.dma_start(g_t.rearrange("a p d -> p a d"), gt).then_inc(s_out, 16)
            sp.wait_ge(s_out, 16)

        @block.tensor
        def _(pe):
            pe.wait_ge(s_in, 160)
            for i, (src, w) in enumerate(((agg, w_p), (t, w_1), (t, w_2), (h, w_3))):
                pe.wait_ge(s_rows[i], 1)
                L[i].tensor(pe, lambda a, src=src: src[:, a, :], w)

        @block.scalar
        def _(act):
            L[0].scalar(act, nc)
            act.wait_ge(s_var, 1)
            nc.scalar.sqrt(var, var).then_inc(s_std, 1)
            L[1].scalar(act, nc)
            act.wait_ge(s_g, 1)
            nc.scalar.activation(t, tmp, ACT.Gelu).then_inc(s_rows[2], 1)
            L[2].scalar(act, nc)
            act.wait_ge(s_var, 2)
            nc.scalar.sqrt(var, var).then_inc(s_std, 1)
            L[3].scalar(act, nc)

        @block.vector
        def _(dve):
            chain = Chain(dve, s_dve)
            for hd in range(HEADS):
                chain(dve.tensor_scalar(rden[:, :, hd], acc[:, :, hd, SUM[hd]], 1e-8, None, ALU.add))
            chain(dve.reciprocal(rden, rden))
            for hd in range(HEADS):
                ins = dve.tensor_tensor(agg[:, :, hd * D:(hd + 1) * D], acc[:, :, hd, VAL[hd]:VAL[hd] + D], spread(rden[:, :, hd], D), ALU.mult)
            ins.then_inc(s_rows[0], 1)
            dve.wait_ge(s_in, 160)
            chain(dve.tensor_tensor(h, h, along(bp_s, NCH), ALU.add))
            for a in range(NCH):
                dve.tensor_tensor(h[:, a, :], L[0].result(dve, a), h[:, a, :], ALU.add).then_inc(L[0].taken, 1)
            dve.wait_ge(L[0].taken, NCH)
            dve_norm(dve, chain, t, h, tmp, (mean, var), s_var, s_std, 1)
            chain(dve.tensor_tensor(t, t, along(g2_s, NCH), ALU.mult))
            dve.tensor_tensor(t, t, along(b2_s, NCH), ALU.add).then_inc(s_rows[1], 1)
            for a in range(NCH):
                dve.tensor_tensor(tmp[:, a, :], L[1].result(dve, a), b1_s, ALU.add).then_inc(L[1].taken, 1)
            dve.wait_ge(L[1].taken, NCH)
            chain(dve.tensor_tensor(xs, xs, h, ALU.add))
            dve.tensor_tensor(xs, xs, along(bb2_s, NCH), ALU.add).then_inc(s_g, 1)
            dve.wait_ge(s_g, 1)
            for a in range(NCH):
                dve.tensor_tensor(xs[:, a, :], L[2].result(dve, a), xs[:, a, :], ALU.add).then_inc(L[2].taken, 1)
            dve.wait_ge(L[2].taken, NCH)
            dve_norm(dve, chain, h, xs, tmp, (mean, var), s_var, s_std, 2)
            dve.tensor_scalar(h, h, 0.0, None, ALU.max).then_inc(s_rows[3], 1)
            for a in range(NCH):
                dve.tensor_tensor(gt[:, a, :], L[3].result(dve, a), b3_s, ALU.add).then_inc(L[3].taken, 1)


def stage_messages(nc, m, keep, w1, efT, g_t):
    with ExitStack() as ctx:
        sem = lambda n: ctx.enter_context(nc.semaphore(n))
        take = Take(m.big)
        halves = lambda a: a.rearrange("p (s c) -> p s c", s=2)
        acc = keep["acc3"]
        take.at = keep["end"]
        w_e = take(D, D)
        G = [halves(take(2 * D)) for _ in range(R)]
        ef = [take(TE, D) for _ in range(R)]
        M = [halves(take(2 * VW)) for _ in range(3)]
        oh = [halves(take(2 * P)) for _ in range(3)]
        idx = take(2 * R).bitcast(I32)
        gateP, gz = take(1), take(1)
        psM = [halves(m.PB[0][:, 0:2 * D]), halves(m.PB[1][:, 0:2 * D])]
        psA = [m.PB[2][:, 0:VW], m.PB[3][:, 0:VW]]
        init = sem("ms_init"); s_in = sem("ms_in"); idx_ready = sem("ms_idx")
        landed_g = [sem(f"ms_g{i}") for i in range(R)]
        landed_e = [sem(f"ms_e{i}") for i in range(R)]
        gated = sem("ms_gated")
        m_done = sem("ms_M")
        m_ready = sem("ms_Ms")
        oh_ready = sem("ms_oh")
        summed = sem("ms_A")
        acc_ready = sem("ms_acc")
        block = ctx.enter_context(nc.Block())

        @block.sync
        def _(sp):
            sp.dma_start(w_e, w1).then_inc(s_in, 16)

            def step(v):
                t = sp.value_load(m.vis[TILE2:TILE2 + 1, bass.ds(v.n, 1)], min_val=0, max_val=T1 - 1)
                wait(sp, m_done, v.n - R + 1)
                sp.dma_start(ef[v.slot(R)], efT[:, bass.ds(t * TE, TE)]).then_inc(landed_e[v.slot(R)], 16)

            walk(sp, step, 0, 0)

        @block.gpsimd
        def _(po):
            po.wait_ge(init, 1)

            def step(v):
                k = v.slot(R)
                wait(po, idx_ready, v.n + 1)
                wait(po, m_done, v.n - R + 1)
                wait(po, gated, v.n)
                po.tensor_tensor(gateP, gz, gz, ALU.add).then_inc(gated, 1)
                for s in range(2):
                    po.indirect_dma_start(G[k][:, s, :], None, g_t.rearrange("a p c -> (a p) c"), bass.IndirectOffsetOnAxis(
                        ap=idx[:, 2 * k + s:2 * k + s + 1], axis=0)).then_inc(landed_g[k], 16)

            walk(po, step, 0, 0)

        @block.tensor
        def _(pe):
            pe.wait_ge(init, 1)
            pe.wait_ge(s_in, 16)

            def step(i):
                v = i + 1
                if v.exists():
                    k = v.slot(R)
                    pe.wait_ge(landed_e[k], v.landed())
                    wait(pe, m_ready, v.n - 1)
                    for s in range(2):
                        pe.matmul(psM[v.slot(2)][:, s, :], ef[k][:, s * P:(s + 1) * P], w_e, start=(s == 0), stop=False)
                    pe.wait_ge(landed_g[k], v.landed() * 2)
                    pe.matmul(psM[v.slot(2)], m.ident[:, :], G[k], start=False, stop=True).then_inc(m_done, 1)
                v = i
                if v.exists():
                    pe.wait_ge(m_ready, v.n + 1)
                    pe.wait_ge(oh_ready, v.n + 1)
                    wait(pe, acc_ready, v.n - 1)
                    for s in range(2):
                        ins = pe.matmul(psA[v.slot(2)], oh[v.slot(3)][:, s, :], M[v.slot(3)][:, s, :], start=(s == 0), stop=(s == 1))
                    ins.then_inc(summed, 1)

            walk(pe, step, 1, 0)

        @block.scalar
        def _(act):
            act.wait_ge(init, 1)

            def step(v):
                act.wait_ge(m_done, v.n + 1)
                wait(act, summed, v.n - 2)
                nc.scalar.activation(M[v.slot(3)][:, :, 0:D], psM[v.slot(2)], ACT.Relu).then_inc(m_ready, 1)

            walk(act, step, 0, 0)

        @block.vector
        def _(dve):
            dve.memset(gz, 0.0)
            dve.memset(gateP, 0.0)
            for k in range(3):
                dve.memset(M[k][:, :, D:], 1.0)
            dve.memset(acc, 0.0).then_inc(init, 1)
            dve.wait_ge(init, 1)

            def step(i):
                v = i + 4
                if v.exists():
                    k = v.slot(R)
                    if not v.fixed or v.n >= R:
                        dve.wait_ge(landed_g[k], (v + -R).landed() * 2)
                    dve.tensor_scalar(idx[:, 2 * k:2 * k + 2], m.src2[:, :, bass.ds(v.n, 1)].rearrange("p s v -> p (s v)"), 0, None,
                                      ALU.add).then_inc(idx_ready, 1)
                v = i + 1
                if v.exists():
                    wait(dve, summed, v.n - 2)
                    for s in range(2):
                        ins = dve.tensor_scalar(oh[v.slot(3)][:, s, :], m.iotaH[:, 0:P], m.rel2[:, s, bass.ds(v.n, 1)], None, ALU.is_equal)
                    ins.then_inc(oh_ready, 1)
                v = i + -1
                if v.exists():
                    j = dve.value_load(m.vis[BLOCK2:BLOCK2 + 1, bass.ds(v.n, 1)], min_val=0, max_val=J2 - 1)
                    dve.wait_ge(summed, v.n + 1)
                    wait(dve, acc_ready, v.n)
                    a = acc[:, bass.ds(j, 1), :].rearrange("p j c -> p (j c)")
                    dve.tensor_tensor(a, a, psA[v.slot(2)], ALU.add).then_inc(acc_ready, 1)

            walk(dve, step, 4, 1)


def stage_output(nc, m, keep, w2, b2, out):
    with ExitStack() as ctx:
        sem = lambda n: ctx.enter_context(nc.semaphore(n))
        take = Take(m.big)
        take.at = keep["end"]
        acc = keep["acc3"]
        both = take(NCH * HC).rearrange("p (a c) -> p a c", a=NCH)
        rcnt, w_s, b_s = take(NCH), take(D), take(D)
        bufs = [take(P) for _ in range(2)]
        xs, h, t, _ = (m.node(i) for i in range(4))
        L = Linear(nc, ctx, "o", m, bufs, HC, D)
        s_in = sem("o_in"); s_dve = sem("o_dve"); s_rows = sem("o_rows"); s_res = sem("o_res"); s_out = sem("o_out")
        s_t = sem("o_t")
        block = ctx.enter_context(nc.Block())

        @block.sync
        def _(sp):
            sp.dma_start(w_s, w2).then_inc(s_in, 16)
            sp.dma_start(b_s, b2.partition_broadcast(P)).then_inc(s_in, 16)
            full = NODES // P
            sp.wait_ge(s_res, NCH)
            sp.dma_start(out[0:full * P, :].rearrange("(a p) d -> p a d", p=P), xs[:, 0:full, :]).then_inc(s_out, 16)
            sp.dma_start(out[full * P:NODES, :], xs[0:NODES - full * P, full, :]).then_inc(s_out, 16)
            sp.wait_ge(s_out, 32)

        @block.tensor
        def _(pe):
            pe.wait_ge(s_in, 32)
            pe.wait_ge(s_rows, 1)
            L.tensor(pe, lambda a: both[:, a, :], w_s)

        @block.scalar
        def _(act):
            L.scalar(act, nc)

        @block.vector
        def _(dve):
            chain = Chain(dve, s_dve)
            chain(dve.tensor_scalar(rcnt, acc[:, :, D], 1.0, None, ALU.max))
            chain(dve.reciprocal(rcnt, rcnt))
            dve.tensor_copy(both[:, :, D:], h)
            dve.tensor_tensor(both[:, :, 0:D], acc[:, :, 0:D], spread(rcnt, D), ALU.mult).then_inc(s_rows, 1)
            dve.wait_ge(s_in, 32)
            for a in range(NCH):
                dve.tensor_tensor(t[:, a, :], L.result(dve, a), b_s, ALU.add).then_inc(L.taken, 1)
                dve.wait_ge(L.taken, a + 1)
                dve.scalar_tensor_tensor(xs[:, a, :], t[:, a, :], 0.0, xs[:, a, :], ALU.max, ALU.add).then_inc(s_res, 1)


def build(nc, last, x, src, dst, w, eaT, efT, L0_gnn_W, L0_gnn_b, L1_gnn_W1, L1_gnn_b1, L1_gnn_W2, L1_gnn_b2, L1_gnn_W3,
          L1_gnn_b3, L2_gnn_Wq, L2_gnn_bq, L2_gnn_Wk, L2_gnn_bk, L2_gnn_Wv, L2_gnn_bv, L2_gnn_We, L2_gnn_Wp, L2_gnn_bp, L2_gnn_ln1_g,
          L2_gnn_ln1_b, L2_gnn_ln2_g, L2_gnn_ln2_b, L2_gnn_W1, L2_gnn_b1, L2_gnn_W2, L2_gnn_b2, L3_gnn_W1, L3_gnn_b1, L3_gnn_W2,
          L3_gnn_b2, out):
    with ExitStack() as ctx:
        m = Mem(nc, ctx)
        scratch = lambda name, shape: nc.dram_tensor(name, shape, F32, kind="Internal").ap()
        aw = scratch("weights_dense", [J1 + RING, P, BCOL])
        kv_t = scratch("kv_table", [NCH, P, 2 * HC])
        q_t = scratch("q_table", [NCH, P, HEADS * P])
        g_t = scratch("message_table", [NCH, P, D])
        xv = x.rearrange("(a p) d -> p a d", p=P)
        half = lambda i: m.work[:, i * 2 * V1P:(i + 1) * 2 * V1P].rearrange("p (h v) -> p h v", h=2)
        behind = 4 * BCOL + OH * (4 * P + BCOL)
        t1 = dict(col=half(0), row=half(1), w=[half(2), half(3), half(4)],
                  keep=m.work2[:, behind:behind + V1P // 2].bitcast(BF16))
        keep = dict(acc=m.big[:, 0:NCH * HEADS * VW].rearrange("p (a h c) -> p a h c", a=NCH, h=HEADS),
                    acc3=m.big[:, 0:NCH * VW].rearrange("p (a c) -> p a c", a=NCH), end=NCH * HEADS * VW)
        tiles = lambda a: a.rearrange("(t e) -> t e", e=TE)
        stage_tables(nc, m, last, tiles(dst), tiles(src), tiles(w), t1)
        stage_build(nc, m, t1, aw)
        stage_layer0_start(nc, m, xv, L0_gnn_W, L0_gnn_b)
        stage_layer0_hops(nc, m, xv)
        stage_layer1(nc, m, aw, [L1_gnn_W1, L1_gnn_W2, L1_gnn_W3], [L1_gnn_b1, L1_gnn_b2, L1_gnn_b3])
        stage_attend_tables(nc, m, keep, L2_gnn_Wq, L2_gnn_Wk, L2_gnn_Wv, L2_gnn_bq, L2_gnn_bk, L2_gnn_bv, L2_gnn_ln1_g,
                            L2_gnn_ln1_b, kv_t, q_t)
        stage_attend(nc, m, keep, L2_gnn_We, eaT, kv_t, q_t)
        stage_nodes(nc, m, keep, L2_gnn_Wp, L2_gnn_bp, L2_gnn_ln2_g, L2_gnn_ln2_b, L2_gnn_W1, L2_gnn_b1, L2_gnn_W2, L2_gnn_b2,
                    L3_gnn_W1[D:, :], L3_gnn_b1, g_t)
        stage_messages(nc, m, keep, L3_gnn_W1[0:D, :], efT, g_t)
        stage_output(nc, m, keep, L3_gnn_W2, L3_gnn_b2, out)


WEIGHTS = ("L0_gnn_W", "L0_gnn_b", "L1_gnn_W1", "L1_gnn_b1", "L1_gnn_W2", "L1_gnn_b2", "L1_gnn_W3", "L1_gnn_b3", "L2_gnn_Wq",
           "L2_gnn_bq", "L2_gnn_Wk", "L2_gnn_bk", "L2_gnn_Wv", "L2_gnn_bv", "L2_gnn_We", "L2_gnn_Wp", "L2_gnn_bp", "L2_gnn_ln1_g",
           "L2_gnn_ln1_b", "L2_gnn_ln2_g", "L2_gnn_ln2_b", "L2_gnn_W1", "L2_gnn_b1", "L2_gnn_W2", "L2_gnn_b2", "L3_gnn_W1",
           "L3_gnn_b1", "L3_gnn_W2", "L3_gnn_b2")


def kernel(**inputs):
    import concourse.bacc as bacc
    from concourse.bass_utils import run_bass_kernel_spmd

    a = {k: np.asarray(v) for k, v in inputs.items()}
    more = EPAD - EDGES
    dst = np.pad(a["dst"], (0, more), constant_values=NDST - 1)
    src = np.pad(a["src"], (0, more))

    n = -(-T1 // P)
    last = np.ascontiguousarray(np.pad(dst[TE - 1::TE], (0, n * P - T1), constant_values=FAR).reshape(n, P).T)

    arrays = dict(
        last=last, x=np.pad(a["x"], ((0, NPAD - NODES), (0, 0))), src=src, dst=dst,
        w=np.pad(a["edge_weight"], (0, more)),
        eaT=np.ascontiguousarray(np.pad(a["edge_attr_32"], ((0, more), (0, 0))).T),
        efT=np.ascontiguousarray(np.pad(a["edge_attr_64"], ((0, more), (0, 0))).T),
        **{k: np.ascontiguousarray(a[k]) for k in WEIGHTS})
    nc = bacc.Bacc("TRN2", target_bir_lowering=False, num_devices=1)
    args = {k: nc.dram_tensor(f"in_{k}", v.shape, mybir.dt.from_np(v.dtype), kind="ExternalInput").ap() for k, v in arrays.items()}
    out = nc.dram_tensor("out_x", (NODES, D), F32, kind="ExternalOutput").ap()
    build(nc, out=out, **args)
    r = run_bass_kernel_spmd(nc, [{f"in_{k}": v for k, v in arrays.items()}], core_ids=[0])
    return r.results[0]["out_x"]
```

```python
from contextlib import ExitStack

import numpy as np

import concourse.bass as bass
from concourse import mybir

F32 = mybir.dt.float32
F16 = mybir.dt.float16
BF16 = mybir.dt.bfloat16
I32 = mybir.dt.int32
I16 = mybir.dt.int16
ALU = mybir.AluOpType
ACT = mybir.ActivationFunctionType
X = mybir.AxisListType.X

P = 128
NODES = 3125
EDGES = 103125
D = 64
NCH = 25
NPAD = NCH * P
HOPS = 10
ALPHA = 0.1
EPS = 1e-5

TE = 256
T1 = -(-EDGES // TE)
EPAD = T1 * TE
BW = 16
J1 = -(-NODES // BW)
NDST = J1 * BW
V1 = T1 + J1 - 1
V1P = 640
BCOL = NCH * BW
OH = 3
RING = 2
J2 = NCH
JPAD = 32
V2 = T1 + J2 - 1
V2P = 448
DC = 512
NDC = -(-NDST // DC)
BLOCK1, PLACE, TILE2, BLOCK2 = 0, 32, 64, 96
RM = 4
R = 8
FAR = 1 << 20


class Chain:

    def __init__(self, eng, sem):
        self.eng, self.sem, self.n = eng, sem, 0

    def __call__(self, ins):
        self.n += 1
        ins.then_inc(self.sem, 1)
        self.eng.wait_ge(self.sem, self.n)


def spread(v, n):
    return v.unsqueeze(2).to_broadcast([P, v.shape[1], n])


def along(v, k):
    return v.unsqueeze(1).to_broadcast([P, k, v.shape[1]])


class Mem:

    def __init__(self, nc, ctx):
        sb = lambda name, shape, dt: ctx.enter_context(nc.sbuf_tensor(name, shape, dt))
        self.big = sb("big", [P, NCH * NDST // 2], F32)
        self.work = sb("work", [P, 4 * NCH * D], F32)
        self.work2 = sb("work2", [P, NDST + NCH * D], F32)
        self.rel2 = sb("rel2", [P, 2, V2P], F32)
        self.src2 = sb("src2", [P, 2, V2P], I32)
        self.vis = sb("vis", [P, V1P], I16)
        self.ident = sb("ident", [P, P], F32)
        self.iotaH = sb("iotaH", [P, BCOL], F16)
        self.onesB = sb("onesB", [P, P], BF16)
        self.colsN = sb("colsN", [P, 8, NCH], F32)
        self.smalls = self.work2[:, 3 * DC + NCH * D:3 * DC + NCH * D + 8 * D]
        self.PB = [ctx.enter_context(nc.psum_tensor(f"bank{i}", [P, 512], F32)) for i in range(8)]

        sem = lambda n: ctx.enter_context(nc.semaphore(n))
        self.rows_landed = sem("rows_landed")
        self.kv_landed = [sem(f"kv_landed{i}") for i in range(R)]
        self.table_landed = [sem(f"table_landed{i}") for i in range(RM)]

    def tiles2(self):
        return self.vis[TILE2:TILE2 + 1, :].bitcast(I32)[:, 0:V2P // 2]

    def tiles_of(self, eng, n):
        x = eng.value_load(self.tiles2()[:, bass.ds(n // 2, 1)], min_val=0, max_val=T1 * T1 - 1)
        return x % T1, x // T1

    def blocks2(self):
        return self.vis[BLOCK2:BLOCK2 + 1, :].bitcast(I32)[:, 0:V2P // 2]

    def blocks_of(self, eng, n):
        x = eng.value_load(self.blocks2()[:, bass.ds(n // 2, 1)], min_val=0, max_val=JPAD ** 4 - 1)
        return [(x >> (5 * i)) & (JPAD - 1) for i in range(4)]

    def counts(self):
        return self.big[:, :].bitcast(F16).rearrange("p (a n) -> p a n", a=NCH)

    def small(self, i):
        return self.smalls[:, i * D:(i + 1) * D]

    def zbuf(self, k):
        base = self.work[:, 0:NCH * D] if k == 0 else self.work2[:, 3 * DC:3 * DC + NCH * D]
        return base.bitcast(F16).rearrange("p (a s d) -> p a s d", a=NCH, s=2)

    def node(self, i):
        return self.work[:, i * NCH * D:(i + 1) * NCH * D].rearrange("p (a d) -> p a d", a=NCH)


def stage_tables(nc, m, last, dst, src, w, t1):
    C = last.shape[1]
    K1, K2 = V1P // P, -(-V2P // P)
    with ExitStack() as ctx:
        sem = lambda n: ctx.enter_context(nc.semaphore(n))
        raw = m.big
        at = [0]

        def take(n):
            at[0] += n
            return raw[:, at[0] - n:at[0]]

        iotaI = take(V1P).bitcast(I32)
        iotaF = take(V1P)
        vmodI = take(V1P).bitcast(I32)
        vmodF = take(V1P)
        schemes = []
        lastI = take(C).bitcast(I32)
        for K, shift in ((K1, 4), (K2, 7)):
            VP = K * P
            schemes.append(dict(
                VP=VP, K=K, shift=shift, blkI=take(C).bitcast(I32),
                tI=take(C).bitcast(I32), blkF=take(C), tF=take(C), end=take(C), cmp=take(C * VP // 2).bitcast(BF16).rearrange("p (c v) -> p c v", c=C),
                tv=take(VP), tvc=take(VP), jv=take(VP + 2), tcol=take(K).bitcast(I32)))
        rowsI = take(K1 * 3 * TE + K2 * 2 * TE).bitcast(I32)
        rowsF = take(K1 * 4 * TE + K2 * 2 * TE)
        abI = take(K1 * 2 * TE).bitcast(I32)
        tabT = take(4 * 2 * V1P).rearrange("p (k h v) -> p k h v", k=4, h=2)
        valid, tmp = take(2 * V1P).rearrange("p (h v) -> p h v", h=2), take(2 * V1P).rearrange("p (h v) -> p h v", h=2)
        src2F = take(2 * V2P).rearrange("p (h v) -> p h v", h=2)
        wB = take(V1P).bitcast(BF16).rearrange("p (h v) -> p h v", h=2)
        r1 = rowsI[:, 0:K1 * 3 * TE].rearrange("p (k a e) -> p k a e", k=K1, a=3)
        r2 = rowsI[:, K1 * 3 * TE:].rearrange("p (k a e) -> p k a e", k=K2, a=2)
        f1 = rowsF[:, 0:K1 * 4 * TE].rearrange("p (k a e) -> p k a e", k=K1, a=4)
        f2 = rowsF[:, K1 * 4 * TE:].rearrange("p (k a e) -> p k a e", k=K2, a=2)
        ab = abI.rearrange("p (k a e) -> p k a e", k=K1, a=2)

        s_iota = sem("tab_iota"); s_last = sem("tab_last"); s_dve = sem("tab_dve"); s_cmp = sem("tab_cmp")
        s_tv = sem("tab_tv"); s_tvs = sem("tab_tvs"); s_tc = sem("tab_tcol"); s_tcs = sem("tab_tcols")
        s_rows = m.rows_landed; s_rowsF = sem("tab_rowsF"); s_tr = sem("tab_tr"); s_trs = sem("tab_trs")
        s_pool = sem("tab_pool"); s_dve2 = sem("tab_dve2")
        items = []
        for k in range(K1):
            for arr in range(4):
                for h in range(2):
                    items.append((f1[:, k, arr, h * P:(h + 1) * P], tabT[:, arr, h, k * P:(k + 1) * P]))
        for k in range(K2):
            for arr, to in enumerate((m.rel2, src2F)):
                for h in range(2):
                    items.append((f2[:, k, arr, h * P:(h + 1) * P], to[:, h, k * P:min((k + 1) * P, V2P)]))
        block = ctx.enter_context(nc.Block())

        @block.sync
        def _(sp):
            sp.dma_start(lastI, last).then_inc(s_last, 16)

        @block.gpsimd
        def _(po):
            po.iota(iotaI, pattern=[[1, V1P]], base=0, channel_multiplier=0).then_inc(s_iota, 1)
            po.iota(vmodI, pattern=[[0, V1P // RING], [1, RING]], base=0, channel_multiplier=0).then_inc(s_iota, 1)
            for s in schemes:
                po.iota(s["tI"], pattern=[[P, C]], base=0, channel_multiplier=1).then_inc(s_iota, 1)
            po.memset(m.ident[:, :], 0.0).then_inc(s_pool, 1)
            po.wait_ge(s_pool, 1)
            po.affine_select(out=m.ident[:, :], in_=m.ident[:, :], compare_op=ALU.not_equal, fill=1.0, base=0,
                             pattern=[[-1, P]], channel_multiplier=1).then_inc(s_iota, 1)
            po.wait_ge(s_tcs, 1)
            for k in range(K1):
                for a, arr in enumerate((dst, src)):
                    po.indirect_dma_start(r1[:, k, a, :], None, arr, bass.IndirectOffsetOnAxis(
                        ap=schemes[0]["tcol"][:, k:k + 1], axis=0)).then_inc(s_rows, 16)
                po.indirect_dma_start(r1[:, k, 2, :].bitcast(F32), None, w, bass.IndirectOffsetOnAxis(
                    ap=schemes[0]["tcol"][:, k:k + 1], axis=0)).then_inc(s_rows, 16)
            po.wait_ge(s_tcs, 2)
            for k in range(K2):
                for a, arr in enumerate((dst, src)):
                    po.indirect_dma_start(r2[:, k, a, :], None, arr, bass.IndirectOffsetOnAxis(
                        ap=schemes[1]["tcol"][:, k:k + 1], axis=0)).then_inc(s_rows, 16)

        @block.tensor
        def _(pe):
            pe.wait_ge(s_iota, 5)
            for n, s in enumerate(schemes):
                pe.wait_ge(s_cmp, n + 1)
                half = s["VP"] // 2
                for q in range(2):
                    for c in range(C):
                        ins = pe.matmul(m.PB[2 * n + q][:, 0:half], m.onesB[:, :], s["cmp"][:, c, q * half:(q + 1) * half],
                                        start=(c == 0), stop=(c == C - 1))
                ins.then_inc(s_tv, 1)
            for n, s in enumerate(schemes):
                pe.wait_ge(s_tvs, n + 1)
                for k in range(s["K"]):
                    ins = pe.transpose(m.PB[4 + 2 * n + k // 4][:, (k % 4) * P:(k % 4 + 1) * P], s["tvc"][:, k * P:(k + 1) * P], m.ident[:, :])
                ins.then_inc(s_tc, 1)
            pe.wait_ge(s_rowsF, 1)
            for i, (a, _) in enumerate(items):
                if i % 4 == 0 and i >= 8:
                    pe.wait_ge(s_trs, i // 4 - 1)
                ins = pe.transpose(m.PB[i // 4 % 2][:, (i % 4) * P:(i % 4 + 1) * P], a, m.ident[:, :])
                if i % 4 == 3 or i == len(items) - 1:
                    ins.then_inc(s_tr, 1)

        @block.scalar
        def _(act):
            for i0 in range(0, len(items), 4):
                act.wait_ge(s_tr, i0 // 4 + 1)
                for i in range(i0, min(i0 + 4, len(items))):
                    ins = nc.scalar.copy(items[i][1], m.PB[i // 4 % 2][:, (i % 4) * P:(i % 4) * P + items[i][1].shape[-1]])
                ins.then_inc(s_trs, 1)

        @block.vector
        def _(dve):
            chain = Chain(dve, s_dve)
            chain(dve.memset(m.onesB[:, :], 1.0))
            dve.wait_ge(s_iota, 5)
            chain(dve.tensor_copy(iotaF, iotaI))
            chain(dve.tensor_copy(vmodF, vmodI))
            chain(dve.tensor_copy(m.iotaH[:, :], iotaI[:, 0:BCOL]))
            dve.wait_ge(s_last, 16)
            for s in schemes:
                chain(dve.tensor_scalar(s["blkI"], lastI, s["shift"], None, ALU.arith_shift_right))
                chain(dve.tensor_copy(s["blkF"], s["blkI"]))
                chain(dve.tensor_copy(s["tF"], s["tI"]))
                chain(dve.tensor_tensor(s["end"], s["blkF"], s["tF"], ALU.add))
                for c in range(C):
                    ins = dve.tensor_scalar(s["cmp"][:, c, :], iotaF[:, 0:s["VP"]], s["end"][:, c:c + 1], None, ALU.is_gt)
                ins.then_inc(s_cmp, 1)
            for n, s in enumerate(schemes):
                dve.wait_ge(s_tv, n + 1)
                half = s["VP"] // 2
                for q in range(2):
                    part = slice(q * half, (q + 1) * half)
                    chain(dve.tensor_copy(s["tv"][:, part], m.PB[2 * n + q][:, 0:half]))
                dve.memset(s["jv"][:, 0:1], -1.0)
                chain(dve.tensor_tensor(s["jv"][:, 1:s["VP"] + 1], iotaF[:, 0:s["VP"]], s["tv"], ALU.subtract))
                dve.tensor_scalar(s["tvc"], s["tv"], float(T1 - 1), None, ALU.min).then_inc(s_tvs, 1)
            for n, s in enumerate(schemes):
                dve.wait_ge(s_tc, n + 1)
                for g in range(-(-s["K"] // 4)):
                    k = min(4, s["K"] - 4 * g)
                    ins = dve.tensor_copy(s["tcol"][:, 4 * g:4 * g + k],
                                          m.PB[4 + 2 * n + g][:, 0:k * P].rearrange("p (k v) -> p k v", k=k)[:, :, 0])
                ins.then_inc(s_tcs, 1)
            j1 = schemes[0]["jv"][:, 1:V1P + 1]
            dve.wait_ge(s_tvs, 2)
            more = tmp[:, 0, :]
            chain(dve.memset(more, 0.0))
            chain(dve.tensor_tensor(more[:, 0:V1 - 1], schemes[0]["jv"][:, 2:V1 + 1], j1[:, 0:V1 - 1], ALU.is_equal))
            spare = tmp[:, 1, :]
            chain(dve.tensor_scalar(spare, vmodF, float(J1), None, ALU.add))
            chain(dve.tensor_tensor(spare, spare, j1, ALU.subtract))
            chain(dve.tensor_tensor(spare, spare, more, ALU.mult))
            chain(dve.tensor_tensor(spare, spare, j1, ALU.add))
            chain(dve.tensor_scalar(m.vis[PLACE:PLACE + 1, 0:V1], spare[PLACE:PLACE + 1, 0:V1], 0.0, None, ALU.add))
            chain(dve.tensor_scalar(m.vis[BLOCK1:BLOCK1 + 1, 0:V1], j1[BLOCK1:BLOCK1 + 1, 0:V1], 0.0, None, ALU.add))
            chain(dve.tensor_tensor(t1["keep"], j1, schemes[0]["jv"][:, 0:V1P], ALU.is_equal))
            dve.wait_ge(s_rows, 16 * (3 * K1 + 2 * K2))
            for k in range(K1):
                chain(dve.tensor_scalar(ab[:, k, 0, :], r1[:, k, 1, :], 7, None, ALU.arith_shift_right))
                chain(dve.tensor_scalar(ab[:, k, 1, :], r1[:, k, 1, :], P - 1, None, ALU.bitwise_and))
                dve.tensor_copy(f1[:, k, 0, :], r1[:, k, 0, :])
                dve.tensor_copy(f1[:, k, 1, :], ab[:, k, 0, :])
                dve.tensor_copy(f1[:, k, 2, :], ab[:, k, 1, :])
                chain(dve.tensor_copy(f1[:, k, 3, :], r1[:, k, 2, :].bitcast(F32)))
            dve.tensor_copy(f2.rearrange("p k a e -> p (k a e)"), r2.rearrange("p k a e -> p (k a e)")).then_inc(s_rowsF, 1)
            dve.wait_ge(s_trs, -(-len(items) // 4))
            dstT, chT, rowT, wT = (tabT[:, i, :, :] for i in range(4))
            for h in range(2):
                chain(dve.scalar_tensor_tensor(tmp[:, h, :], j1, -float(BW), dstT[:, h, :], ALU.mult, ALU.add))
            chain(dve.tensor_scalar(valid, tmp, 0.0, None, ALU.is_ge))
            chain(dve.scalar_tensor_tensor(valid, tmp, float(BW - 1), valid, ALU.is_le, ALU.mult))
            chain(dve.scalar_tensor_tensor(tmp, chT, float(BW), tmp, ALU.mult, ALU.add))
            chain(dve.scalar_tensor_tensor(tmp, tmp, 1.0, valid, ALU.add, ALU.mult))
            chain(dve.tensor_scalar(t1["col"], tmp, -1.0, None, ALU.add))
            chain(dve.tensor_copy(t1["row"], rowT))
            for i in range(3):
                chain(dve.tensor_copy(wB, wT))
                chain(dve.tensor_copy(t1["w"][i], wB))
                if i < 2:
                    chain(dve.tensor_tensor(wT, wT, t1["w"][i], ALU.subtract))
            j2 = schemes[1]["jv"][:, 1:V2P + 1]
            for h in range(2):
                chain(dve.scalar_tensor_tensor(m.rel2[:, h, :], j2, -float(P), m.rel2[:, h, :], ALU.mult, ALU.add))
            chain(dve.tensor_copy(m.src2[:, :, :], src2F))
            two = schemes[1]["tvc"][TILE2:TILE2 + 1, 0:V2P].rearrange("p (k u) -> p k u", u=2)
            chain(dve.scalar_tensor_tensor(m.tiles2(), two[:, :, 1], float(T1), two[:, :, 0], ALU.mult, ALU.add))
            own = tmp[BLOCK2:BLOCK2 + 1, 0, 0:V2P + 4]
            chain(dve.memset(own, 0.0))
            chain(dve.tensor_scalar(own[:, 3:3 + V2P], j2[BLOCK2:BLOCK2 + 1, :], float(J2 - 1), None, ALU.min))
            four = own.rearrange("p (k u) -> p k u", u=2)
            four = [four[:, 0:V2P // 2, 0], four[:, 0:V2P // 2, 1], four[:, 1:1 + V2P // 2, 1], four[:, 2:2 + V2P // 2, 0]]
            more = tmp[BLOCK2:BLOCK2 + 1, 1, 0:V2P // 2]
            chain(dve.scalar_tensor_tensor(more, four[3], float(JPAD), four[2], ALU.mult, ALU.add))
            chain(dve.scalar_tensor_tensor(more, more, float(JPAD), four[1], ALU.mult, ALU.add))
            chain(dve.scalar_tensor_tensor(m.blocks2(), more, float(JPAD), four[0], ALU.mult, ALU.add))


def stage_build(nc, m, t1, aw):
    with ExitStack() as ctx:
        sem = lambda n: ctx.enter_context(nc.semaphore(n))
        cur_c = [m.work2[:, i * BCOL:(i + 1) * BCOL] for i in range(2)]
        cur_w = [m.work2[:, (2 + i) * BCOL:(3 + i) * BCOL] for i in range(2)]
        o = 4 * BCOL
        rows, cols = [], []
        for i in range(OH):
            rows.append(m.work2[:, o:o + 2 * 4 * P // 2].bitcast(BF16).rearrange("p (h k r) -> p h k r", h=2, k=4))
            o += 4 * P
            cols.append(m.work2[:, o:o + BCOL].bitcast(F16).rearrange("p (h c) -> p h c", h=2))
            o += BCOL
        gate, gateP, zero = m.colsN[:, 0, 0:1], m.colsN[:, 1, 0:1], m.colsN[:, 2, 0:1]
        psc = [m.PB[0], m.PB[1]]
        psw = [m.PB[2], m.PB[3]]
        counts = m.counts()

        oh_ready = sem("oh_ready")
        rows_ready = sem("rows_ready")
        vis_done = sem("vis_done")
        cur_ready = sem("cur_ready")
        cnt_stored = sem("cnt_stored")
        w_stored = [sem("w_stored0"), sem("w_stored1")]
        gated = sem("gated")
        gatedP = sem("gatedP")
        init = sem("build_init")
        block = ctx.enter_context(nc.Block())

        @block.sync
        def _(sp):
            with sp.Fori(0, V1, 2) as v:
                for k in range(2):
                    place = sp.value_load(m.vis[PLACE:PLACE + 1, bass.ds(v + k, 1)], min_val=0, max_val=J1 + RING - 1)
                    sp.wait_ge(cur_ready, v + k + 1)
                    sp.dma_start(aw[bass.ds(place, 1), :, :].rearrange("j p c -> p (j c)"), cur_w[k]).then_inc(w_stored[k], 16)
            for k in range(2):
                sp.wait_ge(w_stored[k], 16 * (V1 // 2))

        @block.vector
        def _(dve):
            dve.memset(zero, 0.0)
            dve.memset(gate, 0.0)
            dve.memset(gateP, 0.0)
            dve.memset(m.work2[:, 0:4 * BCOL], 0.0).then_inc(init, 1)
            dve.wait_ge(init, 1)

            def onehots(v, k, first=False):
                if not first:
                    dve.wait_ge(vis_done, v - OH + 1)
                for h in range(2):
                    dve.tensor_scalar(rows[k][:, h, 0, :], m.iotaH[:, 0:P], t1["row"][:, h, bass.ds(v, 1)], None, ALU.is_equal)
                    ins = dve.tensor_scalar(cols[k][:, h, :], m.iotaH[:, :], t1["col"][:, h, bass.ds(v, 1)], None, ALU.is_equal)
                ins.then_inc(oh_ready, 1)

            def running(v, k, first=False):
                keep = t1["keep"][:, bass.ds(v, 1)]
                dve.wait_ge(vis_done, v + 1)
                if not first:
                    dve.wait_ge(cnt_stored, v - 1)
                    dve.wait_ge(w_stored[k], 8 * (v - k))
                if not first or k:
                    dve.wait_ge(cur_ready, v)
                dve.scalar_tensor_tensor(cur_c[k], cur_c[1 - k], keep, psc[k][:, 0:BCOL], ALU.mult, ALU.add)
                dve.scalar_tensor_tensor(cur_w[k], cur_w[1 - k], keep, psw[k][:, 0:BCOL], ALU.mult, ALU.add).then_inc(cur_ready, 1)

            onehots(0, 0, True)
            onehots(1, 1, True)
            onehots(2, 2, True)
            running(0, 0, True)
            onehots(3, 0)
            running(1, 1, True)
            with dve.Fori(2, V1 - 2, 6) as v:
                for u in range(6):
                    onehots(v + u + 2, (4 + u) % OH)
                    running(v + u, u % 2)
            running(V1 - 2, 0)
            running(V1 - 1, 1)

        @block.scalar
        def _(act):
            act.wait_ge(init, 1)

            def weigh(v, k):
                act.wait_ge(gated, v)
                act.wait_ge(oh_ready, v + 1)
                nc.scalar.copy(gate, zero).then_inc(gated, 1)
                for h in range(2):
                    for i in range(3):
                        ins = nc.scalar.activation(rows[k][:, h, 1 + i, :], rows[k][:, h, 0, :], ACT.Copy,
                                                   scale=t1["w"][i][:, h, bass.ds(v, 1)])
                ins.then_inc(rows_ready, 1)

            weigh(0, 0)
            weigh(1, 1)
            with act.Fori(2, V1 - 2, 6) as v:
                for u in range(6):
                    weigh(v + u, (2 + u) % OH)
            weigh(V1 - 2, (V1 - 2) % OH)
            weigh(V1 - 1, (V1 - 1) % OH)

        @block.tensor
        def _(pe):
            def products(v, k, r, first=False, last=False):
                pe.wait_ge(rows_ready, v + 1)
                if not first:
                    pe.wait_ge(cur_ready, v - 1)
                for h in range(2):
                    pe.matmul(psc[k][:, 0:BCOL], rows[r][:, h, 0, :], cols[r][:, h, :], start=(h == 0), stop=(h == 1))
                    pe.matmul(m.PB[4][:, 0:BCOL], rows[r][:, h, 0, :], cols[r][:, h, :],
                              start=(first and v == 0 and h == 0), stop=(last and h == 1))
                    for i in range(3):
                        ins = pe.matmul(psw[k][:, 0:BCOL], rows[r][:, h, 1 + i, :], cols[r][:, h, :],
                                        start=(h == 0 and i == 0), stop=(h == 1 and i == 2))
                ins.then_inc(vis_done, 1)

            products(0, 0, 0, True)
            products(1, 1, 1, True)
            with pe.Fori(2, V1 - 2, 6) as v:
                for u in range(6):
                    products(v + u, u % 2, (2 + u) % OH)
            products(V1 - 2, 0, (V1 - 2) % OH)
            products(V1 - 1, 1, (V1 - 1) % OH, last=True)

        @block.gpsimd
        def _(po):
            po.wait_ge(init, 1)
            with po.Fori(0, V1, 2) as v:
                for k in range(2):
                    j = po.value_load(m.vis[BLOCK1:BLOCK1 + 1, bass.ds(v + k, 1)], min_val=0, max_val=J1 - 1)
                    po.wait_ge(cnt_stored, v + k)
                    po.wait_ge(cur_ready, v + k + 1)
                    po.tensor_tensor(gateP, zero, zero, ALU.add).then_inc(gatedP, 1)
                    po.tensor_copy(counts[:, :, bass.ds(j * BW, BW)], cur_c[k].rearrange("p (a w) -> p a w", a=NCH)).then_inc(cnt_stored, 1)

GROUP = DC // P
LO = 2048.0
HSCALE = 16.0


NG = -(-NCH // GROUP)


def chunks(g):
    return range(g * GROUP, min(NCH, (g + 1) * GROUP))


def of_group(v, g):
    return v[:, g * GROUP:min(NCH, (g + 1) * GROUP)]


def width(c):
    return min(DC, NDST - c * DC)


def dve_norm(dve, chain, out, x, tmp, stat, var_ready, std_ready, n):
    mean, var = stat
    chain(dve.tensor_reduce(mean, x, op=ALU.add, axis=X))
    chain(dve.tensor_scalar(mean, mean, 1.0 / D, None, ALU.mult))
    chain(dve.tensor_tensor(out, x, spread(mean, D), ALU.subtract))
    chain(dve.tensor_tensor(tmp, out, out, ALU.mult))
    chain(dve.tensor_reduce(var, tmp, op=ALU.add, axis=X))
    dve.tensor_scalar(var, var, 1.0 / D, EPS, ALU.mult, ALU.add).then_inc(var_ready, 1)
    dve.wait_ge(std_ready, n)
    chain(dve.reciprocal(var, var))
    chain(dve.tensor_tensor(out, out, spread(var, D), ALU.mult))


class Linear:

    def __init__(self, nc, ctx, name, m, bufs, cin, cout, banks=(0, 1, 2, 3), more=()):
        sem = lambda n: ctx.enter_context(nc.semaphore(f"{name}_{n}"))
        self.turned, self.copied, self.done, self.taken = sem("turned"), sem("copied"), sem("done"), sem("taken")
        self.bufs = bufs
        self.cin, self.cout = cin, cout
        self.psT = [[m.PB[banks[0]], m.PB[banks[1]]]] + [[m.PB[b] for b in more]] * (len(bufs) - 1)
        self.psO = [m.PB[banks[2]], m.PB[banks[3]]]
        self.ident = m.ident[:, :]

    def tensor(self, pe, *parts):
        for g in range(NG + 1):
            if g < NG:
                if g >= 2:
                    pe.wait_ge(self.copied, g - 1)
                for i, (rows, _) in enumerate(parts):
                    for k, a in enumerate(chunks(g)):
                        ins = pe.transpose(self.psT[i][g % 2][0:self.cin, k * P:(k + 1) * P], rows(a), self.ident)
                ins.then_inc(self.turned, 1)
            if g >= 1:
                b = g - 1
                pe.wait_ge(self.copied, b + 1)
                if b >= 2:
                    pe.wait_ge(self.taken, b - 1)
                for k in range(len(chunks(b))):
                    for i, (_, weight) in enumerate(parts):
                        ins = pe.matmul(self.psO[b % 2][:, k * self.cout:(k + 1) * self.cout], self.bufs[i][b % 2][:, k * P:(k + 1) * P],
                                        weight, start=(i == 0), stop=(i == len(parts) - 1))
                ins.then_inc(self.done, 1)

    def scalar(self, act, nc):
        for g in range(NG):
            act.wait_ge(self.turned, g + 1)
            if g >= 2:
                act.wait_ge(self.done, g - 1)
            n = len(chunks(g)) * P
            for buf, ps in zip(self.bufs, self.psT):
                ins = nc.scalar.copy(buf[g % 2][:, 0:n], ps[g % 2][0:self.cin, 0:n])
            ins.then_inc(self.copied, 1)

    def result(self, eng, g):
        eng.wait_ge(self.done, g + 1)
        n = len(chunks(g))
        return self.psO[g % 2][:, 0:n * self.cout].rearrange("p (a c) -> p a c", a=n)


def stage_layer0_start(nc, m, x, wt, bias):
    with ExitStack() as ctx:
        sem = lambda n: ctx.enter_context(nc.semaphore(n))
        small = m.small
        w_sb, bias_sb = small(0), small(1)
        ones16 = small(2).bitcast(F16)
        comb = small(3)
        buf = [m.work2[0:D, i * DC:(i + 1) * DC] for i in range(2)]
        lin = Linear(nc, ctx, "l0", m, [buf], D, D, banks=(5, 6, 7, 4))
        xs, h0, hs, tmp = m.work2[:, 1536:3136].rearrange("p (a d) -> p a d", a=NCH), m.node(1), m.node(2), m.node(3)
        degrow = m.work[:, 2 * NCH * D:4 * NCH * D]
        counts = m.counts()
        cols = m.colsN
        mean, var, din, dout, c1s, c1n, ns = (cols[:, i, :] for i in range(7))
        gm = cols[:, 7, 0:1]; gall = cols[:, 7, 1:2]; ginv = cols[:, 7, 2:3]; gback = cols[:, 7, 3:4]
        s_in = sem("l0_in"); s_dve = sem("l0_dve"); s_one = sem("l0_one"); s_var = sem("l0_var"); s_std = sem("l0_std")
        s_rows = sem("l0_rows"); s_deg = sem("l0_deg"); s_gm = sem("l0_gm"); s_gall = sem("l0_gall")
        s_nvar = sem("l0_nvar"); s_nstd = sem("l0_nstd"); s_dout = sem("l0_dout")
        z16 = m.node(0).rearrange("p a d -> p (a d)").bitcast(F16).rearrange("p (a s d) -> p a s d", a=NCH, s=2)
        block = ctx.enter_context(nc.Block())

        @block.sync
        def _(sp):
            sp.dma_start(xs, x).then_inc(s_in, 16)
            sp.dma_start(w_sb[0:D, :], wt).then_inc(s_in, 16)
            sp.dma_start(bias_sb, bias.partition_broadcast(P)).then_inc(s_in, 16)

        @block.tensor
        def _(pe):
            pe.wait_ge(s_one, 1)
            for c in range(4):
                pe.matmul(m.PB[c][:, 0:width(c)], ones16, counts[:, 0, c * DC:c * DC + width(c)], start=True, stop=False)
            with pe.Fori(1, NCH - 1) as a:
                for c in range(4):
                    pe.matmul(m.PB[c][:, 0:width(c)], ones16, counts[:, bass.ds(a, 1), c * DC:c * DC + width(c)],
                              start=False, stop=False)
            for c in range(4):
                pe.matmul(m.PB[c][:, 0:width(c)], ones16, counts[:, NCH - 1, c * DC:c * DC + width(c)],
                          start=False, stop=True).then_inc(s_deg, 1)
            pe.wait_ge(s_dout, 2)
            for c in range(4, NDC):
                pe.matmul(m.PB[c - 4][:, 0:width(c)], ones16, counts[:, 0, c * DC:c * DC + width(c)], start=True, stop=False)
            with pe.Fori(1, NCH - 1) as a:
                for c in range(4, NDC):
                    pe.matmul(m.PB[c - 4][:, 0:width(c)], ones16, counts[:, bass.ds(a, 1), c * DC:c * DC + width(c)],
                              start=False, stop=False)
            for c in range(4, NDC):
                pe.matmul(m.PB[c - 4][:, 0:width(c)], ones16, counts[:, NCH - 1, c * DC:c * DC + width(c)],
                          start=False, stop=True).then_inc(s_deg, 1)
            pe.wait_ge(s_rows, 1)
            pe.wait_ge(s_in, 48)
            lin.tensor(pe, (lambda a: h0[:, a, :], w_sb[0:D, :]))

        @block.scalar
        def _(act):
            act.wait_ge(s_var, 1)
            nc.scalar.sqrt(var, var).then_inc(s_std, 1)
            act.wait_ge(s_nvar, 1)
            nc.scalar.sqrt(ns, ns).then_inc(s_nstd, 1)
            nc.scalar.sqrt(c1n, c1n).then_inc(s_nstd, 1)
            lin.scalar(act, nc)

        @block.gpsimd
        def _(po):
            po.wait_ge(s_gm, 1)
            po.partition_all_reduce(gall, gm, P, bass.bass_isa.ReduceOp.max).then_inc(s_gall, 1)

        @block.vector
        def _(dve):
            chain = Chain(dve, s_dve)
            dve.memset(ones16, 1.0).then_inc(s_one, 1)
            dve.tensor_copy(comb[0:D, :], m.ident[0:D, 0:D])
            chain(dve.tensor_scalar(comb[D:P, :], m.ident[D:P, D:P], 1.0 / LO, None, ALU.mult))
            dve.wait_ge(s_in, 48)
            dve_norm(dve, chain, h0, xs, tmp, (mean, var), s_var, s_std, 1)
            dve.tensor_scalar(h0, h0, 0.0, None, ALU.max).then_inc(s_rows, 1)
            chain(dve.memset(degrow[:, NDST:], 0.0))
            chain(dve.tensor_reduce(dout, m.PB[4][:, 0:BCOL].rearrange("p (a w) -> p a w", a=NCH), op=ALU.add, axis=X))
            dve.wait_ge(s_deg, 4)
            for c in range(4):
                ins = dve.tensor_copy(degrow[:, c * DC:(c + 1) * DC], m.PB[c][:, :])
            ins.then_inc(s_dout, 2)
            dve.wait_ge(s_deg, NDC)
            for c in range(4, NDC):
                ins = dve.tensor_copy(degrow[:, c * DC:c * DC + width(c)], m.PB[c - 4][:, 0:width(c)])
            chain(ins)
            dr = degrow.rearrange("p (a n) -> p a n", a=NCH)
            chain(dve.tensor_tensor(dr, dr, along(m.ident[:, :], NCH), ALU.mult))
            chain(dve.tensor_reduce(din, dr, op=ALU.add, axis=X))
            chain(dve.tensor_scalar(ns, dout, 1.0, None, ALU.max))
            dve.tensor_scalar(c1n, din, 1.0, None, ALU.max).then_inc(s_nvar, 1)
            dve.wait_ge(s_nstd, 2)
            chain(dve.reciprocal(ns, ns))
            chain(dve.reciprocal(c1n, c1n))
            chain(dve.scalar_tensor_tensor(ns, dout, 0.0, ns, ALU.is_gt, ALU.mult))
            chain(dve.scalar_tensor_tensor(c1n, din, 0.0, c1n, ALU.is_gt, ALU.mult))
            chain(dve.tensor_scalar(c1n, c1n, 1.0 - ALPHA, None, ALU.mult))
            chain(dve.tensor_tensor(c1s, c1n, ns, ALU.mult))
            for g in range(NG):
                ps = lin.result(dve, g)
                dve.tensor_tensor(of_group(h0, g), ps, along(bias_sb, len(chunks(g))), ALU.add).then_inc(lin.taken, 1)
            dve.wait_ge(lin.taken, NG)
            chain(dve.tensor_reduce(gm, h0.rearrange("p a d -> p (a d)"), op=ALU.max, axis=X, apply_absolute_value=True))
            dve.tensor_scalar(gm, gm, 1e-30, None, ALU.max).then_inc(s_gm, 1)
            dve.wait_ge(s_gall, 1)
            chain(dve.reciprocal(ginv, gall))
            chain(dve.tensor_scalar(ginv, ginv, HSCALE, None, ALU.mult))
            chain(dve.tensor_scalar(gback, gall, 1.0 / HSCALE, None, ALU.mult))
            chain(dve.tensor_scalar(h0, h0, ginv, None, ALU.mult))
            chain(dve.tensor_tensor(hs, h0, spread(ns, D), ALU.mult))
            chain(dve.tensor_copy(z16[:, :, 0, :], hs))
            chain(dve.tensor_tensor(tmp, hs, z16[:, :, 0, :], ALU.subtract))
            chain(dve.tensor_scalar(z16[:, :, 1, :], tmp, LO, None, ALU.mult))
            zb = m.zbuf(1)
            chain(dve.memset(zb[:, NCH - 1, :, :], 0.0))
            chain(dve.tensor_scalar(h0, h0, ALPHA, None, ALU.mult))
            chain(dve.tensor_scalar(hs, hs, ALPHA, None, ALU.mult))


def stage_layer0_hops(nc, m, x):
    with ExitStack() as ctx:
        sem = lambda n: ctx.enter_context(nc.semaphore(n))
        counts = m.counts()
        z = [m.zbuf(0), m.zbuf(1)]
        comb = m.small(3)
        h0, hs0, tmp = m.node(1), m.node(2), m.node(3)
        xs = m.node(0)
        c1s, c1n, gback = m.colsN[:, 4, :], m.colsN[:, 5, :], m.colsN[:, 7, 3:4]
        rt = [m.work2[:, i * DC:(i + 1) * DC] for i in range(3)]
        prod_done = sem("hop_prod")
        copied = sem("hop_copied")
        back_done = sem("hop_back")
        mixed = sem("hop_mixed")
        s_dve = sem("hop_dve")
        s_x = sem("hop_x")
        block = ctx.enter_context(nc.Block())

        @block.tensor
        def _(pe):
            def back(t, c):
                pe.wait_ge(copied, NDC * t + c + 1)
                if c >= 2:
                    pe.wait_ge(mixed, NDC * t + c - 1)
                n = width(c)
                for i in range(-(-n // P)):
                    k = min(P, n - i * P)
                    ins = pe.matmul(m.PB[6 + c % 2][0:k, i * D:(i + 1) * D], rt[c % 3][:, i * P:i * P + k], comb,
                                    start=True, stop=True)
                ins.then_inc(back_done, 1)

            def hop(t, k, first=False):
                for c in range(NDC):
                    for a in range(NCH):
                        if c == 0 and a % GROUP == 0 and not first:
                            pe.wait_ge(mixed, NDC * (t - 1) + a // GROUP + 1)
                        ins = pe.matmul(m.PB[c % 4][:, 0:width(c)], z[k][:, a, :, :], counts[:, a, c * DC:c * DC + width(c)],
                                        start=(a == 0), stop=(a == NCH - 1))
                    ins.then_inc(prod_done, 1)
                    if c >= 1:
                        back(t, c - 1)
                back(t, NDC - 1)

            hop(0, 0, True)
            hop(1, 1)
            with pe.Fori(2, HOPS, 2) as t:
                hop(t, 0)
                hop(t + 1, 1)

        @block.scalar
        def _(act):
            with act.Fori(0, HOPS) as t:
                for c in range(NDC):
                    act.wait_ge(prod_done, NDC * t + c + 1)
                    if c >= 3:
                        act.wait_ge(back_done, NDC * t + c - 2)
                    nc.scalar.copy(rt[c % 3][:, 0:width(c)], m.PB[c % 4][:, 0:width(c)]).then_inc(copied, 1)

        @block.sync
        def _(sp):
            sp.wait_ge(prod_done, NDC * (HOPS - 1))
            sp.dma_start(xs, x).then_inc(s_x, 16)

        @block.vector
        def _(dve):
            def mix(t, k, n0, last):
                step = [n0]

                def chain(ins):
                    ins.then_inc(s_dve, 1)
                    step[0] = step[0] + 1
                    dve.wait_ge(s_dve, step[0])

                for c in range(NDC):
                    rows = P if c < NDC - 1 else width(c)
                    g = GROUP if c < NDC - 1 else 1
                    a = slice(c * GROUP, c * GROUP + g)
                    part = lambda v: v[0:rows, a]
                    sp_ = lambda v: v[0:rows, a].unsqueeze(2).to_broadcast([rows, g, D])
                    dve.wait_ge(back_done, NDC * t + c + 1)
                    ps = m.PB[6 + c % 2][0:rows, 0:g * D].rearrange("p (a d) -> p a d", a=g)
                    tc = tmp[0:rows, a, :]
                    if last:
                        chain(dve.tensor_tensor(tc, ps, sp_(c1n), ALU.mult))
                        chain(dve.tensor_tensor(tc, tc, h0[0:rows, a, :], ALU.add))
                        dve.scalar_tensor_tensor(xs[0:rows, a, :], tc, gback[0:rows, :], xs[0:rows, a, :], ALU.mult, ALU.add).then_inc(mixed, 1)
                    else:
                        zn = z[1 - k]
                        chain(dve.tensor_tensor(tc, ps, sp_(c1s), ALU.mult))
                        chain(dve.tensor_tensor(tc, tc, hs0[0:rows, a, :], ALU.add))
                        chain(dve.tensor_copy(zn[0:rows, a, 0, :], tc))
                        chain(dve.tensor_tensor(tc, tc, zn[0:rows, a, 0, :], ALU.subtract))
                        dve.tensor_scalar(zn[0:rows, a, 1, :], tc, LO, None, ALU.mult).then_inc(mixed, 1)

            per = 4 * NDC
            with dve.Fori(0, HOPS - 2, 2) as t:
                mix(t, 0, per * t, False)
                mix(t + 1, 1, per * (t + 1), False)
            mix(HOPS - 2, 0, per * (HOPS - 2), False)
            dve.wait_ge(s_x, 16)
            mix(HOPS - 1, 1, per * (HOPS - 1), True)


def stage_layer1(nc, m, aw, wts, biases):
    with ExitStack() as ctx:
        sem = lambda n: ctx.enter_context(nc.semaphore(n))
        NB = DC // BW
        last = width(NDC - 1) // BW
        st = [m.big[:, i * NB * BCOL:(i + 1) * NB * BCOL].rearrange("p (j c) -> p j c", j=NB) for i in range(2)]
        behind = 2 * NB * BCOL + last * BCOL
        st.append(m.big[:, 2 * NB * BCOL:behind].rearrange("p (j c) -> p j c", j=last))
        buffer = lambda c: 2 if c == NDC - 1 else c % 2
        loads = lambda l, c: l + 1 if c == NDC - 1 else (NDC // 2) * l + c // 2 + 1
        xs, tmp = m.node(0), m.node(3)
        z = [m.node(1), m.node(2)]
        w_sb = [m.small(i) for i in range(3)]
        b_sb = [m.small(3 + i) for i in range(3)]
        ones = m.work2[:, 2 * DC:2 * DC + P]
        rt = [m.work2[:, i * DC:(i + 1) * DC] for i in range(2)]
        degrow = m.big[:, behind:behind + NPAD]
        mean, var, deg, dinv = (m.colsN[:, i, :] for i in range(4))
        s_in = sem("l1_in"); s_ones = sem("l1_ones"); s_dve = sem("l1_dve")
        s_ld = [sem(f"l1_ld{i}") for i in range(3)]; prod_done = sem("l1_prod"); copied = sem("l1_copied")
        back_done = sem("l1_back"); mixed = sem("l1_mixed"); s_var = sem("l1_var"); s_std = sem("l1_std"); s_z = sem("l1_z")
        block = ctx.enter_context(nc.Block())

        @block.sync
        def _(sp):
            for i in range(3):
                sp.dma_start(w_sb[i][0:D, :], wts[i]).then_inc(s_in, 16)
                sp.dma_start(b_sb[i], biases[i].partition_broadcast(P)).then_inc(s_in, 16)
            for l in range(4):
                for c in range(NDC):
                    before = c - 2 if 2 <= c < NDC - 1 else (c - 3 if c < 2 else c - NDC)
                    if l * NDC + before >= 0:
                        sp.wait_ge(prod_done, l * NDC + before + 1)
                    n = width(c) // BW
                    sp.dma_start(st[buffer(c)][:, 0:n, :], aw[c * NB:c * NB + n, :, :].rearrange("j p c -> p j c")).then_inc(s_ld[buffer(c)], 16)

        @block.tensor
        def _(pe):
            def product(l, c, lhsT, rows):
                u = l * NDC + c
                n = width(c)
                pe.wait_ge(s_ld[buffer(c)], 16 * loads(l, c))
                out = m.PB[u % 3][0:rows, 0:n]
                for a in range(NCH):
                    if l > 1 and c == 0 and a % GROUP == 0:
                        pe.wait_ge(mixed, (l - 2) * NDC + a // GROUP + 1)
                    ins = pe.matmul(out, lhsT(a), st[buffer(c)][:, 0:n // BW, a * BW:(a + 1) * BW], start=(a == 0),
                                    stop=(a == NCH - 1 and l == 0))
                if l:
                    for i in range(-(-n // P)):
                        k = min(P, n - i * P)
                        ins = pe.matmul(m.PB[u % 3][0:rows, i * P:i * P + k], lhsT(c * GROUP + i), m.ident[:, 0:k], start=False,
                                        stop=(i == -(-n // P) - 1))
                ins.then_inc(prod_done, 1)

            def back(l, c):
                u = (l - 1) * NDC + c
                pe.wait_ge(copied, u + NDC + 1)
                if u >= 2:
                    pe.wait_ge(mixed, u - 1)
                n = width(c)
                for i in range(-(-n // P)):
                    k = min(P, n - i * P)
                    ins = pe.matmul(m.PB[6 + u % 2][0:k, i * D:(i + 1) * D], rt[u % 2][0:D, i * P:i * P + k],
                                    w_sb[l - 1][0:D, :], start=True, stop=True)
                ins.then_inc(back_done, 1)

            pe.wait_ge(s_ones, 1)
            for c in range(NDC):
                if c >= 3:
                    pe.wait_ge(copied, c - 2)
                product(0, c, lambda a: ones, P)
            pe.wait_ge(s_in, 96)
            pe.wait_ge(s_z, 1)
            for l in range(1, 4):
                for c in range(NDC):
                    u = l * NDC + c
                    pe.wait_ge(copied, u - 2)
                    product(l, c, lambda a: z[(l - 1) % 2][:, a, :], D)
                    if c:
                        back(l, c - 1)
                back(l, NDC - 1)

        @block.scalar
        def _(act):
            for c in range(NDC):
                act.wait_ge(prod_done, c + 1)
                nc.scalar.copy(degrow[:, c * DC:c * DC + width(c)], m.PB[c % 3][:, 0:width(c)]).then_inc(copied, 1)
            for n in range(2):
                act.wait_ge(s_var, n + 1)
                v = (var, dinv)[n]
                nc.scalar.sqrt(v, v).then_inc(s_std, 1)
            for u in range(3 * NDC):
                act.wait_ge(prod_done, NDC + u + 1)
                if u >= 2:
                    act.wait_ge(back_done, u - 1)
                n = width(u % NDC)
                nc.scalar.copy(rt[u % 2][0:D, 0:n], m.PB[(NDC + u) % 3][0:D, 0:n]).then_inc(copied, 1)

        @block.vector
        def _(dve):
            chain = Chain(dve, s_dve)
            dve.memset(ones, 1.0).then_inc(s_ones, 1)
            dve_norm(dve, chain, z[0], xs, tmp, (mean, var), s_var, s_std, 1)
            chain(dve.tensor_scalar(z[0], z[0], 0.0, None, ALU.max))
            chain(dve.memset(degrow[:, NDST:], 0.0))
            chain(dve.memset(z[1][:, NCH - 1, :], 0.0))
            dve.wait_ge(copied, NDC)
            dr = degrow.rearrange("p (a n) -> p a n", a=NCH)
            chain(dve.tensor_tensor(dr, dr, along(m.ident[:, :], NCH), ALU.mult))
            chain(dve.tensor_reduce(deg, dr, op=ALU.add, axis=X))
            chain(dve.tensor_scalar(deg, deg, 1.0, None, ALU.add))
            dve.tensor_scalar(dinv, deg, 1e-30, None, ALU.max).then_inc(s_var, 1)
            dve.wait_ge(s_std, 2)
            chain(dve.reciprocal(dinv, dinv))
            chain(dve.scalar_tensor_tensor(dinv, deg, 0.0, dinv, ALU.is_gt, ALU.mult))
            dve.tensor_tensor(z[0], z[0], spread(dinv, D), ALU.mult).then_inc(s_z, 1)
            dve.wait_ge(s_in, 96)
            for u in range(3 * NDC):
                l, c = divmod(u, NDC)
                dve.wait_ge(back_done, u + 1)
                rows = P if c < NDC - 1 else width(c)
                g = GROUP if c < NDC - 1 else 1
                a = slice(c * GROUP, c * GROUP + g)
                ps = m.PB[6 + u % 2][0:rows, 0:g * D].rearrange("p (a d) -> p a d", a=g)
                di = dinv[0:rows, a].unsqueeze(2).to_broadcast([rows, g, D])
                bb = b_sb[l][0:rows, :].unsqueeze(1).to_broadcast([rows, g, D])
                tc = tmp[0:rows, a, :]
                chain(dve.tensor_tensor(tc, ps, di, ALU.mult))
                chain(dve.tensor_tensor(tc, tc, bb, ALU.add))
                if l < 2:
                    chain(dve.tensor_scalar(tc, tc, 0.0, None, ALU.max))
                    dve.tensor_tensor(z[1 - l][0:rows, a, :], tc, di, ALU.mult).then_inc(mixed, 1)
                else:
                    dve.tensor_tensor(xs[0:rows, a, :], xs[0:rows, a, :], tc, ALU.add).then_inc(mixed, 1)

HEADS = 2
HC = HEADS * D
DE = 32
FW = DE + 1
VW = FW + D
HALFROW = FW + 2 * HC
AHEAD = (0, FW + D + HC)
FEAT = (0, D)
SUM = (DE, D + DE)
VAL = (FW, 0)
MW = D + 1
BIG = 1e30
LOW = 1e20


class Visit:

    def __init__(self, g, c):
        self.g, self.c = g, c

    def __add__(self, n):
        return Visit(self.g, self.c + n)

    @property
    def fixed(self):
        return isinstance(self.g, int)

    @property
    def n(self):
        return self.g * R + self.c

    def slot(self, k):
        return self.c % k

    def landed(self, ring=R, each=1):
        return (self.g * (R // ring) + (self.c // ring + 1)) * (16 * each)

    def exists(self):
        return not self.fixed or 0 <= self.n < V2


def walk(eng, step, before, after):
    head = 2 * R - 2
    rounds = (V2 - head) // R - 1
    for i in range(-before, head):
        step(Visit(0, i))
    with eng.Fori(0, rounds) as g:
        for u in range(R):
            step(Visit(g, head + u))
    for i in range(head + rounds * R, V2 + after):
        step(Visit(0, i))


def wait(eng, sem, n):
    if not isinstance(n, int) or n > 0:
        eng.wait_ge(sem, n)


class Take:
    def __init__(self, region):
        self.region, self.at = region, 0

    def __call__(self, n, rows=P):
        self.at += n
        return self.region[0:rows, self.at - n:self.at]


def stage_attend_tables(nc, m, keep, we, wq, wk, wv, bq, bk, bv, g1, b1, kv_t, q_t):
    with ExitStack() as ctx:
        sem = lambda n: ctx.enter_context(nc.semaphore(n))
        take = Take(m.big)
        kv = take(NCH * 2 * HC).rearrange("p (a c) -> p a c", a=NCH)
        qT = take(NCH * HEADS * P).rearrange("p (a h n) -> p a h n", a=NCH, h=HEADS)
        w_kv, w_q = take(2 * HC, D), take(HC, D)
        b_kv, bq_c = take(2 * HC), take(1)
        g_sb, b_sb = take(D), take(D)
        hT = [take(P, D) for _ in range(2)]
        qf = [take(P) for _ in range(2)]
        w_e = take(HC, DE)
        w_x = keep["w_x"]
        xs, h, hn, tmp = (m.node(i) for i in range(4))
        mean, var = m.colsN[:, 0, :], m.colsN[:, 1, :]
        s_in = sem("at_in"); s_dve = sem("at_dve"); s_var = sem("at_var"); s_std = sem("at_std"); s_rows = sem("at_rows")
        turned = sem("at_turned"); copied = sem("at_copied"); done = sem("at_done"); taken = sem("at_taken"); s_we = sem("at_we"); s_wx = sem("at_wx"); q_ready = sem("at_q")
        x_done = sem("at_x"); x_taken = sem("at_xs"); s_out = sem("at_out")
        block = ctx.enter_context(nc.Block())

        @block.sync
        def _(sp):
            sp.dma_start(w_kv[:, 0:D], wv[:, 0:D]).then_inc(s_in, 16)
            sp.dma_start(w_kv[:, D:D + HC], wk).then_inc(s_in, 16)
            sp.dma_start(w_kv[:, D + HC:], wv[:, D:]).then_inc(s_in, 16)
            sp.dma_start(w_e, we).then_inc(s_in, 16)
            sp.dma_start(w_q, wq).then_inc(s_in, 16)
            sp.dma_start(b_kv[:, 0:D], bv[0:D].partition_broadcast(P)).then_inc(s_in, 16)
            sp.dma_start(b_kv[:, D:D + HC], bk.partition_broadcast(P)).then_inc(s_in, 16)
            sp.dma_start(b_kv[:, D + HC:], bv[D:].partition_broadcast(P)).then_inc(s_in, 16)
            sp.dma_start(bq_c, bq.unsqueeze(1)).then_inc(s_in, 16)
            sp.dma_start(g_sb, g1.partition_broadcast(P)).then_inc(s_in, 16)
            sp.dma_start(b_sb, b1.partition_broadcast(P)).then_inc(s_in, 16)
            for i in range(5):
                sp.wait_ge(taken, 5 * (i + 1))
                sp.wait_ge(x_taken, 5 * (i + 1))
                a = slice(5 * i, 5 * i + 5)
                sp.dma_start(kv_t[a, :, :].rearrange("a p c -> p a c"), kv[:, a, :]).then_inc(s_out, 16)
                sp.dma_start(q_t[a, :, :].rearrange("a p n -> p a n"), qT[:, a, :, :].rearrange("p a h n -> p a (h n)")).then_inc(s_out, 16)
            sp.wait_ge(s_out, 160)

        @block.tensor
        def _(pe):
            pe.wait_ge(s_in, 176)
            pe.transpose(m.PB[6][:, 0:DE], w_e, m.ident[0:DE, 0:DE]).then_inc(s_we, 1)
            pe.wait_ge(s_wx, 2)
            pe.wait_ge(s_rows, 1)
            for a in range(NCH + 2):
                if a < NCH:
                    wait(pe, copied, a - 1)
                    pe.transpose(m.PB[a % 2][0:D, 0:P], hn[:, a, :], m.ident[:, :]).then_inc(turned, 1)
                if a >= 2:
                    b = a - 2
                    pe.wait_ge(q_ready, b + 1)
                    wait(pe, x_taken, b - 1)
                    pe.matmul(m.PB[6 + b % 2][:, 0:P], w_x, qf[b % 2], start=True, stop=True).then_inc(x_done, 1)
                if 1 <= a <= NCH:
                    b = a - 1
                    pe.wait_ge(copied, b + 1)
                    wait(pe, taken, b - 1)
                    pe.matmul(m.PB[2 + b % 2][:, 0:2 * HC], hT[b % 2], w_kv, start=True, stop=True)
                    pe.matmul(m.PB[4 + b % 2][:, 0:P], w_q, hT[b % 2], start=True, stop=True).then_inc(done, 1)

        @block.scalar
        def _(act):
            for n in range(2):
                act.wait_ge(s_var, n + 1)
                nc.scalar.sqrt(var, var).then_inc(s_std, 1)
            for a in range(NCH):
                act.wait_ge(turned, a + 1)
                wait(act, done, a - 1)
                nc.scalar.copy(hT[a % 2], m.PB[a % 2][0:D, 0:P]).then_inc(copied, 1)
                for b in range(max(0, a - 2), a - 1 if a < NCH - 1 else NCH):
                    act.wait_ge(x_done, b + 1)
                    nc.scalar.copy(qT[D:P, b, 0, :], m.PB[6 + b % 2][D:P, 0:P])
                    nc.scalar.copy(qT[0:D, b, 1, :], m.PB[6 + b % 2][0:D, 0:P]).then_inc(x_taken, 1)

        @block.vector
        def _(dve):
            chain = Chain(dve, s_dve)
            dve.memset(w_x, 0.0).then_inc(s_wx, 1)
            dve.wait_ge(s_wx, 1)
            dve.wait_ge(s_we, 1)
            dve.tensor_copy(w_x[0:D, D:D + DE], m.PB[6][0:D, 0:DE])
            dve.tensor_copy(w_x[D:P, 0:DE], m.PB[6][D:P, 0:DE]).then_inc(s_wx, 1)
            dve_norm(dve, chain, h, xs, tmp, (mean, var), s_var, s_std, 1)
            chain(dve.tensor_scalar(h, h, 0.0, None, ALU.max))
            dve_norm(dve, chain, hn, h, tmp, (mean, var), s_var, s_std, 2)
            dve.wait_ge(s_in, 176)
            chain(dve.tensor_tensor(hn, hn, along(g_sb, NCH), ALU.mult))
            dve.tensor_tensor(hn, hn, along(b_sb, NCH), ALU.add).then_inc(s_rows, 1)
            for a in range(NCH):
                dve.wait_ge(done, a + 1)
                wait(dve, x_done, a - 1)
                dve.tensor_scalar(qf[a % 2], m.PB[4 + a % 2][:, 0:P], bq_c, float(D) ** -0.5, ALU.add, ALU.mult).then_inc(q_ready, 1)
                dve.tensor_tensor(kv[:, a, :], m.PB[2 + a % 2][:, 0:2 * HC], b_kv, ALU.add)
                for hd in range(HEADS):
                    rows = slice(hd * D, (hd + 1) * D)
                    ins = dve.tensor_scalar(qT[rows, a, hd, :], m.PB[4 + a % 2][rows, 0:P], bq_c[rows, :], float(D) ** -0.5, ALU.add, ALU.mult)
                ins.then_inc(taken, 1)


def stage_attend(nc, m, keep, ea, eaT, kv_t, q_t):
    with ExitStack() as ctx:
        sem = lambda n: ctx.enter_context(nc.semaphore(n))
        take = Take(m.big)
        halves = lambda a: a.rearrange("p (s c) -> p s c", s=2)
        acc = keep["acc"]
        take.at = keep["end"]
        nmax = take(JPAD * HEADS).rearrange("p (a h) -> p a h", a=JPAD)
        pen = take(P).bitcast(BF16)
        rows = [halves(take(2 * 2 * HALFROW)) for _ in range(R)]
        KF = [take(HEADS * TE).rearrange("p (h e) -> p h e", h=HEADS) for _ in range(R)]
        qT = [take(HEADS * P) for _ in range(R)]
        idx = take(2 * R).bitcast(I32)
        oh = [halves(take(P).bitcast(BF16)) for _ in range(4)]
        Pm = [take(2 * TE) for _ in range(4)]
        PT = [take(2 * TE) for _ in range(2)]
        nm = [take(HEADS) for _ in range(4)]
        rm, df = [take(HEADS) for _ in range(4)], [take(HEADS) for _ in range(4)]
        corr = [take(HEADS) for _ in range(4)]
        gateP, gz = take(1), take(1)
        assert take.at <= NCH * NDST // 2
        psK = m.PB[0][:, 0:TE]
        psS = [m.PB[1 + i][:, :] for i in range(4)]
        psT = m.PB[5][:, :]
        psA = [m.PB[6][:, 0:2 * VW], m.PB[7][:, 0:2 * VW]]

        init = sem("av_init")
        idx_ready = sem("av_idx")
        landed_g = m.kv_landed
        landed_e = [sem(f"av_e{i}") for i in range(R)]
        gated = sem("av_gated")
        k_turned = sem("av_kT")
        k_copied = sem("av_kTs")
        oh_ready = sem("av_oh")
        scored = sem("av_S")
        max_ready = sem("av_max")
        exp_ready = sem("av_P")
        p_turned = sem("av_PT")
        p_copied = sem("av_PTs")
        summed = sem("av_A")
        s_small = sem("av_small")
        acc_ready = sem("av_acc")
        block = ctx.enter_context(nc.Block())

        @block.sync
        def _(sp):
            sp.wait_ge(init, 1)

            tiles = [None, None]

            def step(v):
                k = v.slot(R)
                if v.c % 2 == 0:
                    tiles[:] = m.tiles_of(sp, v.n)
                t = tiles[v.c % 2]
                j = (v.n - t) & (JPAD - 1)
                wait(sp, scored, v.n - R + 1)
                sp.dma_start(KF[k][D:D + DE, 0, :], eaT[:, bass.ds(t * TE, TE)]).then_inc(landed_e[k], 16)
                sp.dma_start(qT[k], q_t[bass.ds(j, 1), :, :].rearrange("j p n -> p (j n)")).then_inc(landed_e[k], 16)
                wait(sp, summed, v.n - R + 1)
                tile = ea[bass.ds(t, 1), :, :].rearrange("t p n -> p (t n)").rearrange("p (s c) -> p s c", s=2)
                to = rows[k].rearrange("p s (x c) -> p s x c", x=2)[:, :, :, 0:DE]
                sp.dma_start(to, tile.unsqueeze(2).to_broadcast([P, 2, 2, DE])).then_inc(landed_e[k], 16)

            walk(sp, step, 0, 0)

        @block.gpsimd
        def _(po):
            po.wait_ge(init, 1)

            def step(v):
                k = v.slot(R)
                wait(po, idx_ready, v.n + 1)
                wait(po, summed, v.n - R + 1)
                wait(po, gated, v.n)
                po.tensor_tensor(gateP, gz, gz, ALU.add).then_inc(gated, 1)
                for s in range(2):
                    po.indirect_dma_start(rows[k][:, s, FW:FW + 2 * HC], None, kv_t.rearrange("a p c -> (a p) c"), bass.IndirectOffsetOnAxis(
                        ap=idx[:, 2 * k + s:2 * k + s + 1], axis=0)).then_inc(landed_g[k], 16)

            walk(po, step, 0, 0)

        @block.tensor
        def _(pe):
            pe.wait_ge(init, 1)

            def step(i):
                v = i + 1
                if v.exists():
                    pe.wait_ge(landed_g[v.slot(R)], v.landed(each=2))
                    wait(pe, k_copied, v.n)
                    for s in range(2):
                        ins = pe.transpose(psK[:, s * P:(s + 1) * P], rows[v.slot(R)][:, s, FW + D:FW + D + HC], m.ident[:, :])
                    ins.then_inc(k_turned, 1)
                v = i
                if v.exists():
                    s = psS[v.slot(4)]
                    pe.wait_ge(oh_ready, v.n + 1)
                    wait(pe, exp_ready, v.n - 3)
                    for e in range(2):
                        pe.matmul(s.rearrange("p (h s e) -> p h s e", h=HEADS, s=2)[:, :, e, :], oh[v.slot(4)][:, e, :],
                                  pen, start=(e == 0), stop=False)
                    pe.wait_ge(k_copied, v.n + 1)
                    pe.wait_ge(landed_e[v.slot(R)], v.landed(each=3))
                    for h in range(HEADS):
                        ins = pe.matmul(s[:, h * TE:(h + 1) * TE], qT[v.slot(R)][:, h * P:(h + 1) * P], KF[v.slot(R)][:, h, :], start=False, stop=(h == 1))
                    ins.then_inc(scored, 1)
                v = i + -2
                if v.exists():
                    pe.wait_ge(exp_ready, v.n + 1)
                    wait(pe, p_copied, v.n)
                    for x in range(2 * HEADS):
                        part = slice(x * P, (x + 1) * P)
                        ins = pe.transpose(psT[:, part], Pm[v.slot(4)][:, part], m.ident[:, :])
                    ins.then_inc(p_turned, 1)
                v = i + -3
                if v.exists():
                    pe.wait_ge(p_copied, v.n + 1)
                    wait(pe, acc_ready, v.n - 1)
                    for h in range(HEADS):
                        for s in range(2):
                            x = 2 * h + s
                            ins = pe.matmul(psA[v.slot(2)][:, h * VW:(h + 1) * VW], PT[v.slot(2)][:, x * P:(x + 1) * P],
                                            rows[v.slot(R)][:, s, AHEAD[h]:AHEAD[h] + VW], start=(s == 0), stop=(s == 1))
                    ins.then_inc(summed, 1)

            walk(pe, step, 1, 3)

        @block.scalar
        def _(act):
            def step(i):
                v = i + 1
                if v.exists():
                    act.wait_ge(k_turned, v.n + 1)
                    wait(act, scored, v.n - R + 1)
                    nc.scalar.copy(KF[v.slot(R)][0:D, 0, :], psK[0:D, :])
                    nc.scalar.copy(KF[v.slot(R)][D:P, 1, :], psK[D:P, :])
                    act.wait_ge(landed_e[v.slot(R)], v.landed(each=3))
                    nc.scalar.copy(KF[v.slot(R)][0:DE, 1, :], KF[v.slot(R)][D:D + DE, 0, :]).then_inc(k_copied, 1)
                v = i + -2
                if v.exists():
                    act.wait_ge(p_turned, v.n + 1)
                    wait(act, summed, v.n - 1)
                    nc.scalar.copy(PT[v.slot(2)], psT).then_inc(p_copied, 1)
                v = i
                if v.exists():
                    act.wait_ge(max_ready, v.n + 1)
                    wait(act, p_turned, v.n - 3)
                    nc.scalar.activation(corr[v.slot(4)], df[v.slot(4)], ACT.Exp)
                    for h in range(HEADS):
                        ins = nc.scalar.activation(Pm[v.slot(4)][:, h * TE:(h + 1) * TE], psS[v.slot(4)][:, h * TE:(h + 1) * TE], ACT.Exp,
                                                   bias=nm[v.slot(4)][:, h:h + 1])
                    ins.then_inc(exp_ready, 1)

            walk(act, step, 2, 2)

        @block.vector
        def _(dve):
            dve.memset(nmax, LOW)
            dve.memset(gz, 0.0)
            dve.memset(gateP, 0.0)
            for k in range(R):
                for h in range(HEADS):
                    at = AHEAD[h] + SUM[h]
                    dve.memset(rows[k][:, :, at:at + 1], 1.0)
                dve.memset(KF[k], 0.0)
            for h in range(HEADS):
                dve.tensor_scalar(pen[:, h * P:(h + 1) * P], m.ident[:, :], BIG, None, ALU.mult)
            dve.memset(acc, 0.0).then_inc(init, 1)
            dve.wait_ge(init, 1)

            def index(v):
                if not v.fixed or v.n >= R:
                    dve.wait_ge(landed_g[v.slot(R)], (v + -R).landed(each=2))
                dve.tensor_scalar(idx[:, 2 * v.slot(R):2 * v.slot(R) + 2], m.src2[:, :, bass.ds(v.n, 1)].rearrange("p s v -> p (s v)"),
                                  0, None, ALU.add).then_inc(idx_ready, 1)

            blocks = [None] * 4

            def onehot(v, s):
                if s == 0:
                    wait(dve, scored, v.n - 3)
                ins = dve.tensor_scalar(oh[v.slot(4)][:, s, :], m.iotaH[:, 0:P], m.rel2[:, s, bass.ds(v.n, 1)], -1.0, ALU.is_equal, ALU.add)
                if s == 1:
                    ins.then_inc(oh_ready, 1)

            def step(i):
                v = i + 6
                if v.exists():
                    index(v)
                m0 = i
                small = 3 * m0.n
                if m0.exists():
                    dve.wait_ge(scored, m0.n + 1)
                    s3 = m0.slot(4)
                    dve.tensor_reduce(rm[s3], psS[m0.slot(4)].rearrange("p (h e) -> p h e", h=HEADS), op=ALU.max, axis=X, negate=True).then_inc(s_small, 1)
                if i.c % 2 == 0 and (not i.fixed or i.c >= 0):
                    blocks[:] = m.blocks_of(dve, m0.n)
                ja, j = blocks[i.c % 2], blocks[i.c % 2 + 2]
                v = i + 2
                if v.exists():
                    onehot(v, 0)
                if m0.exists():
                    nmj = nmax[:, bass.ds(j, 1), :].rearrange("p j h -> p (j h)")
                    dve.wait_ge(s_small, small + 1)
                    dve.tensor_tensor(nm[s3], nmj, rm[s3], ALU.min).then_inc(s_small, 1)
                if v.exists():
                    onehot(v, 1)
                if m0.exists():
                    dve.wait_ge(s_small, small + 2)
                    dve.tensor_tensor(df[s3], nm[s3], nmj, ALU.subtract).then_inc(max_ready, 1)
                v = i + -3
                if v.exists():
                    dve.wait_ge(summed, v.n + 1)
                    wait(dve, acc_ready, v.n)
                    for h in range(HEADS):
                        a = acc[:, bass.ds(ja, 1), h, :].rearrange("p j c -> p (j c)")
                        ins = dve.scalar_tensor_tensor(a, a, corr[v.slot(4)][:, h:h + 1], psA[v.slot(2)][:, h * VW:(h + 1) * VW], ALU.mult, ALU.add)
                    ins.then_inc(acc_ready, 1)
                if m0.exists():
                    dve.wait_ge(max_ready, m0.n + 1)
                    dve.tensor_scalar(nmj, nm[s3], 0.0, None, ALU.add).then_inc(s_small, 1)

            walk(dve, step, 6, 3)


def stage_nodes(nc, m, keep, wp, bp, g2, b2, w1, b1, w2, bb2, w3, b3, g_t):
    with ExitStack() as ctx:
        sem = lambda n: ctx.enter_context(nc.semaphore(n))
        take = Take(m.big)
        take.at = keep["end"]
        acc = keep["acc"][:, 0:NCH]
        agg = take(NCH * HC).rearrange("p (a c) -> p a c", a=NCH)
        feat = take(NCH * P).rearrange("p (a c) -> p a c", a=NCH)
        w_fp = take(D)
        gt = take(NCH * D).rearrange("p (a d) -> p a d", a=NCH)
        rden = take(NCH * HEADS).rearrange("p (a h) -> p a h", a=NCH)
        w_p, w_1, w_2, w_3 = take(D), take(D, D), take(D, D), take(D, D)
        rows = [take(D) for _ in range(6)]
        bp_s, g2_s, b2_s, b1_s, bb2_s, b3_s = rows
        bufs = [take(DC) for _ in range(4)]
        half = [b[0:D, :] for b in bufs[0:2]]
        xs, h, t, tmp = (m.node(i) for i in range(4))
        mean, var = m.colsN[:, 0, :], m.colsN[:, 1, :]
        L = [Linear(nc, ctx, "n0", m, [bufs[0:2], bufs[2:4]], HC, D, more=(4, 5))]
        L += [Linear(nc, ctx, f"n{i}", m, [half], D, D) for i in range(1, 4)]
        s_in = sem("nd_in"); s_dve = sem("nd_dve"); s_var = sem("nd_var"); s_std = sem("nd_std")
        s_rows = [sem(f"nd_rows{i}") for i in range(4)]; s_out = sem("nd_out")
        s_g = sem("nd_g"); s_fp = sem("nd_fp"); s_fps = sem("nd_fps")
        block = ctx.enter_context(nc.Block())

        @block.sync
        def _(sp):
            for a, b in ((w_p, wp), (w_1, w1), (w_2, w2), (w_3, w3)):
                sp.dma_start(a, b).then_inc(s_in, 16)
            for a, b in zip(rows, (bp, g2, b2, b1, bb2, b3)):
                sp.dma_start(a, b.partition_broadcast(P)).then_inc(s_in, 16)
            sp.wait_ge(L[3].taken, NG)
            sp.dma_start(g_t.rearrange("a p d -> p a d"), gt).then_inc(s_out, 16)
            sp.wait_ge(s_out, 16)

        @block.tensor
        def _(pe):
            pe.wait_ge(s_in, 160)
            pe.matmul(m.PB[6][:, 0:D], keep["w_x"], w_p, start=True, stop=True).then_inc(s_fp, 1)
            pe.wait_ge(s_fps, 1)
            pe.wait_ge(s_rows[0], 1)
            L[0].tensor(pe, (lambda a: agg[:, a, :], w_p), (lambda a: feat[:, a, :], w_fp))
            for i, (src, w) in enumerate(((t, w_1), (t, w_2), (h, w_3))):
                pe.wait_ge(s_rows[i + 1], 1)
                L[i + 1].tensor(pe, (lambda a, src=src: src[:, a, :], w))

        @block.scalar
        def _(act):
            act.wait_ge(s_fp, 1)
            nc.scalar.copy(w_fp, m.PB[6][:, 0:D]).then_inc(s_fps, 1)
            L[0].scalar(act, nc)
            act.wait_ge(s_var, 1)
            nc.scalar.sqrt(var, var).then_inc(s_std, 1)
            L[1].scalar(act, nc)
            act.wait_ge(s_g, 1)
            nc.scalar.activation(t, tmp, ACT.Gelu).then_inc(s_rows[2], 1)
            L[2].scalar(act, nc)
            act.wait_ge(s_var, 2)
            nc.scalar.sqrt(var, var).then_inc(s_std, 1)
            L[3].scalar(act, nc)

        @block.vector
        def _(dve):
            chain = Chain(dve, s_dve)
            chain(dve.memset(feat, 0.0))
            for hd in range(HEADS):
                chain(dve.tensor_scalar(rden[:, :, hd], acc[:, :, hd, SUM[hd]], 1e-8, None, ALU.add))
            chain(dve.reciprocal(rden, rden))
            for hd in range(HEADS):
                dve.tensor_tensor(feat[:, :, (1 - hd) * D:(1 - hd) * D + DE], acc[:, :, hd, FEAT[hd]:FEAT[hd] + DE],
                                  spread(rden[:, :, hd], DE), ALU.mult)
                ins = dve.tensor_tensor(agg[:, :, hd * D:(hd + 1) * D], acc[:, :, hd, VAL[hd]:VAL[hd] + D], spread(rden[:, :, hd], D), ALU.mult)
            ins.then_inc(s_rows[0], 1)
            dve.wait_ge(s_in, 160)
            chain(dve.tensor_tensor(h, h, along(bp_s, NCH), ALU.add))
            for g in range(NG):
                dve.tensor_tensor(of_group(h, g), L[0].result(dve, g), of_group(h, g), ALU.add).then_inc(L[0].taken, 1)
            dve.wait_ge(L[0].taken, NG)
            dve_norm(dve, chain, t, h, tmp, (mean, var), s_var, s_std, 1)
            chain(dve.tensor_tensor(t, t, along(g2_s, NCH), ALU.mult))
            dve.tensor_tensor(t, t, along(b2_s, NCH), ALU.add).then_inc(s_rows[1], 1)
            for g in range(NG):
                dve.tensor_tensor(of_group(tmp, g), L[1].result(dve, g), along(b1_s, len(chunks(g))), ALU.add).then_inc(L[1].taken, 1)
            dve.wait_ge(L[1].taken, NG)
            chain(dve.tensor_tensor(xs, xs, h, ALU.add))
            dve.tensor_tensor(xs, xs, along(bb2_s, NCH), ALU.add).then_inc(s_g, 1)
            dve.wait_ge(s_g, 1)
            for g in range(NG):
                dve.tensor_tensor(of_group(xs, g), L[2].result(dve, g), of_group(xs, g), ALU.add).then_inc(L[2].taken, 1)
            dve.wait_ge(L[2].taken, NG)
            dve_norm(dve, chain, h, xs, tmp, (mean, var), s_var, s_std, 2)
            dve.tensor_scalar(h, h, 0.0, None, ALU.max).then_inc(s_rows[3], 1)
            for g in range(NG):
                dve.tensor_tensor(of_group(gt, g), L[3].result(dve, g), along(b3_s, len(chunks(g))), ALU.add).then_inc(L[3].taken, 1)


def stage_messages(nc, m, keep, w1, efT, g_t):
    with ExitStack() as ctx:
        sem = lambda n: ctx.enter_context(nc.semaphore(n))
        take = Take(m.big)
        halves = lambda a: a.rearrange("p (s c) -> p s c", s=2)
        acc = keep["acc3"]
        take.at = keep["end"]
        w_e = take(D, D)
        G = [halves(take(2 * D)) for _ in range(RM)]
        ef = [take(TE, D) for _ in range(RM)]
        M = [halves(take(2 * MW)) for _ in range(4)]
        oh = [halves(take(2 * P)) for _ in range(4)]
        idx = take(2 * RM).bitcast(I32)
        gateP, gz = take(1), take(1)
        psM = [halves(m.PB[0][:, 0:2 * D]), halves(m.PB[1][:, 0:2 * D])]
        psA = [m.PB[2][:, 0:MW], m.PB[3][:, 0:MW]]
        init = sem("ms_init"); s_in = sem("ms_in"); idx_ready = sem("ms_idx")
        landed_g = m.table_landed
        landed_e = [sem(f"ms_e{i}") for i in range(RM)]
        gated = sem("ms_gated")
        m_done = sem("ms_M")
        m_ready = sem("ms_Ms")
        oh_ready = sem("ms_oh")
        summed = sem("ms_A")
        acc_ready = sem("ms_acc")
        block = ctx.enter_context(nc.Block())

        @block.sync
        def _(sp):
            sp.dma_start(w_e, w1).then_inc(s_in, 16)

            tiles = [None, None]

            def step(v):
                if v.c % 2 == 0:
                    tiles[:] = m.tiles_of(sp, v.n)
                t = tiles[v.c % 2]
                wait(sp, m_done, v.n - RM + 1)
                sp.dma_start(ef[v.slot(RM)], efT[:, bass.ds(t * TE, TE)]).then_inc(landed_e[v.slot(RM)], 16)

            walk(sp, step, 0, 0)

        @block.gpsimd
        def _(po):
            po.wait_ge(init, 1)

            def step(v):
                k = v.slot(RM)
                wait(po, idx_ready, v.n + 1)
                wait(po, m_done, v.n - RM + 1)
                wait(po, gated, v.n)
                po.tensor_tensor(gateP, gz, gz, ALU.add).then_inc(gated, 1)
                for s in range(2):
                    po.indirect_dma_start(G[k][:, s, :], None, g_t.rearrange("a p c -> (a p) c"), bass.IndirectOffsetOnAxis(
                        ap=idx[:, 2 * k + s:2 * k + s + 1], axis=0)).then_inc(landed_g[k], 16)

            walk(po, step, 0, 0)

        @block.tensor
        def _(pe):
            pe.wait_ge(init, 1)
            pe.wait_ge(s_in, 16)

            def step(i):
                v = i + 1
                if v.exists():
                    k = v.slot(RM)
                    pe.wait_ge(landed_e[k], v.landed(RM))
                    wait(pe, m_ready, v.n - 1)
                    for s in range(2):
                        pe.matmul(psM[v.slot(2)][:, s, :], ef[k][:, s * P:(s + 1) * P], w_e, start=(s == 0), stop=False)
                    pe.wait_ge(landed_g[k], v.landed(RM, 2))
                    pe.matmul(psM[v.slot(2)], m.ident[:, :], G[k], start=False, stop=True).then_inc(m_done, 1)
                v = i
                if v.exists():
                    pe.wait_ge(m_ready, v.n + 1)
                    pe.wait_ge(oh_ready, v.n + 1)
                    wait(pe, acc_ready, v.n - 1)
                    for s in range(2):
                        ins = pe.matmul(psA[v.slot(2)], oh[v.slot(4)][:, s, :], M[v.slot(4)][:, s, :], start=(s == 0), stop=(s == 1))
                    ins.then_inc(summed, 1)

            walk(pe, step, 1, 0)

        @block.scalar
        def _(act):
            act.wait_ge(init, 1)

            def step(v):
                act.wait_ge(m_done, v.n + 1)
                wait(act, summed, v.n - 3)
                nc.scalar.activation(M[v.slot(4)][:, :, 0:D], psM[v.slot(2)], ACT.Relu).then_inc(m_ready, 1)

            walk(act, step, 0, 0)

        @block.vector
        def _(dve):
            dve.memset(gz, 0.0)
            dve.memset(gateP, 0.0)
            for k in range(4):
                dve.memset(M[k][:, :, D:], 1.0)
            dve.memset(acc, 0.0).then_inc(init, 1)
            dve.wait_ge(init, 1)

            blocks = [None] * 4

            def step(i):
                if i.c % 2 == 0 and (not i.fixed or i.c >= 0):
                    blocks[:] = m.blocks_of(dve, i.n)
                v = i + 3
                if v.exists():
                    k = v.slot(RM)
                    if not v.fixed or v.n >= RM:
                        dve.wait_ge(landed_g[k], (v + -RM).landed(RM, 2))
                    dve.tensor_scalar(idx[:, 2 * k:2 * k + 2], m.src2[:, :, bass.ds(v.n, 1)].rearrange("p s v -> p (s v)"), 0, None,
                                      ALU.add).then_inc(idx_ready, 1)
                v = i + -3
                if v.exists():
                    j = blocks[i.c % 2]
                    dve.wait_ge(summed, v.n + 1)
                    wait(dve, acc_ready, v.n)
                    a = acc[:, bass.ds(j, 1), :].rearrange("p j c -> p (j c)")
                    dve.tensor_tensor(a, a, psA[v.slot(2)], ALU.add).then_inc(acc_ready, 1)
                v = i + 1
                if v.exists():
                    wait(dve, summed, v.n - 3)
                    for s in range(2):
                        ins = dve.tensor_scalar(oh[v.slot(4)][:, s, :], m.iotaH[:, 0:P], m.rel2[:, s, bass.ds(v.n, 1)], None, ALU.is_equal)
                    ins.then_inc(oh_ready, 1)

            walk(dve, step, 3, 3)


def stage_output(nc, m, keep, w2, b2, out):
    with ExitStack() as ctx:
        sem = lambda n: ctx.enter_context(nc.semaphore(n))
        take = Take(m.big)
        take.at = keep["end"]
        acc = keep["acc3"][:, 0:NCH]
        both = take(NCH * HC).rearrange("p (a c) -> p a c", a=NCH)
        rcnt, w_s, b_s = take(NCH), take(D), take(D)
        bufs = [take(DC) for _ in range(2)]
        xs, h, t, _ = (m.node(i) for i in range(4))
        L = Linear(nc, ctx, "o", m, [bufs], HC, D)
        s_in = sem("o_in"); s_dve = sem("o_dve"); s_rows = sem("o_rows"); s_res = sem("o_res"); s_out = sem("o_out")
        s_t = sem("o_t")
        block = ctx.enter_context(nc.Block())

        @block.sync
        def _(sp):
            sp.dma_start(w_s, w2).then_inc(s_in, 16)
            sp.dma_start(b_s, b2.partition_broadcast(P)).then_inc(s_in, 16)
            full = NODES // P
            sp.wait_ge(s_res, NG)
            sp.dma_start(out[0:full * P, :].rearrange("(a p) d -> p a d", p=P), xs[:, 0:full, :]).then_inc(s_out, 16)
            sp.dma_start(out[full * P:NODES, :], xs[0:NODES - full * P, full, :]).then_inc(s_out, 16)
            sp.wait_ge(s_out, 32)

        @block.tensor
        def _(pe):
            pe.wait_ge(s_in, 32)
            pe.wait_ge(s_rows, 1)
            L.tensor(pe, (lambda a: both[:, a, :], w_s))

        @block.scalar
        def _(act):
            L.scalar(act, nc)

        @block.vector
        def _(dve):
            chain = Chain(dve, s_dve)
            chain(dve.tensor_scalar(rcnt, acc[:, :, D], 1.0, None, ALU.max))
            chain(dve.reciprocal(rcnt, rcnt))
            dve.tensor_copy(both[:, :, D:], h)
            dve.tensor_tensor(both[:, :, 0:D], acc[:, :, 0:D], spread(rcnt, D), ALU.mult).then_inc(s_rows, 1)
            dve.wait_ge(s_in, 32)
            for g in range(NG):
                dve.tensor_tensor(of_group(t, g), L.result(dve, g), along(b_s, len(chunks(g))), ALU.add).then_inc(L.taken, 1)
                dve.wait_ge(L.taken, g + 1)
                dve.scalar_tensor_tensor(of_group(xs, g), of_group(t, g), 0.0, of_group(xs, g), ALU.max, ALU.add).then_inc(s_res, 1)


def build(nc, last, x, src, dst, w, ea, eaT, efT, L0_gnn_W, L0_gnn_b, L1_gnn_W1, L1_gnn_b1, L1_gnn_W2, L1_gnn_b2, L1_gnn_W3,
          L1_gnn_b3, L2_gnn_Wq, L2_gnn_bq, L2_gnn_Wk, L2_gnn_bk, L2_gnn_Wv, L2_gnn_bv, L2_gnn_We, L2_gnn_Wp, L2_gnn_bp, L2_gnn_ln1_g,
          L2_gnn_ln1_b, L2_gnn_ln2_g, L2_gnn_ln2_b, L2_gnn_W1, L2_gnn_b1, L2_gnn_W2, L2_gnn_b2, L3_gnn_W1, L3_gnn_b1, L3_gnn_W2,
          L3_gnn_b2, out):
    with ExitStack() as ctx:
        m = Mem(nc, ctx)
        scratch = lambda name, shape: nc.dram_tensor(name, shape, F32, kind="Internal").ap()
        aw = scratch("weights_dense", [J1 + RING, P, BCOL])
        kv_t = scratch("kv_table", [NCH, P, 2 * HC])
        q_t = scratch("q_table", [JPAD, P, HEADS * P])
        g_t = scratch("message_table", [NCH, P, D])
        xv = x.rearrange("(a p) d -> p a d", p=P)
        half = lambda i: m.work[:, i * 2 * V1P:(i + 1) * 2 * V1P].rearrange("p (h v) -> p h v", h=2)
        behind = 4 * BCOL + OH * (4 * P + BCOL)
        t1 = dict(col=half(0), row=half(1), w=[half(2), half(3), half(4)],
                  keep=m.work2[:, behind:behind + V1P // 2].bitcast(BF16))
        keep = dict(acc=m.big[:, 0:JPAD * HEADS * VW].rearrange("p (a h c) -> p a h c", a=JPAD, h=HEADS),
                    acc3=m.big[:, 0:JPAD * MW].rearrange("p (a c) -> p a c", a=JPAD), end=JPAD * HEADS * VW, w_x=m.work2[:, 0:P])
        tiles = lambda a: a.rearrange("(t e) -> t e", e=TE)
        stage_tables(nc, m, last, tiles(dst), tiles(src), tiles(w), t1)
        stage_build(nc, m, t1, aw)
        stage_layer0_start(nc, m, xv, L0_gnn_W, L0_gnn_b)
        stage_layer0_hops(nc, m, xv)
        stage_layer1(nc, m, aw, [L1_gnn_W1, L1_gnn_W2, L1_gnn_W3], [L1_gnn_b1, L1_gnn_b2, L1_gnn_b3])
        stage_attend_tables(nc, m, keep, L2_gnn_We, L2_gnn_Wq, L2_gnn_Wk, L2_gnn_Wv, L2_gnn_bq, L2_gnn_bk, L2_gnn_bv, L2_gnn_ln1_g,
                            L2_gnn_ln1_b, kv_t, q_t)
        stage_attend(nc, m, keep, ea, eaT, kv_t, q_t)
        stage_nodes(nc, m, keep, L2_gnn_Wp, L2_gnn_bp, L2_gnn_ln2_g, L2_gnn_ln2_b, L2_gnn_W1, L2_gnn_b1, L2_gnn_W2, L2_gnn_b2,
                    L3_gnn_W1[D:, :], L3_gnn_b1, g_t)
        stage_messages(nc, m, keep, L3_gnn_W1[0:D, :], efT, g_t)
        stage_output(nc, m, keep, L3_gnn_W2, L3_gnn_b2, out)


WEIGHTS = ("L0_gnn_W", "L0_gnn_b", "L1_gnn_W1", "L1_gnn_b1", "L1_gnn_W2", "L1_gnn_b2", "L1_gnn_W3", "L1_gnn_b3", "L2_gnn_Wq",
           "L2_gnn_bq", "L2_gnn_Wk", "L2_gnn_bk", "L2_gnn_Wv", "L2_gnn_bv", "L2_gnn_We", "L2_gnn_Wp", "L2_gnn_bp", "L2_gnn_ln1_g",
           "L2_gnn_ln1_b", "L2_gnn_ln2_g", "L2_gnn_ln2_b", "L2_gnn_W1", "L2_gnn_b1", "L2_gnn_W2", "L2_gnn_b2", "L3_gnn_W1",
           "L3_gnn_b1", "L3_gnn_W2", "L3_gnn_b2")


def kernel(**inputs):
    import concourse.bacc as bacc
    from concourse.bass_utils import run_bass_kernel_spmd

    a = {k: np.asarray(v) for k, v in inputs.items()}
    more = EPAD - EDGES
    dst = np.pad(a["dst"], (0, more), constant_values=NDST - 1)
    src = np.pad(a["src"], (0, more))

    n = -(-T1 // P)
    last = np.ascontiguousarray(np.pad(dst[TE - 1::TE], (0, n * P - T1), constant_values=FAR).reshape(n, P).T)

    arrays = dict(
        last=last, x=np.pad(a["x"], ((0, NPAD - NODES), (0, 0))), src=src, dst=dst,
        w=np.pad(a["edge_weight"], (0, more)),
        ea=np.ascontiguousarray(np.pad(a["edge_attr_32"], ((0, more), (0, 0))).reshape(T1, 2, P, -1).transpose(0, 2, 1, 3)).reshape(T1, P, -1),
        eaT=np.ascontiguousarray(np.pad(a["edge_attr_32"], ((0, more), (0, 0))).T),
        efT=np.ascontiguousarray(np.pad(a["edge_attr_64"], ((0, more), (0, 0))).T),
        **{k: np.ascontiguousarray(a[k]) for k in WEIGHTS})
    nc = bacc.Bacc("TRN2", target_bir_lowering=False, num_devices=1)
    args = {k: nc.dram_tensor(f"in_{k}", v.shape, mybir.dt.from_np(v.dtype), kind="ExternalInput").ap() for k, v in arrays.items()}
    out = nc.dram_tensor("out_x", (NODES, D), F32, kind="ExternalOutput").ap()
    build(nc, out=out, **args)
    r = run_bass_kernel_spmd(nc, [{f"in_{k}": v for k, v in arrays.items()}], core_ids=[0])
    return r.results[0]["out_x"]
```

```python
from contextlib import ExitStack

import numpy as np

import concourse.bass as bass
from concourse import mybir

F32 = mybir.dt.float32
F16 = mybir.dt.float16
BF16 = mybir.dt.bfloat16
I32 = mybir.dt.int32
I16 = mybir.dt.int16
ALU = mybir.AluOpType
ACT = mybir.ActivationFunctionType
X = mybir.AxisListType.X

P = 128
NODES = 3125
EDGES = 103125
D = 64
NCH = 25
NPAD = NCH * P
HOPS = 10
ALPHA = 0.1
EPS = 1e-5

TE = 256
T1 = -(-EDGES // TE)
EPAD = T1 * TE
BW = 16
J1 = -(-NODES // BW)
NDST = J1 * BW
V1 = T1 + J1 - 1
V1P = 640
BCOL = NCH * BW
OH = 3
SPARE = 4
J2 = NCH
JPAD = 32
V2 = T1 + J2 - 1
V2P = 448
DC = 512
NDC = -(-NDST // DC)
BLOCK1, PLACE, TILE2, BLOCK2 = 0, 32, 64, 96
RM = 4
R = 8
FAR = 1 << 20


class Chain:

    def __init__(self, eng, sem):
        self.eng, self.sem, self.n = eng, sem, 0

    def __call__(self, ins):
        self.n += 1
        ins.then_inc(self.sem, 1)
        self.eng.wait_ge(self.sem, self.n)


def spread(v, n):
    return v.unsqueeze(2).to_broadcast([P, v.shape[1], n])


def along(v, k):
    return v.unsqueeze(1).to_broadcast([P, k, v.shape[1]])


class Mem:

    def __init__(self, nc, ctx):
        sb = lambda name, shape, dt: ctx.enter_context(nc.sbuf_tensor(name, shape, dt))
        self.big = sb("big", [P, NCH * NDST // 2], F32)
        self.work = sb("work", [P, 4 * NCH * D], F32)
        self.work2 = sb("work2", [P, NDST + NCH * D], F32)
        self.rel2 = sb("rel2", [P, 2, V2P], F32)
        self.src2 = sb("src2", [P, 2, V2P], I32)
        self.vis = sb("vis", [P, V1P], I16)
        self.ident = sb("ident", [P, P], F32)
        self.iotaH = sb("iotaH", [P, BCOL], F16)
        self.onesB = sb("onesB", [P, P], BF16)
        self.colsN = sb("colsN", [P, 8, NCH], F32)
        self.smalls = self.work2[:, 3 * DC + NCH * D:3 * DC + NCH * D + 8 * D]
        self.PB = [ctx.enter_context(nc.psum_tensor(f"bank{i}", [P, 512], F32)) for i in range(8)]

        sem = lambda n: ctx.enter_context(nc.semaphore(n))
        self.rows_landed = sem("rows_landed")
        self.kv_landed = [sem(f"kv_landed{i}") for i in range(R)]
        self.table_landed = [sem(f"table_landed{i}") for i in range(RM)]

    def blocks1(self):
        return self.vis[BLOCK1:BLOCK1 + 1, :].bitcast(I32)[:, 0:V1 // 2]

    def tiles2(self):
        return self.vis[TILE2:TILE2 + 1, :].bitcast(I32)[:, 0:V2P // 2]

    def tiles_of(self, eng, n):
        x = eng.value_load(self.tiles2()[:, bass.ds(n // 2, 1)], min_val=0, max_val=T1 * T1 - 1)
        return x % T1, x // T1

    def blocks2(self):
        return self.vis[BLOCK2:BLOCK2 + 1, :].bitcast(I32)[:, 0:V2P // 2]

    def blocks_of(self, eng, n):
        x = eng.value_load(self.blocks2()[:, bass.ds(n // 2, 1)], min_val=0, max_val=JPAD ** 4 - 1)
        return [(x >> (5 * i)) & (JPAD - 1) for i in range(4)]

    def counts(self):
        return self.big[:, :].bitcast(F16).rearrange("p (a n) -> p a n", a=NCH)

    def small(self, i):
        return self.smalls[:, i * D:(i + 1) * D]

    def zbuf(self, k):
        base = self.work[:, 0:NCH * D] if k == 0 else self.work2[:, 3 * DC:3 * DC + NCH * D]
        return base.bitcast(F16).rearrange("p (a s d) -> p a s d", a=NCH, s=2)

    def node(self, i):
        return self.work[:, i * NCH * D:(i + 1) * NCH * D].rearrange("p (a d) -> p a d", a=NCH)


def stage_tables(nc, m, last, dst, src, w, t1):
    C = last.shape[1]
    K1, K2 = V1P // P, -(-V2P // P)
    with ExitStack() as ctx:
        sem = lambda n: ctx.enter_context(nc.semaphore(n))
        raw = m.big
        at = [0]

        def take(n):
            at[0] += n
            return raw[:, at[0] - n:at[0]]

        iotaI = take(V1P).bitcast(I32)
        iotaF = take(V1P)
        vmodI = take(V1P).bitcast(I32)
        vmodF = take(V1P)
        schemes = []
        lastI = take(C).bitcast(I32)
        for K, shift in ((K1, 4), (K2, 7)):
            VP = K * P
            schemes.append(dict(
                VP=VP, K=K, shift=shift, blkI=take(C).bitcast(I32),
                tI=take(C).bitcast(I32), blkF=take(C), tF=take(C), end=take(C), cmp=take(C * VP // 2).bitcast(BF16).rearrange("p (c v) -> p c v", c=C),
                tv=take(VP), tvc=take(VP), jv=take(VP + 2), tcol=take(K).bitcast(I32)))
        rowsI = take(K1 * 3 * TE + K2 * 2 * TE).bitcast(I32)
        rowsF = take(K1 * 4 * TE + K2 * 2 * TE)
        abI = take(K1 * 2 * TE).bitcast(I32)
        tabT = take(4 * 2 * V1P).rearrange("p (k h v) -> p k h v", k=4, h=2)
        valid, tmp = take(2 * V1P).rearrange("p (h v) -> p h v", h=2), take(2 * V1P).rearrange("p (h v) -> p h v", h=2)
        src2F = take(2 * V2P).rearrange("p (h v) -> p h v", h=2)
        wB = take(V1P).bitcast(BF16).rearrange("p (h v) -> p h v", h=2)
        r1 = rowsI[:, 0:K1 * 3 * TE].rearrange("p (k a e) -> p k a e", k=K1, a=3)
        r2 = rowsI[:, K1 * 3 * TE:].rearrange("p (k a e) -> p k a e", k=K2, a=2)
        f1 = rowsF[:, 0:K1 * 4 * TE].rearrange("p (k a e) -> p k a e", k=K1, a=4)
        f2 = rowsF[:, K1 * 4 * TE:].rearrange("p (k a e) -> p k a e", k=K2, a=2)
        ab = abI.rearrange("p (k a e) -> p k a e", k=K1, a=2)

        s_iota = sem("tab_iota"); s_last = sem("tab_last"); s_dve = sem("tab_dve"); s_cmp = sem("tab_cmp")
        s_tv = sem("tab_tv"); s_tvs = sem("tab_tvs"); s_tc = sem("tab_tcol"); s_tcs = sem("tab_tcols")
        s_rows = m.rows_landed; s_rowsF = sem("tab_rowsF"); s_tr = sem("tab_tr"); s_trs = sem("tab_trs")
        s_pool = sem("tab_pool"); s_dve2 = sem("tab_dve2")
        items = []
        for k in range(K1):
            for arr in range(4):
                for h in range(2):
                    items.append((f1[:, k, arr, h * P:(h + 1) * P], tabT[:, arr, h, k * P:(k + 1) * P]))
        for k in range(K2):
            for arr, to in enumerate((m.rel2, src2F)):
                for h in range(2):
                    items.append((f2[:, k, arr, h * P:(h + 1) * P], to[:, h, k * P:min((k + 1) * P, V2P)]))
        block = ctx.enter_context(nc.Block())

        @block.sync
        def _(sp):
            sp.dma_start(lastI, last).then_inc(s_last, 16)

        @block.gpsimd
        def _(po):
            po.iota(iotaI, pattern=[[1, V1P]], base=0, channel_multiplier=0).then_inc(s_iota, 1)
            po.iota(vmodI, pattern=[[0, V1P // SPARE], [1, SPARE]], base=0, channel_multiplier=0).then_inc(s_iota, 1)
            for s in schemes:
                po.iota(s["tI"], pattern=[[P, C]], base=0, channel_multiplier=1).then_inc(s_iota, 1)
            po.memset(m.ident[:, :], 0.0).then_inc(s_pool, 1)
            po.wait_ge(s_pool, 1)
            po.affine_select(out=m.ident[:, :], in_=m.ident[:, :], compare_op=ALU.not_equal, fill=1.0, base=0,
                             pattern=[[-1, P]], channel_multiplier=1).then_inc(s_iota, 1)
            po.wait_ge(s_tcs, 1)
            for k in range(K1):
                for a, arr in enumerate((dst, src)):
                    po.indirect_dma_start(r1[:, k, a, :], None, arr, bass.IndirectOffsetOnAxis(
                        ap=schemes[0]["tcol"][:, k:k + 1], axis=0)).then_inc(s_rows, 16)
                po.indirect_dma_start(r1[:, k, 2, :].bitcast(F32), None, w, bass.IndirectOffsetOnAxis(
                    ap=schemes[0]["tcol"][:, k:k + 1], axis=0)).then_inc(s_rows, 16)
            po.wait_ge(s_tcs, 2)
            for k in range(K2):
                for a, arr in enumerate((dst, src)):
                    po.indirect_dma_start(r2[:, k, a, :], None, arr, bass.IndirectOffsetOnAxis(
                        ap=schemes[1]["tcol"][:, k:k + 1], axis=0)).then_inc(s_rows, 16)

        @block.tensor
        def _(pe):
            pe.wait_ge(s_iota, 5)
            for n, s in enumerate(schemes):
                pe.wait_ge(s_cmp, n + 1)
                half = s["VP"] // 2
                for q in range(2):
                    for c in range(C):
                        ins = pe.matmul(m.PB[2 * n + q][:, 0:half], m.onesB[:, :], s["cmp"][:, c, q * half:(q + 1) * half],
                                        start=(c == 0), stop=(c == C - 1))
                ins.then_inc(s_tv, 1)
            for n, s in enumerate(schemes):
                pe.wait_ge(s_tvs, n + 1)
                for k in range(s["K"]):
                    ins = pe.transpose(m.PB[4 + 2 * n + k // 4][:, (k % 4) * P:(k % 4 + 1) * P], s["tvc"][:, k * P:(k + 1) * P], m.ident[:, :])
                ins.then_inc(s_tc, 1)
            pe.wait_ge(s_rowsF, 1)
            for i, (a, _) in enumerate(items):
                if i % 4 == 0 and i >= 8:
                    pe.wait_ge(s_trs, i // 4 - 1)
                ins = pe.transpose(m.PB[i // 4 % 2][:, (i % 4) * P:(i % 4 + 1) * P], a, m.ident[:, :])
                if i % 4 == 3 or i == len(items) - 1:
                    ins.then_inc(s_tr, 1)

        @block.scalar
        def _(act):
            for i0 in range(0, len(items), 4):
                act.wait_ge(s_tr, i0 // 4 + 1)
                for i in range(i0, min(i0 + 4, len(items))):
                    ins = nc.scalar.copy(items[i][1], m.PB[i // 4 % 2][:, (i % 4) * P:(i % 4) * P + items[i][1].shape[-1]])
                ins.then_inc(s_trs, 1)

        @block.vector
        def _(dve):
            chain = Chain(dve, s_dve)
            chain(dve.memset(m.onesB[:, :], 1.0))
            dve.wait_ge(s_iota, 5)
            chain(dve.tensor_copy(iotaF, iotaI))
            chain(dve.tensor_copy(vmodF, vmodI))
            chain(dve.tensor_copy(m.iotaH[:, :], iotaI[:, 0:BCOL]))
            dve.wait_ge(s_last, 16)
            for s in schemes:
                chain(dve.tensor_scalar(s["blkI"], lastI, s["shift"], None, ALU.arith_shift_right))
                chain(dve.tensor_copy(s["blkF"], s["blkI"]))
                chain(dve.tensor_copy(s["tF"], s["tI"]))
                chain(dve.tensor_tensor(s["end"], s["blkF"], s["tF"], ALU.add))
                for c in range(C):
                    ins = dve.tensor_scalar(s["cmp"][:, c, :], iotaF[:, 0:s["VP"]], s["end"][:, c:c + 1], None, ALU.is_gt)
                ins.then_inc(s_cmp, 1)
            for n, s in enumerate(schemes):
                dve.wait_ge(s_tv, n + 1)
                half = s["VP"] // 2
                for q in range(2):
                    part = slice(q * half, (q + 1) * half)
                    chain(dve.tensor_copy(s["tv"][:, part], m.PB[2 * n + q][:, 0:half]))
                dve.memset(s["jv"][:, 0:1], -1.0)
                chain(dve.tensor_tensor(s["jv"][:, 1:s["VP"] + 1], iotaF[:, 0:s["VP"]], s["tv"], ALU.subtract))
                dve.tensor_scalar(s["tvc"], s["tv"], float(T1 - 1), None, ALU.min).then_inc(s_tvs, 1)
            for n, s in enumerate(schemes):
                dve.wait_ge(s_tc, n + 1)
                for g in range(-(-s["K"] // 4)):
                    k = min(4, s["K"] - 4 * g)
                    ins = dve.tensor_copy(s["tcol"][:, 4 * g:4 * g + k],
                                          m.PB[4 + 2 * n + g][:, 0:k * P].rearrange("p (k v) -> p k v", k=k)[:, :, 0])
                ins.then_inc(s_tcs, 1)
            j1 = schemes[0]["jv"][:, 1:V1P + 1]
            dve.wait_ge(s_tvs, 2)
            more = tmp[:, 0, :]
            chain(dve.memset(more, 0.0))
            chain(dve.tensor_tensor(more[:, 0:V1 - 1], schemes[0]["jv"][:, 2:V1 + 1], j1[:, 0:V1 - 1], ALU.is_equal))
            spare = tmp[:, 1, :]
            chain(dve.tensor_scalar(spare, vmodF, float(J1), None, ALU.add))
            chain(dve.tensor_tensor(spare, spare, j1, ALU.subtract))
            chain(dve.tensor_tensor(spare, spare, more, ALU.mult))
            chain(dve.tensor_tensor(spare, spare, j1, ALU.add))
            chain(dve.tensor_scalar(m.vis[PLACE:PLACE + 1, 0:V1], spare[PLACE:PLACE + 1, 0:V1], 0.0, None, ALU.add))
            two = j1[BLOCK1:BLOCK1 + 1, 0:V1].rearrange("p (k u) -> p k u", u=2)
            chain(dve.scalar_tensor_tensor(m.blocks1(), two[:, :, 1], float(J1), two[:, :, 0], ALU.mult, ALU.add))
            chain(dve.tensor_tensor(t1["keep"], j1, schemes[0]["jv"][:, 0:V1P], ALU.is_equal))
            dve.wait_ge(s_rows, 16 * (3 * K1 + 2 * K2))
            for k in range(K1):
                chain(dve.tensor_scalar(ab[:, k, 0, :], r1[:, k, 1, :], 7, None, ALU.arith_shift_right))
                chain(dve.tensor_scalar(ab[:, k, 1, :], r1[:, k, 1, :], P - 1, None, ALU.bitwise_and))
                dve.tensor_copy(f1[:, k, 0, :], r1[:, k, 0, :])
                dve.tensor_copy(f1[:, k, 1, :], ab[:, k, 0, :])
                dve.tensor_copy(f1[:, k, 2, :], ab[:, k, 1, :])
                chain(dve.tensor_copy(f1[:, k, 3, :], r1[:, k, 2, :].bitcast(F32)))
            dve.tensor_copy(f2.rearrange("p k a e -> p (k a e)"), r2.rearrange("p k a e -> p (k a e)")).then_inc(s_rowsF, 1)
            dve.wait_ge(s_trs, -(-len(items) // 4))
            dstT, chT, rowT, wT = (tabT[:, i, :, :] for i in range(4))
            for h in range(2):
                chain(dve.scalar_tensor_tensor(tmp[:, h, :], j1, -float(BW), dstT[:, h, :], ALU.mult, ALU.add))
            chain(dve.tensor_scalar(valid, tmp, 0.0, None, ALU.is_ge))
            chain(dve.scalar_tensor_tensor(valid, tmp, float(BW - 1), valid, ALU.is_le, ALU.mult))
            chain(dve.scalar_tensor_tensor(tmp, chT, float(BW), tmp, ALU.mult, ALU.add))
            chain(dve.scalar_tensor_tensor(tmp, tmp, 1.0, valid, ALU.add, ALU.mult))
            chain(dve.tensor_scalar(t1["col"], tmp, -1.0, None, ALU.add))
            chain(dve.tensor_copy(t1["row"], rowT))
            for i in range(3):
                chain(dve.tensor_copy(wB, wT))
                chain(dve.tensor_copy(t1["w"][i], wB))
                if i < 2:
                    chain(dve.tensor_tensor(wT, wT, t1["w"][i], ALU.subtract))
            j2 = schemes[1]["jv"][:, 1:V2P + 1]
            for h in range(2):
                chain(dve.scalar_tensor_tensor(m.rel2[:, h, :], j2, -float(P), m.rel2[:, h, :], ALU.mult, ALU.add))
            chain(dve.tensor_copy(m.src2[:, :, :], src2F))
            two = schemes[1]["tvc"][TILE2:TILE2 + 1, 0:V2P].rearrange("p (k u) -> p k u", u=2)
            chain(dve.scalar_tensor_tensor(m.tiles2(), two[:, :, 1], float(T1), two[:, :, 0], ALU.mult, ALU.add))
            own = tmp[BLOCK2:BLOCK2 + 1, 0, 0:V2P + 4]
            chain(dve.memset(own, 0.0))
            chain(dve.tensor_scalar(own[:, 3:3 + V2P], j2[BLOCK2:BLOCK2 + 1, :], float(J2 - 1), None, ALU.min))
            four = own.rearrange("p (k u) -> p k u", u=2)
            four = [four[:, 0:V2P // 2, 0], four[:, 0:V2P // 2, 1], four[:, 1:1 + V2P // 2, 1], four[:, 2:2 + V2P // 2, 0]]
            more = tmp[BLOCK2:BLOCK2 + 1, 1, 0:V2P // 2]
            chain(dve.scalar_tensor_tensor(more, four[3], float(JPAD), four[2], ALU.mult, ALU.add))
            chain(dve.scalar_tensor_tensor(more, more, float(JPAD), four[1], ALU.mult, ALU.add))
            chain(dve.scalar_tensor_tensor(m.blocks2(), more, float(JPAD), four[0], ALU.mult, ALU.add))


def stage_build(nc, m, t1, aw):
    with ExitStack() as ctx:
        sem = lambda n: ctx.enter_context(nc.semaphore(n))
        cnt = [m.work2[:, i * BCOL // 2:(i + 1) * BCOL // 2].bitcast(F16) for i in range(2)]
        cur_w = [m.work2[:, (1 + i) * BCOL:(2 + i) * BCOL] for i in range(3)]
        o = 4 * BCOL
        rows, cols = [], []
        for i in range(OH):
            rows.append(m.work2[:, o:o + 2 * 4 * P // 2].bitcast(BF16).rearrange("p (h k r) -> p h k r", h=2, k=4))
            o += 4 * P
            cols.append(m.work2[:, o:o + BCOL].bitcast(F16).rearrange("p (h c) -> p h c", h=2))
            o += BCOL
        gate, gateP, zero = m.colsN[:, 0, 0:1], m.colsN[:, 1, 0:1], m.colsN[:, 2, 0:1]
        psc = [m.PB[0], m.PB[1]]
        psw = [m.PB[2], m.PB[3]]
        counts = m.counts()

        oh_ready = sem("oh_ready")
        rows_ready = sem("rows_ready")
        vis_done = sem("vis_done")
        cur_ready = sem("cur_ready")
        cnt_copied = sem("cnt_copied")
        cnt_stored = sem("cnt_stored")
        cleared = sem("cleared")
        w_stored = [sem(f"w_stored{i}") for i in range(3)]
        gated = sem("gated")
        gatedP = sem("gatedP")
        init = sem("build_init")
        block = ctx.enter_context(nc.Block())

        @block.sync
        def _(sp):
            def store(v, k):
                place = sp.value_load(m.vis[PLACE:PLACE + 1, bass.ds(v, 1)], min_val=0, max_val=J1 + SPARE - 1)
                sp.wait_ge(cur_ready, v + 1)
                sp.dma_start(aw[bass.ds(place, 1), :, :].rearrange("j p c -> p (j c)"), cur_w[k]).then_inc(w_stored[k], 16)

            with sp.Fori(0, V1 // 3) as n:
                for u in range(3):
                    store(n * 3 + u, u)
            for v in range(V1 // 3 * 3, V1):
                store(v, v % 3)
            for k in range(3):
                sp.wait_ge(w_stored[k], 16 * len(range(k, V1, 3)))

        @block.vector
        def _(dve):
            dve.memset(zero, 0.0)
            dve.memset(gate, 0.0)
            dve.memset(gateP, 0.0)
            dve.memset(m.work2[:, 0:4 * BCOL], 0.0).then_inc(init, 1)
            dve.wait_ge(init, 1)

            def onehots(v, k, first=False):
                if not first:
                    dve.wait_ge(vis_done, v - OH + 1)
                for h in range(2):
                    dve.tensor_scalar(rows[k][:, h, 0, :], m.iotaH[:, 0:P], t1["row"][:, h, bass.ds(v, 1)], None, ALU.is_equal)
                    dve.tensor_scalar(cols[k][:, h, :], m.iotaH[:, :], t1["col"][:, h, bass.ds(v, 1)], None, ALU.is_equal)
                for i in (1, 2):
                    ins = dve.tensor_scalar(rows[k][:, 1, 1 + i, :], m.iotaH[:, 0:P], t1["row"][:, 1, bass.ds(v, 1)],
                                            t1["w"][i][:, 1, bass.ds(v, 1)], ALU.is_equal, ALU.mult)
                ins.then_inc(oh_ready, 1)

            def running(v, k, w, stores, first=False):
                keep = t1["keep"][:, bass.ds(v, 1)]
                dve.wait_ge(vis_done, v + 1)
                if not isinstance(stores, int) or stores:
                    dve.wait_ge(w_stored[w], stores * 16)
                if not first or k:
                    dve.wait_ge(cur_ready, v)
                dve.scalar_tensor_tensor(cur_w[w], cur_w[(w + 2) % 3], keep, psw[k][:, 0:BCOL], ALU.mult, ALU.add).then_inc(cur_ready, 1)

            onehots(0, 0, True)
            onehots(1, 1, True)
            onehots(2, 2, True)
            dve.memset(m.big[:, 0:NCH * NDST // 4].bitcast(F16), 0.0).then_inc(cleared, 1)
            running(0, 0, 0, 0, True)
            onehots(3, 0)
            running(1, 1, 1, 0, True)
            for u in range(6):
                onehots(4 + u, (4 + u) % OH)
                running(2 + u, u % 2, (2 + u) % 3, (2 + u) // 3)
            with dve.Fori(1, (V1 - 4) // 6) as n:
                for u in range(6):
                    v = n * 6 + (2 + u)
                    onehots(v + 2, (4 + u) % OH)
                    running(v, u % 2, (2 + u) % 3, n * 2 + (2 + u) // 3)
            for v in (V1 - 2, V1 - 1):
                running(v, v % 2, v % 3, v // 3)

        @block.scalar
        def _(act):
            act.wait_ge(init, 1)

            def copy_counts(v, k, first=False):
                act.wait_ge(vis_done, v + 1)
                if not first:
                    act.wait_ge(cnt_stored, v - 1)
                nc.scalar.copy(cnt[k], psc[k][:, 0:BCOL]).then_inc(cnt_copied, 1)

            def weigh(v, k):
                act.wait_ge(gated, v)
                act.wait_ge(oh_ready, v + 1)
                nc.scalar.copy(gate, zero).then_inc(gated, 1)
                for h in range(2):
                    for i in range(3 if h == 0 else 1):
                        ins = nc.scalar.activation(rows[k][:, h, 1 + i, :], rows[k][:, h, 0, :], ACT.Copy,
                                                   scale=t1["w"][i][:, h, bass.ds(v, 1)])
                    ins.then_inc(rows_ready, 1)

            weigh(0, 0)
            weigh(1, 1)
            for v in range(2, 8):
                copy_counts(v - 2, v % 2, v < 4)
                weigh(v, v % OH)
            with act.Fori(8, V1 - 2, 6) as v:
                for u in range(6):
                    copy_counts(v + u - 2, u % 2)
                    weigh(v + u, (2 + u) % OH)
            for v in (V1 - 2, V1 - 1):
                copy_counts(v - 2, v % 2)
                weigh(v, v % OH)
            for v in (V1 - 2, V1 - 1):
                copy_counts(v, v % 2)

        @block.tensor
        def _(pe):
            def products(v, k, r, first=False, last=False):
                if not first:
                    pe.wait_ge(cur_ready, v - 1)
                    pe.wait_ge(cnt_copied, v - 1)
                for h in range(2):
                    pe.wait_ge(rows_ready, v * 2 + (h + 1))
                    pe.matmul(psc[k][:, 0:BCOL], rows[r][:, h, 0, :], cols[r][:, h, :], start=(h == 0), stop=(h == 1))
                    pe.matmul(m.PB[4][:, 0:BCOL], rows[r][:, h, 0, :], cols[r][:, h, :],
                              start=(first and v == 0 and h == 0), stop=(last and h == 1))
                    for i in range(3):
                        ins = pe.matmul(psw[k][:, 0:BCOL], rows[r][:, h, 1 + i, :], cols[r][:, h, :],
                                        start=(h == 0 and i == 0), stop=(h == 1 and i == 2))
                ins.then_inc(vis_done, 1)

            products(0, 0, 0, True)
            products(1, 1, 1, True)
            with pe.Fori(2, V1 - 2, 6) as v:
                for u in range(6):
                    products(v + u, u % 2, (2 + u) % OH)
            products(V1 - 2, 0, (V1 - 2) % OH)
            products(V1 - 1, 1, (V1 - 1) % OH, last=True)

        @block.gpsimd
        def _(po):
            po.memset(m.big[:, NCH * NDST // 4:], 0.0).then_inc(cleared, 1)
            po.wait_ge(init, 1)
            po.wait_ge(cleared, 2)

            def count(v, k, j):
                if not isinstance(v, int) or v:
                    po.wait_ge(cnt_stored, v)
                po.wait_ge(cnt_copied, v + 1)
                po.tensor_tensor(gateP, zero, zero, ALU.add).then_inc(gatedP, 1)
                block = counts[:, :, bass.ds(j * BW, BW)]
                po.tensor_tensor(block, block, cnt[k].rearrange("p (a w) -> p a w", a=NCH), ALU.add).then_inc(cnt_stored, 1)

            def pair(g):
                x = po.value_load(m.blocks1()[:, bass.ds(g, 1)], min_val=0, max_val=J1 * J1 - 1)
                count(g * 2, 0, x % J1)
                count(g * 2 + 1, 1, x // J1)

            pair(0)
            with po.Fori(1, V1 // 2) as g:
                pair(g)

GROUP = DC // P
LO = 2048.0
HSCALE = 16.0


BLOCKS = P // BW
NPAIRS = HOPS // 2
SUMMED = 5 * BLOCKS
SUMMED_LAST = J1 - SUMMED * (NPAIRS - 1)
NG = -(-NCH // GROUP)


def chunks(g):
    return range(g * GROUP, min(NCH, (g + 1) * GROUP))


def of_group(v, g):
    return v[:, g * GROUP:min(NCH, (g + 1) * GROUP)]


def width(c):
    return min(DC, NDST - c * DC)


def dve_norm(dve, chain, out, x, tmp, stat, var_ready, std_ready, n):
    mean, var = stat
    chain(dve.tensor_reduce(mean, x, op=ALU.add, axis=X))
    chain(dve.tensor_scalar(mean, mean, 1.0 / D, None, ALU.mult))
    chain(dve.tensor_tensor(out, x, spread(mean, D), ALU.subtract))
    chain(dve.tensor_tensor(tmp, out, out, ALU.mult))
    chain(dve.tensor_reduce(var, tmp, op=ALU.add, axis=X))
    dve.tensor_scalar(var, var, 1.0 / D, EPS, ALU.mult, ALU.add).then_inc(var_ready, 1)
    dve.wait_ge(std_ready, n)
    chain(dve.reciprocal(var, var))
    chain(dve.tensor_tensor(out, out, spread(var, D), ALU.mult))


class Linear:

    def __init__(self, nc, ctx, name, m, bufs, cin, cout, banks=(0, 1, 2, 3), more=(), after=None):
        if after:
            self.turned, self.copied, self.done, self.taken, self.base = after.turned, after.copied, after.done, after.taken, after.base + NG
        else:
            sem = lambda n: ctx.enter_context(nc.semaphore(f"{name}_{n}"))
            self.turned, self.copied, self.done, self.taken, self.base = sem("turned"), sem("copied"), sem("done"), sem("taken"), 0
        self.bufs = bufs
        self.cin, self.cout = cin, cout
        self.psT = [[m.PB[banks[0]], m.PB[banks[1]]]] + [[m.PB[b] for b in more]] * (len(bufs) - 1)
        self.psO = [m.PB[banks[2]], m.PB[banks[3]]]
        self.ident = m.ident[:, :]

    def tensor(self, pe, *parts):
        n0 = self.base
        for g in range(NG + 1):
            if g < NG:
                if n0 + g >= 2:
                    pe.wait_ge(self.copied, n0 + g - 1)
                for i, (rows, _) in enumerate(parts):
                    for k, a in enumerate(chunks(g)):
                        ins = pe.transpose(self.psT[i][g % 2][0:self.cin, k * P:(k + 1) * P], rows(a), self.ident)
                ins.then_inc(self.turned, 1)
            if g >= 1:
                b = g - 1
                pe.wait_ge(self.copied, n0 + b + 1)
                if n0 + b >= 2:
                    pe.wait_ge(self.taken, n0 + b - 1)
                for k in range(len(chunks(b))):
                    for i, (_, weight) in enumerate(parts):
                        ins = pe.matmul(self.psO[b % 2][:, k * self.cout:(k + 1) * self.cout], self.bufs[i][b % 2][:, k * P:(k + 1) * P],
                                        weight, start=(i == 0), stop=(i == len(parts) - 1))
                ins.then_inc(self.done, 1)

    def scalar(self, act, nc):
        n0 = self.base
        for g in range(NG):
            act.wait_ge(self.turned, n0 + g + 1)
            if n0 + g >= 2:
                act.wait_ge(self.done, n0 + g - 1)
            n = len(chunks(g)) * P
            for buf, ps in zip(self.bufs, self.psT):
                ins = nc.scalar.copy(buf[g % 2][:, 0:n], ps[g % 2][0:self.cin, 0:n])
            ins.then_inc(self.copied, 1)

    def result(self, eng, g):
        eng.wait_ge(self.done, self.base + g + 1)
        n = len(chunks(g))
        return self.psO[g % 2][:, 0:n * self.cout].rearrange("p (a c) -> p a c", a=n)

    def all_taken(self, eng):
        eng.wait_ge(self.taken, self.base + NG)


def stage_layer0_start(nc, m, x, wt, bias):
    with ExitStack() as ctx:
        sem = lambda n: ctx.enter_context(nc.semaphore(n))
        small = m.small
        w_sb, bias_sb = small(0), small(1)
        ones16 = small(2).bitcast(F16)
        comb = small(3)
        buf = [m.work2[0:D, i * DC:(i + 1) * DC] for i in range(2)]
        lin = Linear(nc, ctx, "l0", m, [buf], D, D, banks=(5, 6, 7, 4))
        xs, h0, hs, tmp = m.work2[:, 1536:3136].rearrange("p (a d) -> p a d", a=NCH), m.node(1), m.node(2), m.node(3)
        degrow = m.work[:, 2 * NCH * D:4 * NCH * D]
        counts = m.counts()
        cols = m.colsN
        mean, var, din, dout, c1s, c1n, ns = (cols[:, i, :] for i in range(7))
        gm = cols[:, 7, 0:1]; gall = cols[:, 7, 1:2]; ginv = cols[:, 7, 2:3]; gback = cols[:, 7, 3:4]
        s_in = sem("l0_in"); s_dve = sem("l0_dve"); s_one = sem("l0_one"); s_var = sem("l0_var"); s_std = sem("l0_std")
        s_rows = sem("l0_rows"); s_deg = sem("l0_deg"); s_gm = sem("l0_gm"); s_gall = sem("l0_gall")
        s_nvar = sem("l0_nvar"); s_nstd = sem("l0_nstd"); s_dout = sem("l0_dout")
        z16 = m.node(0).rearrange("p a d -> p (a d)").bitcast(F16).rearrange("p (a s d) -> p a s d", a=NCH, s=2)
        block = ctx.enter_context(nc.Block())

        @block.sync
        def _(sp):
            sp.dma_start(xs, x).then_inc(s_in, 16)
            sp.dma_start(w_sb[0:D, :], wt).then_inc(s_in, 16)
            sp.dma_start(bias_sb, bias.partition_broadcast(P)).then_inc(s_in, 16)

        @block.tensor
        def _(pe):
            pe.wait_ge(s_one, 1)
            for c in range(4):
                pe.matmul(m.PB[c][:, 0:width(c)], ones16, counts[:, 0, c * DC:c * DC + width(c)], start=True, stop=False)
            with pe.Fori(1, NCH - 1) as a:
                for c in range(4):
                    pe.matmul(m.PB[c][:, 0:width(c)], ones16, counts[:, bass.ds(a, 1), c * DC:c * DC + width(c)],
                              start=False, stop=False)
            for c in range(4):
                pe.matmul(m.PB[c][:, 0:width(c)], ones16, counts[:, NCH - 1, c * DC:c * DC + width(c)],
                          start=False, stop=True).then_inc(s_deg, 1)
            pe.wait_ge(s_rows, 1)
            pe.wait_ge(s_in, 48)
            pe.wait_ge(s_dout, 1)
            lin.tensor(pe, (lambda a: h0[:, a, :], w_sb[0:D, :]))
            pe.wait_ge(s_dout, 2)
            for c in range(4, NDC):
                pe.matmul(m.PB[c - 4][:, 0:width(c)], ones16, counts[:, 0, c * DC:c * DC + width(c)], start=True, stop=False)
            with pe.Fori(1, NCH - 1) as a:
                for c in range(4, NDC):
                    pe.matmul(m.PB[c - 4][:, 0:width(c)], ones16, counts[:, bass.ds(a, 1), c * DC:c * DC + width(c)],
                              start=False, stop=False)
            for c in range(4, NDC):
                pe.matmul(m.PB[c - 4][:, 0:width(c)], ones16, counts[:, NCH - 1, c * DC:c * DC + width(c)],
                          start=False, stop=True).then_inc(s_deg, 1)

        @block.scalar
        def _(act):
            act.wait_ge(s_var, 1)
            nc.scalar.sqrt(var, var).then_inc(s_std, 1)
            lin.scalar(act, nc)
            act.wait_ge(s_nvar, 1)
            nc.scalar.sqrt(ns, ns).then_inc(s_nstd, 1)
            nc.scalar.sqrt(c1n, c1n).then_inc(s_nstd, 1)

        @block.gpsimd
        def _(po):
            po.wait_ge(s_gm, 1)
            po.partition_all_reduce(gall, gm, P, bass.bass_isa.ReduceOp.max).then_inc(s_gall, 1)

        @block.vector
        def _(dve):
            chain = Chain(dve, s_dve)
            dve.memset(ones16, 1.0).then_inc(s_one, 1)
            dve.tensor_copy(comb[0:D, :], m.ident[0:D, 0:D])
            chain(dve.tensor_scalar(comb[D:P, :], m.ident[D:P, D:P], 1.0 / LO, None, ALU.mult))
            dve.wait_ge(s_in, 48)
            dve_norm(dve, chain, h0, xs, tmp, (mean, var), s_var, s_std, 1)
            dve.tensor_scalar(h0, h0, 0.0, None, ALU.max).then_inc(s_rows, 1)
            dve.tensor_reduce(dout, m.PB[4][:, 0:BCOL].rearrange("p (a w) -> p a w", a=NCH), op=ALU.add, axis=X).then_inc(s_dout, 1)
            chain(dve.memset(degrow[:, NDST:], 0.0))
            dr = degrow.rearrange("p (a n) -> p a n", a=NCH)

            def own(a, b):
                chain(dve.tensor_tensor(dr[:, a:b, :], dr[:, a:b, :], along(m.ident[:, :], b - a), ALU.mult))
                chain(dve.tensor_reduce(din[:, a:b], dr[:, a:b, :], op=ALU.add, axis=X))

            dve.wait_ge(s_deg, 4)
            for c in range(4):
                ins = dve.tensor_copy(degrow[:, c * DC:(c + 1) * DC], m.PB[c][:, :])
            ins.then_inc(s_dout, 1)
            for g in range(NG):
                ps = lin.result(dve, g)
                dve.tensor_tensor(of_group(h0, g), ps, along(bias_sb, len(chunks(g))), ALU.add).then_inc(lin.taken, 1)
            lin.all_taken(dve)
            chain(dve.tensor_reduce(gm, h0.rearrange("p a d -> p (a d)"), op=ALU.max, axis=X, apply_absolute_value=True))
            dve.tensor_scalar(gm, gm, 1e-30, None, ALU.max).then_inc(s_gm, 1)
            dve.wait_ge(s_dout, 2)
            own(0, 4 * GROUP)
            dve.wait_ge(s_gall, 1)
            chain(dve.reciprocal(ginv, gall))
            chain(dve.tensor_scalar(ginv, ginv, HSCALE, None, ALU.mult))
            chain(dve.tensor_scalar(gback, gall, 1.0 / HSCALE, None, ALU.mult))
            chain(dve.tensor_scalar(h0, h0, ginv, None, ALU.mult))
            dve.wait_ge(s_deg, NDC)
            for c in range(4, NDC):
                ins = dve.tensor_copy(degrow[:, c * DC:c * DC + width(c)], m.PB[c - 4][:, 0:width(c)])
            chain(ins)
            own(4 * GROUP, NCH)
            chain(dve.tensor_scalar(ns, dout, 1.0, None, ALU.max))
            dve.tensor_scalar(c1n, din, 1.0, None, ALU.max).then_inc(s_nvar, 1)
            dve.wait_ge(s_nstd, 2)
            chain(dve.reciprocal(ns, ns))
            chain(dve.reciprocal(c1n, c1n))
            chain(dve.scalar_tensor_tensor(ns, dout, 0.0, ns, ALU.is_gt, ALU.mult))
            chain(dve.scalar_tensor_tensor(c1n, din, 0.0, c1n, ALU.is_gt, ALU.mult))
            chain(dve.tensor_scalar(c1n, c1n, 1.0 - ALPHA, None, ALU.mult))
            chain(dve.tensor_tensor(c1s, c1n, ns, ALU.mult))
            chain(dve.tensor_tensor(hs, h0, spread(ns, D), ALU.mult))
            chain(dve.tensor_copy(z16[:, :, 0, :], hs))
            chain(dve.tensor_tensor(tmp, hs, z16[:, :, 0, :], ALU.subtract))
            chain(dve.tensor_scalar(z16[:, :, 1, :], tmp, LO, None, ALU.mult))
            zb = m.zbuf(1)
            chain(dve.memset(zb[:, NCH - 1, :, :], 0.0))
            chain(dve.tensor_scalar(h0, h0, ALPHA, None, ALU.mult))
            chain(dve.tensor_scalar(hs, hs, ALPHA, None, ALU.mult))


def stage_layer0_hops(nc, m, x, aw):
    with ExitStack() as ctx:
        sem = lambda n: ctx.enter_context(nc.semaphore(n))
        counts = m.counts()
        z = [m.zbuf(0), m.zbuf(1)]
        comb = m.small(3)
        h0, hs0, tmp = m.node(1), m.node(2), m.node(3)
        xs = m.node(0)
        c1s, c1n, gback = m.colsN[:, 4, :], m.colsN[:, 5, :], m.colsN[:, 7, 3:4]
        rt = [m.work2[:, i * DC:(i + 1) * DC] for i in range(2)]
        free = 2 * DC + NCH * D + DC + 4 * D
        ring = [m.work2[:, free + i * BCOL:free + (i + 1) * BCOL] for i in range(3)] + [m.work2[:, 2 * DC:2 * DC + BCOL]]
        part = [m.work2[:, free + 3 * BCOL:free + 3 * BCOL + P], m.smalls[:, 0:P]]
        one = m.small(2)[:, 0:1]
        deg = m.colsN[:, 2, :]
        prod_done = sem("hop_prod")
        copied = sem("hop_copied")
        back_done = sem("hop_back")
        mixed = sem("hop_mixed")
        s_dve = sem("hop_dve")
        s_x = sem("hop_x")
        w_landed = [sem(f"hop_w{i}") for i in range(4)]
        s_one = sem("hop_one")
        reduced = sem("hop_reduced")
        deg_done = sem("hop_deg")
        deg_taken = sem("hop_deg_taken")
        summed_in = lambda pair: SUMMED_LAST if isinstance(pair, int) and pair == NPAIRS - 1 else SUMMED
        block = ctx.enter_context(nc.Block())

        @block.tensor
        def _(pe):
            def back(t, c):
                pe.wait_ge(copied, NDC * t + c + 1)
                if c >= 2:
                    pe.wait_ge(mixed, NDC * t + c - 1)
                n = width(c)
                for i in range(-(-n // P)):
                    k = min(P, n - i * P)
                    ins = pe.matmul(m.PB[6 + c % 2][0:k, i * D:(i + 1) * D], rt[c % 2][:, i * P:i * P + k], comb,
                                    start=True, stop=True)
                ins.then_inc(back_done, 1)

            def degrees(pair, q, first=False):
                pe.wait_ge(reduced, pair * SUMMED + min(BLOCKS * (q + 1), summed_in(pair)))
                if q == 0 and not first:
                    pe.wait_ge(deg_taken, pair)
                pe.matmul(m.PB[5][:, q:q + 1], part[q % 2], one, start=True, stop=True).then_inc(deg_done, 1)

            def hop(t, k, pair, first=False):
                for c in range(NDC):
                    for a in range(NCH):
                        if c == 0 and a % GROUP == 0 and not first:
                            pe.wait_ge(mixed, NDC * (t - 1) + a // GROUP + 1)
                        ins = pe.matmul(m.PB[c % 4][:, 0:width(c)], z[k][:, a, :, :], counts[:, a, c * DC:c * DC + width(c)],
                                        start=(a == 0), stop=(a == NCH - 1))
                    ins.then_inc(prod_done, 1)
                    if c >= 1:
                        back(t, c - 1)
                    at = NDC * k + c
                    if at in (4, 6, 8, 10, 12):
                        degrees(pair, (at - 4) // 2, isinstance(pair, int) and pair == 0)
                back(t, NDC - 1)

            pe.wait_ge(s_one, 1)
            hop(0, 0, 0, True)
            hop(1, 1, 0)
            with pe.Fori(1, NPAIRS - 1) as pair:
                hop(pair * 2, 0, pair)
                hop(pair * 2 + 1, 1, pair)
            hop(HOPS - 2, 0, NPAIRS - 1)
            hop(HOPS - 1, 1, NPAIRS - 1)

        @block.scalar
        def _(act):
            def copies(t):
                for c in range(NDC):
                    act.wait_ge(prod_done, NDC * t + c + 1)
                    if c >= 2:
                        act.wait_ge(back_done, NDC * t + c - 1)
                    nc.scalar.copy(rt[c % 2][:, 0:width(c)], m.PB[c % 4][:, 0:width(c)]).then_inc(copied, 1)

            with act.Fori(0, HOPS - 1) as t:
                copies(t)
            act.wait_ge(prod_done, NDC * (HOPS - 1))
            act.dma_start(xs, x).then_inc(s_x, 16)
            copies(HOPS - 1)

        @block.sync
        def _(sp):
            for b in range(4):
                sp.dma_start(ring[b], aw[b, :, :]).then_inc(w_landed[b], 16)
            with sp.Fori(1, J1 // 4) as g:
                for k in range(4):
                    sp.wait_ge(reduced, g * 4 + (k - 3))
                    sp.dma_start(ring[k], aw[bass.ds(g * 4 + k, 1), :, :].rearrange("j p c -> p (j c)")).then_inc(w_landed[k], 16)

        @block.vector
        def _(dve):
            def reduce(pair, i):
                q, r = divmod(i, BLOCKS)
                fixed = isinstance(pair, int)
                dve.wait_ge(w_landed[i % 4], pair * (16 * SUMMED // 4) + 16 * (i // 4 + 1))
                if r == 0 and (q >= 2 or not fixed or pair):
                    dve.wait_ge(deg_done, pair * 5 + (q - 1 if q else 0))
                dve.tensor_reduce(part[q % 2][:, r * BW:(r + 1) * BW], ring[i % 4].rearrange("p (a w) -> p w a", a=NCH),
                                  op=ALU.add, axis=X).then_inc(reduced, 1)

            def take_degrees(pair):
                dve.wait_ge(deg_done, pair * 5 + 5)
                at = pair * 5
                to = deg[:, at:at + 5] if isinstance(pair, int) else deg[:, bass.ds(at, 5)]
                dve.tensor_copy(to, m.PB[5][:, 0:5]).then_inc(deg_taken, 1)

            def mix(t, k, n0, last, pair):
                step = [n0]

                def chain(ins):
                    ins.then_inc(s_dve, 1)
                    step[0] = step[0] + 1
                    dve.wait_ge(s_dve, step[0])

                for c in range(NDC):
                    rows = P if c < NDC - 1 else width(c)
                    g = GROUP if c < NDC - 1 else 1
                    a = slice(c * GROUP, c * GROUP + g)
                    part = lambda v: v[0:rows, a]
                    sp_ = lambda v: v[0:rows, a].unsqueeze(2).to_broadcast([rows, g, D])
                    dve.wait_ge(back_done, NDC * t + c + 1)
                    ps = m.PB[6 + c % 2][0:rows, 0:g * D].rearrange("p (a d) -> p a d", a=g)
                    tc = tmp[0:rows, a, :]
                    if last:
                        chain(dve.tensor_tensor(tc, ps, sp_(c1n), ALU.mult))
                        chain(dve.tensor_tensor(tc, tc, h0[0:rows, a, :], ALU.add))
                        dve.scalar_tensor_tensor(xs[0:rows, a, :], tc, gback[0:rows, :], xs[0:rows, a, :], ALU.mult, ALU.add).then_inc(mixed, 1)
                    else:
                        zn = z[1 - k]
                        chain(dve.tensor_tensor(tc, ps, sp_(c1s), ALU.mult))
                        chain(dve.tensor_tensor(tc, tc, hs0[0:rows, a, :], ALU.add))
                        chain(dve.tensor_copy(zn[0:rows, a, 0, :], tc))
                        chain(dve.tensor_tensor(tc, tc, zn[0:rows, a, 0, :], ALU.subtract))
                        dve.tensor_scalar(zn[0:rows, a, 1, :], tc, LO, None, ALU.mult).then_inc(mixed, 1)
                    for i in range(4 * (NDC * k + c), 4 * (NDC * k + c) + 4):
                        if i < summed_in(pair):
                            reduce(pair, i)
                if k:
                    take_degrees(pair)

            per = 4 * NDC
            dve.memset(one, 1.0).then_inc(s_one, 1)
            mix(0, 0, 0, False, 0)
            mix(1, 1, per, False, 0)
            with dve.Fori(1, NPAIRS - 1) as pair:
                mix(pair * 2, 0, per * 2 * pair, False, pair)
                mix(pair * 2 + 1, 1, per * 2 * pair + per, False, pair)
            mix(HOPS - 2, 0, per * (HOPS - 2), False, NPAIRS - 1)
            dve.wait_ge(s_x, 16)
            mix(HOPS - 1, 1, per * (HOPS - 1), True, NPAIRS - 1)


def stage_layer1(nc, m, aw, wts, biases):
    with ExitStack() as ctx:
        sem = lambda n: ctx.enter_context(nc.semaphore(n))
        NB = DC // BW
        last = width(NDC - 1) // BW
        st = [m.big[:, i * NB * BCOL:(i + 1) * NB * BCOL].rearrange("p (j c) -> p j c", j=NB) for i in range(2)]
        behind = 2 * NB * BCOL + last * BCOL
        st.append(m.big[:, 2 * NB * BCOL:behind].rearrange("p (j c) -> p j c", j=last))
        buffer = lambda c: 2 if c == NDC - 1 else c % 2
        loads = lambda l, c: l + 1 if c == NDC - 1 else (NDC // 2) * l + c // 2 + 1
        xs, tmp = m.node(0), m.node(3)
        z = [m.node(1), m.node(2)]
        w_sb = [m.small(i) for i in range(3)]
        b_sb = [m.small(3 + i) for i in range(3)]
        rt = [m.work2[:, i * DC:(i + 1) * DC] for i in range(2)]
        mean, var, deg, dinv = (m.colsN[:, i, :] for i in range(4))
        s_in = sem("l1_in"); s_dve = sem("l1_dve")
        s_ld = [sem(f"l1_ld{i}") for i in range(3)]; prod_done = sem("l1_prod"); copied = sem("l1_copied")
        back_done = sem("l1_back"); mixed = sem("l1_mixed"); s_var = sem("l1_var"); s_std = sem("l1_std"); s_z = sem("l1_z")
        block = ctx.enter_context(nc.Block())

        @block.sync
        def _(sp):
            for i in range(3):
                sp.dma_start(w_sb[i][0:D, :], wts[i]).then_inc(s_in, 16)
                sp.dma_start(b_sb[i], biases[i].partition_broadcast(P)).then_inc(s_in, 16)
            for l in range(3):
                for c in range(NDC):
                    before = c - 2 if 2 <= c < NDC - 1 else (c - 3 if c < 2 else c - NDC)
                    if l * NDC + before >= 0:
                        sp.wait_ge(prod_done, l * NDC + before + 1)
                    n = width(c) // BW
                    sp.dma_start(st[buffer(c)][:, 0:n, :], aw[c * NB:c * NB + n, :, :].rearrange("j p c -> p j c")).then_inc(s_ld[buffer(c)], 16)

        @block.tensor
        def _(pe):
            def product(l, c, lhsT, rows):
                u = l * NDC + c
                n = width(c)
                pe.wait_ge(s_ld[buffer(c)], 16 * loads(l, c))
                if u >= 3:
                    pe.wait_ge(copied, u - 2)
                out = m.PB[u % 3][0:rows, 0:n]
                for a in range(NCH):
                    if l and c == 0 and a % GROUP == 0:
                        pe.wait_ge(mixed, (l - 1) * NDC + a // GROUP + 1)
                    ins = pe.matmul(out, lhsT(a), st[buffer(c)][:, 0:n // BW, a * BW:(a + 1) * BW], start=(a == 0), stop=False)
                for i in range(-(-n // P)):
                    k = min(P, n - i * P)
                    ins = pe.matmul(m.PB[u % 3][0:rows, i * P:i * P + k], lhsT(c * GROUP + i), m.ident[:, 0:k], start=False,
                                    stop=(i == -(-n // P) - 1))
                ins.then_inc(prod_done, 1)

            def back(l, c):
                u = l * NDC + c
                pe.wait_ge(copied, u + 1)
                if u >= 2:
                    pe.wait_ge(mixed, u - 1)
                n = width(c)
                for i in range(-(-n // P)):
                    k = min(P, n - i * P)
                    ins = pe.matmul(m.PB[6 + u % 2][0:k, i * D:(i + 1) * D], rt[u % 2][0:D, i * P:i * P + k],
                                    w_sb[l][0:D, :], start=True, stop=True)
                ins.then_inc(back_done, 1)

            pe.wait_ge(s_in, 96)
            pe.wait_ge(s_z, 1)
            for l in range(3):
                for c in range(NDC):
                    product(l, c, lambda a: z[l % 2][:, a, :], D)
                    if c:
                        back(l, c - 1)
                back(l, NDC - 1)

        @block.scalar
        def _(act):
            for n in range(2):
                act.wait_ge(s_var, n + 1)
                v = (var, dinv)[n]
                nc.scalar.sqrt(v, v).then_inc(s_std, 1)
            for u in range(3 * NDC):
                act.wait_ge(prod_done, u + 1)
                if u >= 2:
                    act.wait_ge(back_done, u - 1)
                n = width(u % NDC)
                nc.scalar.copy(rt[u % 2][0:D, 0:n], m.PB[u % 3][0:D, 0:n]).then_inc(copied, 1)

        @block.vector
        def _(dve):
            chain = Chain(dve, s_dve)
            dve_norm(dve, chain, z[0], xs, tmp, (mean, var), s_var, s_std, 1)
            chain(dve.tensor_scalar(z[0], z[0], 0.0, None, ALU.max))
            chain(dve.memset(z[1][:, NCH - 1, :], 0.0))
            chain(dve.tensor_scalar(deg, deg, 1.0, None, ALU.add))
            dve.tensor_scalar(dinv, deg, 1e-30, None, ALU.max).then_inc(s_var, 1)
            dve.wait_ge(s_std, 2)
            chain(dve.reciprocal(dinv, dinv))
            chain(dve.scalar_tensor_tensor(dinv, deg, 0.0, dinv, ALU.is_gt, ALU.mult))
            dve.tensor_tensor(z[0], z[0], spread(dinv, D), ALU.mult).then_inc(s_z, 1)
            dve.wait_ge(s_in, 96)
            for u in range(3 * NDC):
                l, c = divmod(u, NDC)
                dve.wait_ge(back_done, u + 1)
                rows = P if c < NDC - 1 else width(c)
                g = GROUP if c < NDC - 1 else 1
                a = slice(c * GROUP, c * GROUP + g)
                ps = m.PB[6 + u % 2][0:rows, 0:g * D].rearrange("p (a d) -> p a d", a=g)
                di = dinv[0:rows, a].unsqueeze(2).to_broadcast([rows, g, D])
                bb = b_sb[l][0:rows, :].unsqueeze(1).to_broadcast([rows, g, D])
                tc = tmp[0:rows, a, :]
                chain(dve.tensor_tensor(tc, ps, di, ALU.mult))
                chain(dve.tensor_tensor(tc, tc, bb, ALU.add))
                if l < 2:
                    chain(dve.tensor_scalar(tc, tc, 0.0, None, ALU.max))
                    dve.tensor_tensor(z[1 - l][0:rows, a, :], tc, di, ALU.mult).then_inc(mixed, 1)
                else:
                    dve.tensor_tensor(xs[0:rows, a, :], xs[0:rows, a, :], tc, ALU.add).then_inc(mixed, 1)

HEADS = 2
HC = HEADS * D
DE = 32
FW = DE + 1
VW = FW + D
HALFROW = FW + 2 * HC
AHEAD = (0, FW + D + HC)
FEAT = (0, D)
SUM = (DE, D + DE)
VAL = (FW, 0)
MW = D + 1
BIG = 1e30
LOW = 1e20


class Visit:

    def __init__(self, g, c):
        self.g, self.c = g, c

    def __add__(self, n):
        return Visit(self.g, self.c + n)

    @property
    def fixed(self):
        return isinstance(self.g, int)

    @property
    def n(self):
        return self.g * R + self.c

    def slot(self, k):
        return self.c % k

    def landed(self, ring=R, each=1):
        return (self.g * (R // ring) + (self.c // ring + 1)) * (16 * each)

    def exists(self):
        return not self.fixed or 0 <= self.n < V2


def walk(eng, step, before, after):
    head = 2 * R - 2
    rounds = (V2 - head) // R - 1
    for i in range(-before, head):
        step(Visit(0, i))
    with eng.Fori(0, rounds) as g:
        for u in range(R):
            step(Visit(g, head + u))
    for i in range(head + rounds * R, V2 + after):
        step(Visit(0, i))


def wait(eng, sem, n):
    if not isinstance(n, int) or n > 0:
        eng.wait_ge(sem, n)


class Take:
    def __init__(self, region):
        self.region, self.at = region, 0

    def __call__(self, n, rows=P):
        self.at += n
        return self.region[0:rows, self.at - n:self.at]


def stage_attend_tables(nc, m, keep, we, wq, wk, wv, bq, bk, bv, g1, b1, kv_t, q_t):
    with ExitStack() as ctx:
        sem = lambda n: ctx.enter_context(nc.semaphore(n))
        take = Take(m.big)
        kv = take(NCH * 2 * HC).rearrange("p (a c) -> p a c", a=NCH)
        qT = take(NCH * HEADS * P).rearrange("p (a h n) -> p a h n", a=NCH, h=HEADS)
        w_kv, w_q = take(2 * HC, D), take(HC, D)
        b_kv, bq_c = take(2 * HC), take(1)
        g_sb, b_sb = take(D), take(D)
        hT = [take(P, D) for _ in range(2)]
        qf = [take(P) for _ in range(2)]
        w_e = take(HC, DE)
        w_x = keep["w_x"]
        xs, h, hn, tmp = (m.node(i) for i in range(4))
        mean, var = m.colsN[:, 0, :], m.colsN[:, 1, :]
        s_in = sem("at_in"); s_dve = sem("at_dve"); s_var = sem("at_var"); s_std = sem("at_std"); s_rows = sem("at_rows")
        turned = sem("at_turned"); copied = sem("at_copied"); done = sem("at_done"); taken = sem("at_taken"); s_we = sem("at_we"); s_wx = sem("at_wx"); q_ready = sem("at_q")
        q_done = sem("at_q_done"); x_done = sem("at_x"); x_taken = sem("at_xs"); s_out = sem("at_out")
        block = ctx.enter_context(nc.Block())

        @block.sync
        def _(sp):
            sp.dma_start(w_kv[:, 0:D], wv[:, 0:D]).then_inc(s_in, 16)
            sp.dma_start(w_kv[:, D:D + HC], wk).then_inc(s_in, 16)
            sp.dma_start(w_kv[:, D + HC:], wv[:, D:]).then_inc(s_in, 16)
            sp.dma_start(w_e, we).then_inc(s_in, 16)
            sp.dma_start(w_q, wq).then_inc(s_in, 16)
            sp.dma_start(b_kv[:, 0:D], bv[0:D].partition_broadcast(P)).then_inc(s_in, 16)
            sp.dma_start(b_kv[:, D:D + HC], bk.partition_broadcast(P)).then_inc(s_in, 16)
            sp.dma_start(b_kv[:, D + HC:], bv[D:].partition_broadcast(P)).then_inc(s_in, 16)
            sp.dma_start(bq_c, bq.unsqueeze(1)).then_inc(s_in, 16)
            sp.dma_start(g_sb, g1.partition_broadcast(P)).then_inc(s_in, 16)
            sp.dma_start(b_sb, b1.partition_broadcast(P)).then_inc(s_in, 16)
            for i in range(5):
                sp.wait_ge(taken, 5 * (i + 1))
                sp.wait_ge(x_taken, 5 * (i + 1))
                a = slice(5 * i, 5 * i + 5)
                sp.dma_start(kv_t[a, :, :].rearrange("a p c -> p a c"), kv[:, a, :]).then_inc(s_out, 16)
                sp.dma_start(q_t[a, :, :].rearrange("a p n -> p a n"), qT[:, a, :, :].rearrange("p a h n -> p a (h n)")).then_inc(s_out, 16)
            sp.wait_ge(s_out, 160)

        @block.tensor
        def _(pe):
            pe.wait_ge(s_in, 176)
            pe.transpose(m.PB[6][:, 0:DE], w_e, m.ident[0:DE, 0:DE]).then_inc(s_we, 1)
            pe.wait_ge(s_wx, 2)
            pe.wait_ge(s_rows, 1)
            for a in range(NCH + 2):
                if a < NCH:
                    wait(pe, copied, a - 1)
                    pe.transpose(m.PB[a % 2][0:D, 0:P], hn[:, a, :], m.ident[:, :]).then_inc(turned, 1)
                if 1 <= a <= NCH:
                    b = a - 1
                    pe.wait_ge(copied, b + 1)
                    wait(pe, taken, b - 1)
                    pe.matmul(m.PB[4 + b % 2][:, 0:P], w_q, hT[b % 2], start=True, stop=True).then_inc(q_done, 1)
                    pe.matmul(m.PB[2 + b % 2][:, 0:2 * HC], hT[b % 2], w_kv, start=True, stop=True).then_inc(done, 1)
                if a >= 2:
                    b = a - 2
                    pe.wait_ge(q_ready, b + 1)
                    wait(pe, x_taken, b - 1)
                    pe.matmul(m.PB[6 + b % 2][:, 0:P], w_x, qf[b % 2], start=True, stop=True).then_inc(x_done, 1)

        @block.scalar
        def _(act):
            for n in range(2):
                act.wait_ge(s_var, n + 1)
                nc.scalar.sqrt(var, var).then_inc(s_std, 1)
            for a in range(NCH):
                act.wait_ge(turned, a + 1)
                wait(act, done, a - 1)
                nc.scalar.copy(hT[a % 2], m.PB[a % 2][0:D, 0:P]).then_inc(copied, 1)
                for b in range(max(0, a - 2), a - 1 if a < NCH - 1 else NCH):
                    act.wait_ge(x_done, b + 1)
                    nc.scalar.copy(qT[D:P, b, 0, :], m.PB[6 + b % 2][D:P, 0:P])
                    nc.scalar.copy(qT[0:D, b, 1, :], m.PB[6 + b % 2][0:D, 0:P]).then_inc(x_taken, 1)

        @block.vector
        def _(dve):
            chain = Chain(dve, s_dve)
            dve.memset(w_x, 0.0).then_inc(s_wx, 1)
            dve.wait_ge(s_wx, 1)
            dve.wait_ge(s_we, 1)
            dve.tensor_copy(w_x[0:D, D:D + DE], m.PB[6][0:D, 0:DE])
            dve.tensor_copy(w_x[D:P, 0:DE], m.PB[6][D:P, 0:DE]).then_inc(s_wx, 1)
            dve_norm(dve, chain, h, xs, tmp, (mean, var), s_var, s_std, 1)
            chain(dve.tensor_scalar(h, h, 0.0, None, ALU.max))
            dve_norm(dve, chain, hn, h, tmp, (mean, var), s_var, s_std, 2)
            dve.wait_ge(s_in, 176)
            chain(dve.tensor_tensor(hn, hn, along(g_sb, NCH), ALU.mult))
            dve.tensor_tensor(hn, hn, along(b_sb, NCH), ALU.add).then_inc(s_rows, 1)
            for a in range(NCH):
                dve.wait_ge(q_done, a + 1)
                wait(dve, x_done, a - 1)
                dve.tensor_scalar(qf[a % 2], m.PB[4 + a % 2][:, 0:P], bq_c, float(D) ** -0.5, ALU.add, ALU.mult).then_inc(q_ready, 1)
                for hd in range(HEADS):
                    rows = slice(hd * D, (hd + 1) * D)
                    dve.tensor_scalar(qT[rows, a, hd, :], m.PB[4 + a % 2][rows, 0:P], bq_c[rows, :], float(D) ** -0.5, ALU.add, ALU.mult)
                dve.wait_ge(done, a + 1)
                dve.tensor_tensor(kv[:, a, :], m.PB[2 + a % 2][:, 0:2 * HC], b_kv, ALU.add).then_inc(taken, 1)


def stage_attend(nc, m, keep, ea, eaT, kv_t, q_t):
    with ExitStack() as ctx:
        sem = lambda n: ctx.enter_context(nc.semaphore(n))
        take = Take(m.big)
        halves = lambda a: a.rearrange("p (s c) -> p s c", s=2)
        acc = keep["acc"]
        take.at = keep["end"]
        nmax = take(JPAD * HEADS).rearrange("p (a h) -> p a h", a=JPAD)
        pen = take(P).bitcast(BF16)
        rows = [halves(take(2 * 2 * HALFROW)) for _ in range(R)]
        KF = [take(HEADS * TE).rearrange("p (h e) -> p h e", h=HEADS) for _ in range(R)]
        qT = [take(HEADS * P) for _ in range(R)]
        idx = take(2 * R).bitcast(I32)
        oh = [halves(take(P).bitcast(BF16)) for _ in range(4)]
        Pm = [take(2 * TE) for _ in range(4)]
        PT = [take(2 * TE) for _ in range(2)]
        nm = [take(HEADS) for _ in range(4)]
        rm, df = [take(HEADS) for _ in range(4)], [take(HEADS) for _ in range(4)]
        corr = [take(HEADS) for _ in range(4)]
        gateP, gz = take(1), take(1)
        assert take.at <= NCH * NDST // 2
        psK = m.PB[0][:, 0:TE]
        psS = [m.PB[1 + i][:, :] for i in range(4)]
        psT = m.PB[5][:, :]
        psA = [m.PB[6][:, 0:2 * VW], m.PB[7][:, 0:2 * VW]]

        init = sem("av_init")
        idx_ready = sem("av_idx")
        landed_g = m.kv_landed
        landed_e = [sem(f"av_e{i}") for i in range(R)]
        gated = sem("av_gated")
        k_turned = sem("av_kT")
        k_copied = sem("av_kTs")
        oh_ready = sem("av_oh")
        scored = sem("av_S")
        max_ready = sem("av_max")
        exp_ready = sem("av_P")
        p_turned = sem("av_PT")
        p_copied = sem("av_PTs")
        summed = sem("av_A")
        s_small = sem("av_small")
        acc_ready = sem("av_acc")
        block = ctx.enter_context(nc.Block())

        @block.sync
        def _(sp):
            sp.wait_ge(init, 1)

            tiles = [None, None]

            def step(v):
                k = v.slot(R)
                if v.c % 2 == 0:
                    tiles[:] = m.tiles_of(sp, v.n)
                t = tiles[v.c % 2]
                j = (v.n - t) & (JPAD - 1)
                wait(sp, scored, v.n - R + 1)
                sp.dma_start(KF[k][D:D + DE, 0, :], eaT[:, bass.ds(t * TE, TE)]).then_inc(landed_e[k], 16)
                sp.dma_start(qT[k], q_t[bass.ds(j, 1), :, :].rearrange("j p n -> p (j n)")).then_inc(landed_e[k], 16)
                wait(sp, summed, v.n - R + 1)
                tile = ea[bass.ds(t, 1), :, :].rearrange("t p n -> p (t n)").rearrange("p (s c) -> p s c", s=2)
                to = rows[k].rearrange("p s (x c) -> p s x c", x=2)[:, :, :, 0:DE]
                sp.dma_start(to, tile.unsqueeze(2).to_broadcast([P, 2, 2, DE])).then_inc(landed_e[k], 16)

            walk(sp, step, 0, 0)

        @block.gpsimd
        def _(po):
            po.wait_ge(init, 1)

            def step(v):
                k = v.slot(R)
                wait(po, idx_ready, v.n + 1)
                wait(po, summed, v.n - R + 1)
                wait(po, gated, v.n)
                po.tensor_tensor(gateP, gz, gz, ALU.add).then_inc(gated, 1)
                for s in range(2):
                    po.indirect_dma_start(rows[k][:, s, FW:FW + 2 * HC], None, kv_t.rearrange("a p c -> (a p) c"), bass.IndirectOffsetOnAxis(
                        ap=idx[:, 2 * k + s:2 * k + s + 1], axis=0)).then_inc(landed_g[k], 16)

            walk(po, step, 0, 0)

        @block.tensor
        def _(pe):
            pe.wait_ge(init, 1)

            def step(i):
                v = i + 1
                if v.exists():
                    pe.wait_ge(landed_g[v.slot(R)], v.landed(each=2))
                    wait(pe, k_copied, v.n)
                    for s in range(2):
                        ins = pe.transpose(psK[:, s * P:(s + 1) * P], rows[v.slot(R)][:, s, FW + D:FW + D + HC], m.ident[:, :])
                    ins.then_inc(k_turned, 1)
                v = i
                if v.exists():
                    s = psS[v.slot(4)]
                    pe.wait_ge(oh_ready, v.n + 1)
                    wait(pe, exp_ready, v.n - 3)
                    for e in range(2):
                        pe.matmul(s.rearrange("p (h s e) -> p h s e", h=HEADS, s=2)[:, :, e, :], oh[v.slot(4)][:, e, :],
                                  pen, start=(e == 0), stop=False)
                    pe.wait_ge(k_copied, v.n + 1)
                    pe.wait_ge(landed_e[v.slot(R)], v.landed(each=3))
                    for h in range(HEADS):
                        ins = pe.matmul(s[:, h * TE:(h + 1) * TE], qT[v.slot(R)][:, h * P:(h + 1) * P], KF[v.slot(R)][:, h, :], start=False, stop=(h == 1))
                    ins.then_inc(scored, 1)
                v = i + -2
                if v.exists():
                    pe.wait_ge(exp_ready, v.n + 1)
                    wait(pe, p_copied, v.n)
                    for x in range(2 * HEADS):
                        part = slice(x * P, (x + 1) * P)
                        ins = pe.transpose(psT[:, part], Pm[v.slot(4)][:, part], m.ident[:, :])
                    ins.then_inc(p_turned, 1)
                v = i + -3
                if v.exists():
                    pe.wait_ge(p_copied, v.n + 1)
                    wait(pe, acc_ready, v.n - 1)
                    for h in range(HEADS):
                        for s in range(2):
                            x = 2 * h + s
                            ins = pe.matmul(psA[v.slot(2)][:, h * VW:(h + 1) * VW], PT[v.slot(2)][:, x * P:(x + 1) * P],
                                            rows[v.slot(R)][:, s, AHEAD[h]:AHEAD[h] + VW], start=(s == 0), stop=(s == 1))
                    ins.then_inc(summed, 1)

            walk(pe, step, 1, 3)

        @block.scalar
        def _(act):
            def step(i):
                v = i + 1
                if v.exists():
                    act.wait_ge(k_turned, v.n + 1)
                    wait(act, scored, v.n - R + 1)
                    nc.scalar.copy(KF[v.slot(R)][0:D, 0, :], psK[0:D, :])
                    nc.scalar.copy(KF[v.slot(R)][D:P, 1, :], psK[D:P, :])
                    act.wait_ge(landed_e[v.slot(R)], v.landed(each=3))
                    nc.scalar.copy(KF[v.slot(R)][0:DE, 1, :], KF[v.slot(R)][D:D + DE, 0, :]).then_inc(k_copied, 1)
                v = i + -2
                if v.exists():
                    act.wait_ge(p_turned, v.n + 1)
                    wait(act, summed, v.n - 1)
                    nc.scalar.copy(PT[v.slot(2)], psT).then_inc(p_copied, 1)
                v = i
                if v.exists():
                    act.wait_ge(max_ready, v.n + 1)
                    wait(act, p_turned, v.n - 3)
                    nc.scalar.activation(corr[v.slot(4)], df[v.slot(4)], ACT.Exp)
                    for h in range(HEADS):
                        ins = nc.scalar.activation(Pm[v.slot(4)][:, h * TE:(h + 1) * TE], psS[v.slot(4)][:, h * TE:(h + 1) * TE], ACT.Exp,
                                                   bias=nm[v.slot(4)][:, h:h + 1])
                    ins.then_inc(exp_ready, 1)

            walk(act, step, 2, 2)

        @block.vector
        def _(dve):
            dve.memset(nmax, LOW)
            dve.memset(gz, 0.0)
            dve.memset(gateP, 0.0)
            for k in range(R):
                for h in range(HEADS):
                    at = AHEAD[h] + SUM[h]
                    dve.memset(rows[k][:, :, at:at + 1], 1.0)
                dve.memset(KF[k], 0.0)
            for h in range(HEADS):
                dve.tensor_scalar(pen[:, h * P:(h + 1) * P], m.ident[:, :], BIG, None, ALU.mult)
            dve.memset(acc, 0.0).then_inc(init, 1)
            dve.wait_ge(init, 1)

            def index(v):
                if not v.fixed or v.n >= R:
                    dve.wait_ge(landed_g[v.slot(R)], (v + -R).landed(each=2))
                dve.tensor_scalar(idx[:, 2 * v.slot(R):2 * v.slot(R) + 2], m.src2[:, :, bass.ds(v.n, 1)].rearrange("p s v -> p (s v)"),
                                  0, None, ALU.add).then_inc(idx_ready, 1)

            blocks = [None] * 4

            def onehot(v, s):
                if s == 0:
                    wait(dve, scored, v.n - 3)
                ins = dve.tensor_scalar(oh[v.slot(4)][:, s, :], m.iotaH[:, 0:P], m.rel2[:, s, bass.ds(v.n, 1)], -1.0, ALU.is_equal, ALU.add)
                if s == 1:
                    ins.then_inc(oh_ready, 1)

            def step(i):
                v = i + 6
                if v.exists():
                    index(v)
                m0 = i
                small = 3 * m0.n
                if m0.exists():
                    dve.wait_ge(scored, m0.n + 1)
                    s3 = m0.slot(4)
                    dve.tensor_reduce(rm[s3], psS[m0.slot(4)].rearrange("p (h e) -> p h e", h=HEADS), op=ALU.max, axis=X, negate=True).then_inc(s_small, 1)
                if i.c % 2 == 0 and (not i.fixed or i.c >= 0):
                    blocks[:] = m.blocks_of(dve, m0.n)
                ja, j = blocks[i.c % 2], blocks[i.c % 2 + 2]
                v = i + 2
                if v.exists():
                    onehot(v, 0)
                if m0.exists():
                    nmj = nmax[:, bass.ds(j, 1), :].rearrange("p j h -> p (j h)")
                    dve.wait_ge(s_small, small + 1)
                    dve.tensor_tensor(nm[s3], nmj, rm[s3], ALU.min).then_inc(s_small, 1)
                if v.exists():
                    onehot(v, 1)
                if m0.exists():
                    dve.wait_ge(s_small, small + 2)
                    dve.tensor_tensor(df[s3], nm[s3], nmj, ALU.subtract).then_inc(max_ready, 1)
                v = i + -3
                if v.exists():
                    dve.wait_ge(summed, v.n + 1)
                    wait(dve, acc_ready, v.n)
                    for h in range(HEADS):
                        a = acc[:, bass.ds(ja, 1), h, :].rearrange("p j c -> p (j c)")
                        ins = dve.scalar_tensor_tensor(a, a, corr[v.slot(4)][:, h:h + 1], psA[v.slot(2)][:, h * VW:(h + 1) * VW], ALU.mult, ALU.add)
                    ins.then_inc(acc_ready, 1)
                if m0.exists():
                    dve.wait_ge(max_ready, m0.n + 1)
                    dve.tensor_scalar(nmj, nm[s3], 0.0, None, ALU.add).then_inc(s_small, 1)

            walk(dve, step, 6, 3)


def stage_nodes(nc, m, keep, wp, bp, g2, b2, w1, b1, w2, bb2, w3, b3, g_t):
    with ExitStack() as ctx:
        sem = lambda n: ctx.enter_context(nc.semaphore(n))
        take = Take(m.big)
        take.at = keep["end"]
        acc = keep["acc"][:, 0:NCH]
        agg = take(NCH * HC).rearrange("p (a c) -> p a c", a=NCH)
        feat = take(NCH * P).rearrange("p (a c) -> p a c", a=NCH)
        w_fp = take(D)
        gt = take(NCH * D).rearrange("p (a d) -> p a d", a=NCH)
        rden = take(NCH * HEADS).rearrange("p (a h) -> p a h", a=NCH)
        w_p, w_1, w_2, w_3 = take(D), take(D, D), take(D, D), take(D, D)
        rows = [take(D) for _ in range(6)]
        bp_s, g2_s, b2_s, b1_s, bb2_s, b3_s = rows
        bufs = [take(DC) for _ in range(4)]
        half = [b[0:D, :] for b in bufs[0:2]]
        xs, h, t, tmp = (m.node(i) for i in range(4))
        mean, var = m.colsN[:, 0, :], m.colsN[:, 1, :]
        L = [Linear(nc, ctx, "n0", m, [bufs[0:2], bufs[2:4]], HC, D, more=(4, 5))]
        for i in range(1, 4):
            L.append(Linear(nc, ctx, f"n{i}", m, [half], D, D, after=L[-1]))
        s_in = sem("nd_in"); s_dve = sem("nd_dve"); s_var = sem("nd_var"); s_std = sem("nd_std")
        s_rows = [sem(f"nd_rows{i}") for i in range(4)]; s_out = sem("nd_out")
        s_g = sem("nd_g"); s_fp = sem("nd_fp"); s_fps = sem("nd_fps")
        block = ctx.enter_context(nc.Block())

        @block.sync
        def _(sp):
            for a, b in ((w_p, wp), (w_1, w1), (w_2, w2), (w_3, w3)):
                sp.dma_start(a, b).then_inc(s_in, 16)
            for a, b in zip(rows, (bp, g2, b2, b1, bb2, b3)):
                sp.dma_start(a, b.partition_broadcast(P)).then_inc(s_in, 16)
            L[3].all_taken(sp)
            sp.dma_start(g_t.rearrange("a p d -> p a d"), gt).then_inc(s_out, 16)
            sp.wait_ge(s_out, 16)

        @block.tensor
        def _(pe):
            pe.wait_ge(s_in, 160)
            pe.matmul(m.PB[6][:, 0:D], keep["w_x"], w_p, start=True, stop=True).then_inc(s_fp, 1)
            pe.wait_ge(s_fps, 1)
            pe.wait_ge(s_rows[0], 1)
            L[0].tensor(pe, (lambda a: agg[:, a, :], w_p), (lambda a: feat[:, a, :], w_fp))
            for i, (src, w) in enumerate(((t, w_1), (t, w_2), (h, w_3))):
                pe.wait_ge(s_rows[i + 1], 1)
                L[i + 1].tensor(pe, (lambda a, src=src: src[:, a, :], w))

        @block.scalar
        def _(act):
            act.wait_ge(s_fp, 1)
            nc.scalar.copy(w_fp, m.PB[6][:, 0:D]).then_inc(s_fps, 1)
            L[0].scalar(act, nc)
            act.wait_ge(s_var, 1)
            nc.scalar.sqrt(var, var).then_inc(s_std, 1)
            L[1].scalar(act, nc)
            act.wait_ge(s_g, 1)
            nc.scalar.activation(t, tmp, ACT.Gelu).then_inc(s_rows[2], 1)
            L[2].scalar(act, nc)
            act.wait_ge(s_var, 2)
            nc.scalar.sqrt(var, var).then_inc(s_std, 1)
            L[3].scalar(act, nc)

        @block.vector
        def _(dve):
            chain = Chain(dve, s_dve)
            for hd in range(HEADS):
                ins = dve.memset(feat[:, :, hd * D + DE:(hd + 1) * D], 0.0)
            chain(ins)
            for hd in range(HEADS):
                chain(dve.tensor_scalar(rden[:, :, hd], acc[:, :, hd, SUM[hd]], 1e-8, None, ALU.add))
            chain(dve.reciprocal(rden, rden))
            for hd in range(HEADS):
                dve.tensor_tensor(feat[:, :, (1 - hd) * D:(1 - hd) * D + DE], acc[:, :, hd, FEAT[hd]:FEAT[hd] + DE],
                                  spread(rden[:, :, hd], DE), ALU.mult)
                ins = dve.tensor_tensor(agg[:, :, hd * D:(hd + 1) * D], acc[:, :, hd, VAL[hd]:VAL[hd] + D], spread(rden[:, :, hd], D), ALU.mult)
            ins.then_inc(s_rows[0], 1)
            dve.wait_ge(s_in, 160)
            chain(dve.tensor_tensor(h, h, along(bp_s, NCH), ALU.add))
            for g in range(NG):
                dve.tensor_tensor(of_group(h, g), L[0].result(dve, g), of_group(h, g), ALU.add).then_inc(L[0].taken, 1)
            L[0].all_taken(dve)
            dve_norm(dve, chain, t, h, tmp, (mean, var), s_var, s_std, 1)
            chain(dve.tensor_tensor(t, t, along(g2_s, NCH), ALU.mult))
            dve.tensor_tensor(t, t, along(b2_s, NCH), ALU.add).then_inc(s_rows[1], 1)
            for g in range(NG):
                dve.tensor_tensor(of_group(tmp, g), L[1].result(dve, g), along(b1_s, len(chunks(g))), ALU.add).then_inc(L[1].taken, 1)
            L[1].all_taken(dve)
            chain(dve.tensor_tensor(xs, xs, h, ALU.add))
            dve.tensor_tensor(xs, xs, along(bb2_s, NCH), ALU.add).then_inc(s_g, 1)
            dve.wait_ge(s_g, 1)
            for g in range(NG):
                dve.tensor_tensor(of_group(xs, g), L[2].result(dve, g), of_group(xs, g), ALU.add).then_inc(L[2].taken, 1)
            L[2].all_taken(dve)
            dve_norm(dve, chain, h, xs, tmp, (mean, var), s_var, s_std, 2)
            dve.tensor_scalar(h, h, 0.0, None, ALU.max).then_inc(s_rows[3], 1)
            for g in range(NG):
                dve.tensor_tensor(of_group(gt, g), L[3].result(dve, g), along(b3_s, len(chunks(g))), ALU.add).then_inc(L[3].taken, 1)


def stage_messages(nc, m, keep, w1, efT, g_t):
    with ExitStack() as ctx:
        sem = lambda n: ctx.enter_context(nc.semaphore(n))
        take = Take(m.big)
        halves = lambda a: a.rearrange("p (s c) -> p s c", s=2)
        acc = keep["acc3"]
        take.at = keep["end"]
        w_e = take(D, D)
        G = [halves(take(2 * D)) for _ in range(RM)]
        ef = [take(TE, D) for _ in range(RM)]
        M = [halves(take(2 * MW)) for _ in range(4)]
        oh = [halves(take(2 * P)) for _ in range(4)]
        idx = take(2 * RM).bitcast(I32)
        gateP, gz = take(1), take(1)
        psM = [halves(m.PB[0][:, 0:2 * D]), halves(m.PB[1][:, 0:2 * D])]
        psA = [m.PB[2][:, 0:MW], m.PB[3][:, 0:MW]]
        init = sem("ms_init"); s_in = sem("ms_in"); idx_ready = sem("ms_idx")
        landed_g = m.table_landed
        landed_e = [sem(f"ms_e{i}") for i in range(RM)]
        gated = sem("ms_gated")
        m_done = sem("ms_M")
        m_ready = sem("ms_Ms")
        oh_ready = sem("ms_oh")
        summed = sem("ms_A")
        acc_ready = sem("ms_acc")
        block = ctx.enter_context(nc.Block())

        @block.sync
        def _(sp):
            sp.dma_start(w_e, w1).then_inc(s_in, 16)

            tiles = [None, None]

            def step(v):
                if v.c % 2 == 0:
                    tiles[:] = m.tiles_of(sp, v.n)
                t = tiles[v.c % 2]
                wait(sp, m_done, v.n - RM + 1)
                sp.dma_start(ef[v.slot(RM)], efT[:, bass.ds(t * TE, TE)]).then_inc(landed_e[v.slot(RM)], 16)

            walk(sp, step, 0, 0)

        @block.gpsimd
        def _(po):
            po.wait_ge(init, 1)

            def step(v):
                k = v.slot(RM)
                if v.c % 2 == 0:
                    n = v.n + 1 if not v.fixed else min(v.n + 1, V2 - 1)
                    wait(po, idx_ready, n + 1)
                    wait(po, m_done, n - RM + 1)
                    wait(po, gated, v.g * (R // 2) + v.c // 2)
                    po.tensor_tensor(gateP, gz, gz, ALU.add).then_inc(gated, 1)
                for s in range(2):
                    po.indirect_dma_start(G[k][:, s, :], None, g_t.rearrange("a p c -> (a p) c"), bass.IndirectOffsetOnAxis(
                        ap=idx[:, 2 * k + s:2 * k + s + 1], axis=0)).then_inc(landed_g[k], 16)

            walk(po, step, 0, 0)

        @block.tensor
        def _(pe):
            pe.wait_ge(init, 1)
            pe.wait_ge(s_in, 16)

            def step(i):
                v = i + 1
                if v.exists():
                    k = v.slot(RM)
                    pe.wait_ge(landed_e[k], v.landed(RM))
                    wait(pe, m_ready, v.n - 1)
                    for s in range(2):
                        pe.matmul(psM[v.slot(2)][:, s, :], ef[k][:, s * P:(s + 1) * P], w_e, start=(s == 0), stop=False)
                    pe.wait_ge(landed_g[k], v.landed(RM, 2))
                    pe.matmul(psM[v.slot(2)], m.ident[:, :], G[k], start=False, stop=True).then_inc(m_done, 1)
                v = i
                if v.exists():
                    pe.wait_ge(m_ready, v.n + 1)
                    pe.wait_ge(oh_ready, v.n + 1)
                    wait(pe, acc_ready, v.n - 1)
                    for s in range(2):
                        ins = pe.matmul(psA[v.slot(2)], oh[v.slot(4)][:, s, :], M[v.slot(4)][:, s, :], start=(s == 0), stop=(s == 1))
                    ins.then_inc(summed, 1)

            walk(pe, step, 1, 0)

        @block.scalar
        def _(act):
            act.wait_ge(init, 1)

            def step(v):
                act.wait_ge(m_done, v.n + 1)
                wait(act, summed, v.n - 3)
                nc.scalar.activation(M[v.slot(4)][:, :, 0:D], psM[v.slot(2)], ACT.Relu).then_inc(m_ready, 1)

            walk(act, step, 0, 0)

        @block.vector
        def _(dve):
            dve.memset(gz, 0.0)
            dve.memset(gateP, 0.0)
            for k in range(4):
                dve.memset(M[k][:, :, D:], 1.0)
            dve.memset(acc, 0.0).then_inc(init, 1)
            dve.wait_ge(init, 1)

            blocks = [None] * 4

            def step(i):
                if i.c % 2 == 0 and (not i.fixed or i.c >= 0):
                    blocks[:] = m.blocks_of(dve, i.n)
                v = i + 3
                if v.exists():
                    k = v.slot(RM)
                    if not v.fixed or v.n >= RM:
                        dve.wait_ge(landed_g[k], (v + -RM).landed(RM, 2))
                    dve.tensor_scalar(idx[:, 2 * k:2 * k + 2], m.src2[:, :, bass.ds(v.n, 1)].rearrange("p s v -> p (s v)"), 0, None,
                                      ALU.add).then_inc(idx_ready, 1)
                v = i + -3
                if v.exists():
                    j = blocks[i.c % 2]
                    dve.wait_ge(summed, v.n + 1)
                    wait(dve, acc_ready, v.n)
                    a = acc[:, bass.ds(j, 1), :].rearrange("p j c -> p (j c)")
                    dve.tensor_tensor(a, a, psA[v.slot(2)], ALU.add).then_inc(acc_ready, 1)
                v = i + 1
                if v.exists():
                    wait(dve, summed, v.n - 3)
                    for s in range(2):
                        ins = dve.tensor_scalar(oh[v.slot(4)][:, s, :], m.iotaH[:, 0:P], m.rel2[:, s, bass.ds(v.n, 1)], None, ALU.is_equal)
                    ins.then_inc(oh_ready, 1)

            walk(dve, step, 3, 3)


def stage_output(nc, m, keep, w2, b2, out):
    with ExitStack() as ctx:
        sem = lambda n: ctx.enter_context(nc.semaphore(n))
        take = Take(m.big)
        take.at = keep["end"]
        acc = keep["acc3"][:, 0:NCH]
        both = take(NCH * HC).rearrange("p (a c) -> p a c", a=NCH)
        rcnt, w_s, b_s = take(NCH), take(D), take(D)
        bufs = [take(DC) for _ in range(2)]
        xs, h, t, _ = (m.node(i) for i in range(4))
        L = Linear(nc, ctx, "o", m, [bufs], HC, D)
        s_in = sem("o_in"); s_dve = sem("o_dve"); s_rows = sem("o_rows"); s_res = sem("o_res"); s_out = sem("o_out")
        s_t = sem("o_t")
        block = ctx.enter_context(nc.Block())

        @block.sync
        def _(sp):
            sp.dma_start(w_s, w2).then_inc(s_in, 16)
            sp.dma_start(b_s, b2.partition_broadcast(P)).then_inc(s_in, 16)
            full = NODES // P
            sp.wait_ge(s_res, NG)
            sp.dma_start(out[0:full * P, :].rearrange("(a p) d -> p a d", p=P), xs[:, 0:full, :]).then_inc(s_out, 16)
            sp.dma_start(out[full * P:NODES, :], xs[0:NODES - full * P, full, :]).then_inc(s_out, 16)
            sp.wait_ge(s_out, 32)

        @block.tensor
        def _(pe):
            pe.wait_ge(s_in, 32)
            pe.wait_ge(s_rows, 1)
            L.tensor(pe, (lambda a: both[:, a, :], w_s))

        @block.scalar
        def _(act):
            L.scalar(act, nc)

        @block.vector
        def _(dve):
            chain = Chain(dve, s_dve)
            chain(dve.tensor_scalar(rcnt, acc[:, :, D], 1.0, None, ALU.max))
            chain(dve.reciprocal(rcnt, rcnt))
            dve.tensor_copy(both[:, :, D:], h)
            dve.tensor_tensor(both[:, :, 0:D], acc[:, :, 0:D], spread(rcnt, D), ALU.mult).then_inc(s_rows, 1)
            dve.wait_ge(s_in, 32)
            for g in range(NG):
                dve.tensor_tensor(of_group(t, g), L.result(dve, g), along(b_s, len(chunks(g))), ALU.add).then_inc(L.taken, 1)
                dve.wait_ge(L.taken, g + 1)
                dve.scalar_tensor_tensor(of_group(xs, g), of_group(t, g), 0.0, of_group(xs, g), ALU.max, ALU.add).then_inc(s_res, 1)


def build(nc, last, x, src, dst, w, ea, eaT, efT, L0_gnn_W, L0_gnn_b, L1_gnn_W1, L1_gnn_b1, L1_gnn_W2, L1_gnn_b2, L1_gnn_W3,
          L1_gnn_b3, L2_gnn_Wq, L2_gnn_bq, L2_gnn_Wk, L2_gnn_bk, L2_gnn_Wv, L2_gnn_bv, L2_gnn_We, L2_gnn_Wp, L2_gnn_bp, L2_gnn_ln1_g,
          L2_gnn_ln1_b, L2_gnn_ln2_g, L2_gnn_ln2_b, L2_gnn_W1, L2_gnn_b1, L2_gnn_W2, L2_gnn_b2, L3_gnn_W1, L3_gnn_b1, L3_gnn_W2,
          L3_gnn_b2, out):
    with ExitStack() as ctx:
        m = Mem(nc, ctx)
        scratch = lambda name, shape: nc.dram_tensor(name, shape, F32, kind="Internal").ap()
        aw = scratch("weights_dense", [J1 + SPARE, P, BCOL])
        kv_t = scratch("kv_table", [NCH, P, 2 * HC])
        q_t = scratch("q_table", [JPAD, P, HEADS * P])
        g_t = scratch("message_table", [NCH, P, D])
        xv = x.rearrange("(a p) d -> p a d", p=P)
        half = lambda i: m.work[:, i * 2 * V1P:(i + 1) * 2 * V1P].rearrange("p (h v) -> p h v", h=2)
        behind = 4 * BCOL + OH * (4 * P + BCOL)
        t1 = dict(col=half(0), row=half(1), w=[half(2), half(3), half(4)],
                  keep=m.work2[:, behind:behind + V1P // 2].bitcast(BF16))
        keep = dict(acc=m.big[:, 0:JPAD * HEADS * VW].rearrange("p (a h c) -> p a h c", a=JPAD, h=HEADS),
                    acc3=m.big[:, 0:JPAD * MW].rearrange("p (a c) -> p a c", a=JPAD), end=JPAD * HEADS * VW, w_x=m.work2[:, 0:P])
        tiles = lambda a: a.rearrange("(t e) -> t e", e=TE)
        stage_tables(nc, m, last, tiles(dst), tiles(src), tiles(w), t1)
        stage_build(nc, m, t1, aw)
        stage_layer0_start(nc, m, xv, L0_gnn_W, L0_gnn_b)
        stage_layer0_hops(nc, m, xv, aw)
        stage_layer1(nc, m, aw, [L1_gnn_W1, L1_gnn_W2, L1_gnn_W3], [L1_gnn_b1, L1_gnn_b2, L1_gnn_b3])
        stage_attend_tables(nc, m, keep, L2_gnn_We, L2_gnn_Wq, L2_gnn_Wk, L2_gnn_Wv, L2_gnn_bq, L2_gnn_bk, L2_gnn_bv, L2_gnn_ln1_g,
                            L2_gnn_ln1_b, kv_t, q_t)
        stage_attend(nc, m, keep, ea, eaT, kv_t, q_t)
        stage_nodes(nc, m, keep, L2_gnn_Wp, L2_gnn_bp, L2_gnn_ln2_g, L2_gnn_ln2_b, L2_gnn_W1, L2_gnn_b1, L2_gnn_W2, L2_gnn_b2,
                    L3_gnn_W1[D:, :], L3_gnn_b1, g_t)
        stage_messages(nc, m, keep, L3_gnn_W1[0:D, :], efT, g_t)
        stage_output(nc, m, keep, L3_gnn_W2, L3_gnn_b2, out)


WEIGHTS = ("L0_gnn_W", "L0_gnn_b", "L1_gnn_W1", "L1_gnn_b1", "L1_gnn_W2", "L1_gnn_b2", "L1_gnn_W3", "L1_gnn_b3", "L2_gnn_Wq",
           "L2_gnn_bq", "L2_gnn_Wk", "L2_gnn_bk", "L2_gnn_Wv", "L2_gnn_bv", "L2_gnn_We", "L2_gnn_Wp", "L2_gnn_bp", "L2_gnn_ln1_g",
           "L2_gnn_ln1_b", "L2_gnn_ln2_g", "L2_gnn_ln2_b", "L2_gnn_W1", "L2_gnn_b1", "L2_gnn_W2", "L2_gnn_b2", "L3_gnn_W1",
           "L3_gnn_b1", "L3_gnn_W2", "L3_gnn_b2")


def kernel(**inputs):
    import concourse.bacc as bacc
    from concourse.bass_utils import run_bass_kernel_spmd

    a = {k: np.asarray(v) for k, v in inputs.items()}
    more = EPAD - EDGES
    dst = np.pad(a["dst"], (0, more), constant_values=NDST - 1)
    src = np.pad(a["src"], (0, more))

    n = -(-T1 // P)
    last = np.ascontiguousarray(np.pad(dst[TE - 1::TE], (0, n * P - T1), constant_values=FAR).reshape(n, P).T)

    arrays = dict(
        last=last, x=np.pad(a["x"], ((0, NPAD - NODES), (0, 0))), src=src, dst=dst,
        w=np.pad(a["edge_weight"], (0, more)),
        ea=np.ascontiguousarray(np.pad(a["edge_attr_32"], ((0, more), (0, 0))).reshape(T1, 2, P, -1).transpose(0, 2, 1, 3)).reshape(T1, P, -1),
        eaT=np.ascontiguousarray(np.pad(a["edge_attr_32"], ((0, more), (0, 0))).T),
        efT=np.ascontiguousarray(np.pad(a["edge_attr_64"], ((0, more), (0, 0))).T),
        **{k: np.ascontiguousarray(a[k]) for k in WEIGHTS})
    nc = bacc.Bacc("TRN2", target_bir_lowering=False, num_devices=1)
    args = {k: nc.dram_tensor(f"in_{k}", v.shape, mybir.dt.from_np(v.dtype), kind="ExternalInput").ap() for k, v in arrays.items()}
    out = nc.dram_tensor("out_x", (NODES, D), F32, kind="ExternalOutput").ap()
    build(nc, out=out, **args)
    r = run_bass_kernel_spmd(nc, [{f"in_{k}": v for k, v in arrays.items()}], core_ids=[0])
    return r.results[0]["out_x"]
```
